# Optimizing a Trainium2 kernel written in Bass

```python
import numpy as np
import jax
import jax.numpy as jnp

def _softmax(x, axis=-1):
    return jax.nn.softmax(x, axis=axis)

def _gelu(x):
    return jax.nn.gelu(x, approximate=True)

def _silu(x):
    return jax.nn.silu(x)

def _sigmoid(x):
    return jax.nn.sigmoid(x)

def _layernorm(x, axis=-1, eps=1e-05):
    m = jnp.mean(x, axis=axis, keepdims=True)
    v = jnp.var(x, axis=axis, keepdims=True)
    return (x - m) / jnp.sqrt(v + eps)

def _scatter_add(tgt, idx, src, axis=0):
    return tgt.at[idx].add(src)

def _segment_sum(src, seg, n):
    return jax.ops.segment_sum(src, seg, n)
kernel_name = 'mk_audio_tower_d2_tok_audfeat768_r4_f1310f'

def setup_inputs(seed: int=0):
    np.random.seed(seed)
    _w = jnp.asarray

    def _rec_inputs():
        import jax
        import jax.numpy as jnp
        _rk = jax.random.key(seed)
        x = -0.00040386 + 0.999972 * jax.random.normal(jax.random.fold_in(_rk, 1), (16, 512, 192), jnp.float32)
        return x
    x = _rec_inputs()

    def _L0_tok_setup():
        import jax, jax.numpy as jnp
        import numpy as np
        HEADS = 12
        Q_STRIDE = 4
        WINDOW_SIZE = 64
        key = jax.random.key(seed)
        ks = jax.random.split(key, 3)
        B, N, dim = (8, 512, 192)
        x = jax.random.normal(ks[0], (B, N, dim), dtype=jnp.float32)
        w_qkv = jax.random.normal(ks[1], (3 * dim, dim), dtype=jnp.float32) * dim ** (-0.5)
        b_qkv = jnp.zeros((3 * dim,), dtype=jnp.float32)
        w_proj = jax.random.normal(ks[2], (dim, dim), dtype=jnp.float32) * dim ** (-0.5)
        b_proj = jnp.zeros((dim,), dtype=jnp.float32)
        return {'x': x, 'w_qkv': w_qkv, 'b_qkv': b_qkv, 'w_proj': w_proj, 'b_proj': b_proj}
    _L0_tok_all = _L0_tok_setup()
    _L0_tok_in = {k: v for k, v in _L0_tok_all.items() if k in ('w_qkv', 'b_qkv', 'w_proj', 'b_proj')}
    del _L0_tok_all

    def _L0_attn_setup():
        import jax, jax.numpy as jnp
        import numpy as np
        import math
        DIM = 192
        NUM_HEADS = 12

        def _xavier_uniform(key, out_f, in_f):
            a = math.sqrt(6.0 / (in_f + out_f))
            return jax.random.uniform(key, (out_f, in_f), jnp.float32, -a, a)
        key = jax.random.key(seed)
        k_x, k_qw, k_qB, k_pw, k_pB = jax.random.split(key, 5)
        B, N = (16, 256)
        x = jax.random.normal(k_x, (B, N, DIM), jnp.float32)
        qkv_w = _xavier_uniform(k_qw, 3 * DIM, DIM)
        qkv_b = jnp.zeros((3 * DIM,), jnp.float32)
        qkv_B = jax.random.normal(k_qB, (3 * DIM, DIM), jnp.float32) * math.sqrt(1.0 / DIM)
        proj_w = _xavier_uniform(k_pw, DIM, DIM)
        proj_b = jnp.zeros((DIM,), jnp.float32)
        proj_B = jax.random.normal(k_pB, (DIM, DIM), jnp.float32) * math.sqrt(1.0 / DIM)
        return {'x': x, 'qkv_w': qkv_w, 'qkv_b': qkv_b, 'qkv_B': qkv_B, 'proj_w': proj_w, 'proj_b': proj_b, 'proj_B': proj_B}
    _L0_attn_all = _L0_attn_setup()
    _L0_attn_in = {k: v for k, v in _L0_attn_all.items() if k in ('qkv_w', 'qkv_b', 'qkv_B', 'proj_w', 'proj_b', 'proj_B')}
    del _L0_attn_all

    def _L0_ffn_setup():
        import jax, jax.numpy as jnp
        import numpy as np
        DIM = 192
        HEADS = 12
        HIDDEN = 768
        E = 8
        TOPK = 2
        EPS = 1e-05

        def _ln(x, g, b):
            m = x.mean(-1, keepdims=True)
            v = jnp.mean((x - m) ** 2, axis=-1, keepdims=True)
            return (x - m) * jax.lax.rsqrt(v + EPS) * g + b
        key = jax.random.key(seed)
        ks = jax.random.split(key, 10)
        s = 0.02
        return {'x': jax.random.normal(ks[0], (8, 256, DIM), jnp.float32), 'ln1_g': jnp.ones((DIM,), jnp.float32), 'ln1_b': jnp.zeros((DIM,), jnp.float32), 'qkv_w': jax.random.normal(ks[1], (DIM, 3 * DIM), jnp.float32) * s, 'proj_w': jax.random.normal(ks[2], (DIM, DIM), jnp.float32) * s, 'proj_b': jnp.zeros((DIM,), jnp.float32), 'ln2_g': jnp.ones((DIM,), jnp.float32), 'ln2_b': jnp.zeros((DIM,), jnp.float32), 'gate_w': jax.random.normal(ks[3], (DIM, E), jnp.float32) * s, 'gate_b': jnp.zeros((E,), jnp.float32), 'w1': jax.random.normal(ks[4], (E, DIM, HIDDEN), jnp.float32) * s, 'b1': jnp.zeros((E, HIDDEN), jnp.float32), 'w2': jax.random.normal(ks[5], (E, HIDDEN, DIM), jnp.float32) * s, 'b2': jnp.zeros((E, DIM), jnp.float32)}
    _L0_ffn_all = _L0_ffn_setup()
    _L0_ffn_in = {k: v for k, v in _L0_ffn_all.items() if k in ('ln1_g', 'ln1_b', 'qkv_w', 'proj_w', 'proj_b', 'ln2_g', 'ln2_b', 'gate_w', 'gate_b', 'w1', 'b1', 'w2', 'b2')}
    del _L0_ffn_all

    def _L1_attn_setup():
        import jax, jax.numpy as jnp
        import numpy as np
        NUM_HEADS = 12
        OT_REG = 0.1
        SINKHORN_ITERS = 10
        DIAG_VAL = 1000.0

        def _sot(q):
            N = q.shape[-2]
            qn = q / (jnp.linalg.norm(q, axis=-1, keepdims=True) + 1e-08)
            C = 1.0 - jnp.einsum('bhnd,bhmd->bhnm', qn, qn)
            eye = jnp.eye(N, dtype=bool)
            C = jnp.where(eye, DIAG_VAL, C)
            log_K = -C / OT_REG
            log_marg = -jnp.log(jnp.float32(N))
            log_v = jnp.zeros(q.shape[:2] + (N,), dtype=q.dtype)
            for _ in range(SINKHORN_ITERS):
                log_u = log_marg - jax.nn.logsumexp(log_K + log_v[..., None, :], axis=-1)
                log_v = log_marg - jax.nn.logsumexp(log_K + log_u[..., :, None], axis=-2)
            log_T = log_u[..., :, None] + log_K + log_v[..., None, :]
            z = jnp.exp(log_T)
            z = z / jnp.max(z, axis=(-2, -1), keepdims=True)
            z = jnp.where(eye, 1.0, z)
            return z
        key = jax.random.key(seed)
        k1, k2, k3 = jax.random.split(key, 3)
        B, N, C = (64, 64, 192)
        x = jax.random.normal(k1, (B, N, C), dtype=jnp.float32)
        w_qkv = jax.random.normal(k2, (3 * C, C), dtype=jnp.float32) * C ** (-0.5)
        w_proj = jax.random.normal(k3, (C, C), dtype=jnp.float32) * C ** (-0.5)
        b_proj = jnp.zeros((C,), dtype=jnp.float32)
        return {'x': x, 'w_qkv': w_qkv, 'w_proj': w_proj, 'b_proj': b_proj}
    _L1_attn_all = _L1_attn_setup()
    _L1_attn_in = {k: v for k, v in _L1_attn_all.items() if k in ('w_qkv', 'w_proj', 'b_proj')}
    del _L1_attn_all

    def _L1_ffn_setup():
        import jax, jax.numpy as jnp
        import numpy as np
        LN2 = jnp.log(jnp.float32(2.0))
        ALPHA = 0.5
        A_BITS = 8
        W_BITS = 8
        EPS = 1e-08

        def round_ln(x):
            y = jnp.floor(jnp.log(x) / LN2)
            up = x - 2.0 ** y > 2.0 ** (y + 1.0) - x
            return y + up.astype(x.dtype)

        def fq_act_asym(x, bits=A_BITS):
            qmax = 2 ** bits - 1
            xmin = jnp.minimum(x.min(), 0.0)
            xmax = jnp.maximum(x.max(), 0.0)
            scale = jnp.maximum((xmax - xmin) / qmax, EPS)
            zp = jnp.round(-xmin / scale)
            q = jnp.clip(jnp.round(x / scale) + zp, 0, qmax)
            return (q - zp) * scale

        def fq_act_sym(x, bits=A_BITS):
            qmax = 2 ** (bits - 1) - 1
            scale = jnp.maximum(jnp.abs(x).max() / qmax, EPS)
            q = jnp.clip(jnp.round(x / scale), -qmax - 1, qmax)
            return q * scale

        def fq_weight(w, bits=W_BITS):
            qmax = 2 ** (bits - 1) - 1
            scale = jnp.maximum(jnp.abs(w).max(axis=1, keepdims=True) / qmax, EPS)
            q = jnp.clip(jnp.round(w / scale), -qmax - 1, qmax)
            return q * scale
        key = jax.random.key(seed)
        ks = jax.random.split(key, 5)
        B, N, C, H = (64, 197, 192, 768)
        x = jax.random.normal(ks[0], (B, N, C), dtype=jnp.float32)
        w1 = jax.random.normal(ks[1], (H, C), dtype=jnp.float32) * 0.02
        b1 = jax.random.normal(ks[2], (H,), dtype=jnp.float32) * 0.02
        w2 = jax.random.normal(ks[3], (C, H), dtype=jnp.float32) * 0.02
        b2 = jax.random.normal(ks[4], (C,), dtype=jnp.float32) * 0.02
        return {'x': x, 'w1': w1, 'b1': b1, 'w2': w2, 'b2': b2}
    _L1_ffn_all = _L1_ffn_setup()
    _L1_ffn_in = {k: v for k, v in _L1_ffn_all.items() if k in ('w1', 'b1', 'w2', 'b2')}
    del _L1_ffn_all
    return {'x': x, 'L0_tok_w_qkv': _L0_tok_in['w_qkv'], 'L0_tok_b_qkv': _L0_tok_in['b_qkv'], 'L0_tok_w_proj': _L0_tok_in['w_proj'], 'L0_tok_b_proj': _L0_tok_in['b_proj'], 'L0_attn_qkv_w': _L0_attn_in['qkv_w'], 'L0_attn_qkv_b': _L0_attn_in['qkv_b'], 'L0_attn_qkv_B': _L0_attn_in['qkv_B'], 'L0_attn_proj_w': _L0_attn_in['proj_w'], 'L0_attn_proj_b': _L0_attn_in['proj_b'], 'L0_attn_proj_B': _L0_attn_in['proj_B'], 'L0_ffn_ln1_g': _L0_ffn_in['ln1_g'], 'L0_ffn_ln1_b': _L0_ffn_in['ln1_b'], 'L0_ffn_qkv_w': _L0_ffn_in['qkv_w'], 'L0_ffn_proj_w': _L0_ffn_in['proj_w'], 'L0_ffn_proj_b': _L0_ffn_in['proj_b'], 'L0_ffn_ln2_g': _L0_ffn_in['ln2_g'], 'L0_ffn_ln2_b': _L0_ffn_in['ln2_b'], 'L0_ffn_gate_w': _L0_ffn_in['gate_w'], 'L0_ffn_gate_b': _L0_ffn_in['gate_b'], 'L0_ffn_w1': _L0_ffn_in['w1'], 'L0_ffn_b1': _L0_ffn_in['b1'], 'L0_ffn_w2': _L0_ffn_in['w2'], 'L0_ffn_b2': _L0_ffn_in['b2'], 'L1_attn_w_qkv': _L1_attn_in['w_qkv'], 'L1_attn_w_proj': _L1_attn_in['w_proj'], 'L1_attn_b_proj': _L1_attn_in['b_proj'], 'L1_ffn_w1': _L1_ffn_in['w1'], 'L1_ffn_b1': _L1_ffn_in['b1'], 'L1_ffn_w2': _L1_ffn_in['w2'], 'L1_ffn_b2': _L1_ffn_in['b2']}

def reference(x, L0_tok_w_qkv, L0_tok_b_qkv, L0_tok_w_proj, L0_tok_b_proj, L0_attn_qkv_w, L0_attn_qkv_b, L0_attn_qkv_B, L0_attn_proj_w, L0_attn_proj_b, L0_attn_proj_B, L0_ffn_ln1_g, L0_ffn_ln1_b, L0_ffn_qkv_w, L0_ffn_proj_w, L0_ffn_proj_b, L0_ffn_ln2_g, L0_ffn_ln2_b, L0_ffn_gate_w, L0_ffn_gate_b, L0_ffn_w1, L0_ffn_b1, L0_ffn_w2, L0_ffn_b2, L1_attn_w_qkv, L1_attn_w_proj, L1_attn_b_proj, L1_ffn_w1, L1_ffn_b1, L1_ffn_w2, L1_ffn_b2):
    import jax
    import jax.numpy as jnp

    def _L0_tok_ref(x, w_qkv, b_qkv, w_proj, b_proj):
        import jax, jax.numpy as jnp
        import numpy as np
        HEADS = 12
        Q_STRIDE = 4
        WINDOW_SIZE = 64
        B, N, dim = x.shape
        head_dim = dim // HEADS
        num_windows = N // (Q_STRIDE * WINDOW_SIZE)
        tpw = N // num_windows
        qkv = x @ w_qkv.T + b_qkv
        qkv = qkv.reshape(B, tpw, num_windows, 3, HEADS, head_dim)
        qkv = jnp.transpose(qkv, (3, 0, 4, 2, 1, 5))
        q, k, v = (qkv[0], qkv[1], qkv[2])
        q = q.reshape(B, HEADS, num_windows, Q_STRIDE, WINDOW_SIZE, head_dim).max(axis=3)
        scale = head_dim ** (-0.5)
        attn = jnp.einsum('bhwqd,bhwkd->bhwqk', q * scale, k)
        attn = jax.nn.softmax(attn, axis=-1)
        o = jnp.einsum('bhwqk,bhwkd->bhwqd', attn, v)
        o = jnp.transpose(o, (0, 3, 2, 1, 4)).reshape(B, WINDOW_SIZE * num_windows, dim)
        return o @ w_proj.T + b_proj

    def _L0_attn_ref(x, qkv_w, qkv_b, qkv_B, proj_w, proj_b, proj_B):
        import jax, jax.numpy as jnp
        import numpy as np
        import math
        DIM = 192
        NUM_HEADS = 12

        def _xavier_uniform(key, out_f, in_f):
            a = math.sqrt(6.0 / (in_f + out_f))
            return jax.random.uniform(key, (out_f, in_f), jnp.float32, -a, a)
        B, N, C = x.shape
        hd = C // NUM_HEADS
        scale = hd ** (-0.5)
        qkv = x @ qkv_w.T + qkv_b
        qkv = qkv.reshape(B, N, 3, NUM_HEADS, hd).transpose(2, 0, 3, 1, 4)
        q, k, v = (qkv[0], qkv[1], qkv[2])
        attn = jnp.einsum('bhnd,bhmd->bhnm', q, k) * scale
        attn = jax.nn.softmax(attn, axis=-1)
        out = jnp.einsum('bhnm,bhmd->bhnd', attn, v)
        out = out.transpose(0, 2, 1, 3).reshape(B, N, C)
        return out @ proj_w.T + proj_b

    def _L0_ffn_ref(x, ln1_g, ln1_b, qkv_w, proj_w, proj_b, ln2_g, ln2_b, gate_w, gate_b, w1, b1, w2, b2):
        import jax, jax.numpy as jnp
        import numpy as np
        DIM = 192
        HEADS = 12
        HIDDEN = 768
        E = 8
        TOPK = 2
        EPS = 1e-05

        def _ln(x, g, b):
            m = x.mean(-1, keepdims=True)
            v = jnp.mean((x - m) ** 2, axis=-1, keepdims=True)
            return (x - m) * jax.lax.rsqrt(v + EPS) * g + b
        B, S, D = x.shape
        hd = D // HEADS
        h = _ln(x, ln1_g, ln1_b)
        qkv = (h @ qkv_w).reshape(B, S, 3, HEADS, hd).transpose(2, 0, 3, 1, 4)
        q, k, v = (qkv[0], qkv[1], qkv[2])
        att = jax.nn.softmax(jnp.einsum('bhqd,bhkd->bhqk', q, k) * hd ** (-0.5), axis=-1)
        o = jnp.einsum('bhqk,bhkd->bhqd', att, v).transpose(0, 2, 1, 3).reshape(B, S, D)
        x = x + o @ proj_w + proj_b
        h2 = _ln(x, ln2_g, ln2_b).reshape(B * S, D)
        logits = h2 @ gate_w + gate_b
        wts, sel = jax.lax.top_k(logits, TOPK)
        wts = jax.nn.softmax(wts.astype(jnp.float32), axis=-1).astype(x.dtype)
        cw = (jax.nn.one_hot(sel, E, dtype=x.dtype) * wts[..., None]).sum(axis=1)
        res = jnp.zeros_like(h2)
        for e in range(E):
            he = jax.nn.gelu(h2 @ w1[e] + b1[e], approximate=False)
            res = res + cw[:, e:e + 1] * (he @ w2[e] + b2[e])
        return x + res.reshape(B, S, D)

    def _L1_attn_ref(x, w_qkv, w_proj, b_proj):
        import jax, jax.numpy as jnp
        import numpy as np
        NUM_HEADS = 12
        OT_REG = 0.1
        SINKHORN_ITERS = 10
        DIAG_VAL = 1000.0

        def _sot(q):
            N = q.shape[-2]
            qn = q / (jnp.linalg.norm(q, axis=-1, keepdims=True) + 1e-08)
            C = 1.0 - jnp.einsum('bhnd,bhmd->bhnm', qn, qn)
            eye = jnp.eye(N, dtype=bool)
            C = jnp.where(eye, DIAG_VAL, C)
            log_K = -C / OT_REG
            log_marg = -jnp.log(jnp.float32(N))
            log_v = jnp.zeros(q.shape[:2] + (N,), dtype=q.dtype)
            for _ in range(SINKHORN_ITERS):
                log_u = log_marg - jax.nn.logsumexp(log_K + log_v[..., None, :], axis=-1)
                log_v = log_marg - jax.nn.logsumexp(log_K + log_u[..., :, None], axis=-2)
            log_T = log_u[..., :, None] + log_K + log_v[..., None, :]
            z = jnp.exp(log_T)
            z = z / jnp.max(z, axis=(-2, -1), keepdims=True)
            z = jnp.where(eye, 1.0, z)
            return z
        B, N, C = x.shape
        H = NUM_HEADS
        hd = C // H
        scale = hd ** (-0.5)
        qkv = jnp.einsum('bnc,oc->bno', x, w_qkv)
        qkv = qkv.reshape(B, N, 3, H, hd).transpose(2, 0, 3, 1, 4)
        q, k, v = (qkv[0], qkv[1], qkv[2])
        attn = _sot(q)
        attn = jax.nn.softmax(attn * scale, axis=-1)
        out = jnp.einsum('bhnm,bhmd->bhnd', attn, v)
        out = out.transpose(0, 2, 1, 3).reshape(B, N, C)
        out = jnp.einsum('bnc,oc->bno', out, w_proj) + b_proj
        return out

    def _L1_ffn_ref(x, w1, b1, w2, b2):
        import jax, jax.numpy as jnp
        import numpy as np
        LN2 = jnp.log(jnp.float32(2.0))
        ALPHA = 0.5
        A_BITS = 8
        W_BITS = 8
        EPS = 1e-08

        def round_ln(x):
            y = jnp.floor(jnp.log(x) / LN2)
            up = x - 2.0 ** y > 2.0 ** (y + 1.0) - x
            return y + up.astype(x.dtype)

        def fq_act_asym(x, bits=A_BITS):
            qmax = 2 ** bits - 1
            xmin = jnp.minimum(x.min(), 0.0)
            xmax = jnp.maximum(x.max(), 0.0)
            scale = jnp.maximum((xmax - xmin) / qmax, EPS)
            zp = jnp.round(-xmin / scale)
            q = jnp.clip(jnp.round(x / scale) + zp, 0, qmax)
            return (q - zp) * scale

        def fq_act_sym(x, bits=A_BITS):
            qmax = 2 ** (bits - 1) - 1
            scale = jnp.maximum(jnp.abs(x).max() / qmax, EPS)
            q = jnp.clip(jnp.round(x / scale), -qmax - 1, qmax)
            return q * scale

        def fq_weight(w, bits=W_BITS):
            qmax = 2 ** (bits - 1) - 1
            scale = jnp.maximum(jnp.abs(w).max(axis=1, keepdims=True) / qmax, EPS)
            q = jnp.clip(jnp.round(w / scale), -qmax - 1, qmax)
            return q * scale
        global_max_x = jnp.abs(x).max(axis=(0, 1))
        max_weight = jnp.abs(w1).max(axis=0)
        cs = global_max_x ** ALPHA / max_weight ** (1.0 - ALPHA)
        cs = 2.0 ** round_ln(cs)
        x_smoothed = x / cs[None, None, :]
        w1_smoothed = w1 * cs[None, :]
        xq = fq_act_asym(x_smoothed)
        h = jnp.einsum('bnc,hc->bnh', xq, fq_weight(w1_smoothed)) + b1
        h = jax.nn.gelu(h, approximate=False)
        hq = fq_act_sym(h)
        out = jnp.einsum('bnh,ch->bnc', hq, fq_weight(w2)) + b2
        out = fq_act_asym(out)
        return out
    h = _L0_tok_ref(x, L0_tok_w_qkv, L0_tok_b_qkv, L0_tok_w_proj, L0_tok_b_proj)
    h = h + _L0_attn_ref(_layernorm(h, axis=-1), L0_attn_qkv_w, L0_attn_qkv_b, L0_attn_qkv_B, L0_attn_proj_w, L0_attn_proj_b, L0_attn_proj_B)
    h = h + _L0_ffn_ref(_layernorm(h, axis=-1), L0_ffn_ln1_g, L0_ffn_ln1_b, L0_ffn_qkv_w, L0_ffn_proj_w, L0_ffn_proj_b, L0_ffn_ln2_g, L0_ffn_ln2_b, L0_ffn_gate_w, L0_ffn_gate_b, L0_ffn_w1, L0_ffn_b1, L0_ffn_w2, L0_ffn_b2)
    h = h + _L1_attn_ref(_layernorm(h, axis=-1), L1_attn_w_qkv, L1_attn_w_proj, L1_attn_b_proj)
    h = h + _L1_ffn_ref(_layernorm(h, axis=-1), L1_ffn_w1, L1_ffn_b1, L1_ffn_w2, L1_ffn_b2)
    return h

_drawn_inputs = setup_inputs


def setup_inputs(seed=0):
    import zlib

    import numpy as np

    out = dict(_drawn_inputs(seed))
    spreads = {'L0_tok_b_qkv': (0.0, 0.1),
     'L0_tok_b_proj': (0.0, 0.1),
     'L0_attn_qkv_b': (0.0, 0.1),
     'L0_attn_proj_b': (0.0, 0.1),
     'L0_ffn_ln1_g': (1.0, 0.6),
     'L0_ffn_ln1_b': (0.0, 0.8),
     'L0_ffn_proj_b': (0.0, 0.1),
     'L0_ffn_ln2_g': (1.0, 0.546),
     'L0_ffn_ln2_b': (0.0, 0.621),
     'L0_ffn_gate_b': (0.0, 0.1),
     'L0_ffn_b1': (0.0, 0.64),
     'L0_ffn_b2': (0.0, 0.1),
     'L1_attn_b_proj': (0.0, 0.1)}
    factors = {'L1_ffn_b1': 8.0, 'L1_ffn_b2': 6.059}
    for name, (base, spread) in spreads.items():
        noise = np.random.default_rng([zlib.crc32(name.encode()), seed]).standard_normal(out[name].shape)
        drawn = base * np.exp(spread * noise) if base else spread * noise
        out[name] = jnp.asarray(drawn.astype(out[name].dtype))
    for name, factor in factors.items():
        out[name] = (out[name] * factor).astype(out[name].dtype)
    return out
```

```python
from contextlib import ExitStack

import numpy as np

import concourse.bass as bass
from concourse import mybir
from concourse.alu_op_type import AluOpType as ALU

ACT = mybir.ActivationFunctionType
F32 = mybir.dt.float32
BF16 = mybir.dt.bfloat16
I32 = mybir.dt.int32
U32 = mybir.dt.uint32
X = mybir.AxisListType.X

P = 128
B = 16
N_IN = 512
C = 192
HEADS = 12
HD = C // HEADS
STRIDE = 4
WINDOWS = 2
WQ = 64
HC = C // 2
GROUPS = 3
EXPERTS = 8
HIDDEN = 768
HT = HIDDEN // P
T = B * P
TG = 512
NG = T // TG
LN_EPS = 1e-5
SCALE = float(HD) ** -0.5
OT_REG = 0.1
SINKHORN_ITERS = 10
DIAG_VAL = 1000.0
Q_EPS = 1e-8
ROUND = 12582912.0
STREAMS = 2

SHARED = {
    **{k: [("n0", "n1", "n2", "n3", "n5")] for k in ("stats", "kept")},
    "mv": [("n0", "n1", "n2", "n3", "n4", "n5")],
    **{k: [("at", "ff", "ff2", "l1", "q")] for k in ("xn", "xturned")},
    "xT": [("at", "ff", "ff2", "l1")],
    **{k: [("at", "ff")] for k in ("qkv", "pad", "qkturned", "qkT")},
    **{k: [("tok1", "at", "ff")] for k in ("scores", "max", "shifted", "pturned", "pT_a", "pT_b")},
    "probs": [("tok1", "at", "ff", "l1")],
    **{k: [("tok", "at", "ff", "l1")] for k in ("pv", "rec", "on", "oturned", "onT", "proj")},
    **{k: [("at", "ff", "l1")] for k in ("biased", "h")},
}

LAYOUT = [
    ("tok_w", HC, 2 * 3 * C), ("tok_b", P, 3 * C), ("tok_pw", HC, 2 * C), ("tok_pb", P, C),
    ("at_w", HC, 2 * 3 * C), ("at_b", P, 3 * C), ("at_pw", HC, 2 * C), ("at_pb", P, C),
    ("ff_w", HC, 2 * 3 * C), ("ff_pw", HC, 2 * C), ("ff_pb", P, C), ("ln1_g", HC, 2), ("ln1_b", HC, 2),
    ("ln2_g", HC, 2), ("ln2_b", HC, 2), ("gate_w", HC, 2 * EXPERTS), ("gate_b", P, EXPERTS),
    ("b1", P, EXPERTS * HT), ("b2", EXPERTS, C),
    ("l1_w", HC, 2 * 3 * C), ("l1_pw", HC, 2 * C), ("l1_pb", P, C),
    ("q_b1", P, HT), ("q_b2", P, C), ("q_w1", P, HT * C), ("q_w2", HC, 2 * HIDDEN),
]
OFFSET = {}
_at = 0
for _name, _rows, _cols in LAYOUT:
    OFFSET[_name] = (_at, _rows, _cols)
    _at += _cols
PACKED = _at


def build(nc, x, packed, w1, w2, out):
    with ExitStack() as ctx:
        def sb(name, shape, dt=F32):
            return ctx.enter_context(nc.sbuf_tensor(name, shape, dt))

        sems = {}

        def shared(name):
            part, _, stage = name.partition("_")
            parts = SHARED.get(stage, ())
            for group in parts:
                if part in group:
                    return stage + "_" * parts.index(group), group.index(part)
            return name, 0

        def after(name, n):
            return sem(name), n + B * shared(name)[1]

        def sem(name):
            name = shared(name)[0]
            if name not in sems:
                sems[name] = ctx.enter_context(nc.semaphore(name))
            return sems[name]

        ps = [ctx.enter_context(nc.psum_tensor(f"ps{s}", [P, 4, 512], F32)) for s in range(STREAMS)]

        consts = sb("consts", [P, PACKED])

        def const(name):
            at, rows, cols = OFFSET[name]
            return consts[0:rows, at:at + cols]

        def chunks(name):
            return const(name).rearrange("p (c n) -> p c n", c=2)

        ident = sb("ident", [P, P])
        identb = sb("identb", [P, P], BF16)
        diag_off = sb("diag_off", [P, GROUPS, P], BF16)
        diag_one = sb("diag_one", [P, P])
        ones = sb("ones", [P, P])
        pick = sb("pick", [3 * HEADS, HEADS, P], BF16)
        iota8 = sb("iota8", [P, EXPERTS])

        hs = sb("hs", [P, B, C])
        featT = sb("featT", [HC, 2, T])
        logits = sb("logits", [P, B, EXPERTS])
        cw = sb("cw", [P, B, EXPERTS])

        ARENA = 9984
        arena = sb("arena", [P, STREAMS, ARENA])

        ffw = sb("ffw", [P, HT * T // 2])
        ew1 = [ffw[0:HC, k * 2 * HIDDEN:(k + 1) * 2 * HIDDEN].rearrange("p (c n) -> p c n", c=2) for k in range(2)]
        ew2 = [ffw[:, 4 * HIDDEN + k * HT * C:4 * HIDDEN + (k + 1) * HT * C].rearrange("p (m n) -> p m n", m=HT)
               for k in range(2)]
        hqs = [ffw[:, g * HT * TG // 2:(g + 1) * HT * TG // 2].bitcast(BF16).rearrange("p (m n) -> p m n", m=HT)
               for g in range(NG)]
        small = sb("small", [P, 96])
        allstats = sb("allstats", [P, B, 6])
        meanvar = sb("meanvar", [P, B, 2])
        rstd = sb("rstd", [P, B])
        newton = sb("newton", [P, B])
        varp = sb("varp", [P, B])
        x3 = sb("x3", [P, B, C])
        b1cur = sb("b1cur", [P, 2, HT])
        cwcur = sb("cwcur", [P, 2, B])
        neg_reg = sb("neg_reg", [P, 1])
        idx8 = sb("idx8", [P, B, 8], U32)
        top8 = sb("top8", [P, B, 8])
        gidx = sb("gidx", [P, B, 2])
        gw = sb("gw", [P, B, 4])
        sw2row = sb("sw2row", [P, C])
        xq = sb("xq", [HC, 2, T], BF16)

        class Buffers:
            pass

        bufs = []
        for s in range(STREAMS):
            b = Buffers()
            used = [0]

            def take(*dims, rows=P):
                n = int(np.prod(dims))
                v = arena[0:rows, s, used[0]:used[0] + n]
                used[0] += n
                if len(dims) == 2:
                    return v.rearrange("p (a b) -> p a b", a=dims[0])
                if len(dims) == 3:
                    return v.rearrange("p (a b c) -> p a b c", a=dims[0], b=dims[1])
                return v

            b.qk_pad = take(5 * HEADS, 32)
            b.v_ext = take(4 * HEADS, HD + 1)
            b.qT = take(GROUPS, P)
            b.kT = take(GROUPS, STRIDE, P)
            parts = b.kT.rearrange("p g t n -> p (g t n)").bitcast(BF16)
            b.hi, b.lo = parts[:, 0:HEADS * P], parts[:, HEADS * P:2 * HEADS * P]
            spare = b.qk_pad.rearrange("p h d -> p (h d)")[:, 2 * HEADS * 32:5 * HEADS * 32].bitcast(BF16)
            b.v_hi = spare[:, 0:204].rearrange("p (h d) -> p h d", h=HEADS)
            b.v_lo = spare[:, 204:408].rearrange("p (h d) -> p h d", h=HEADS)
            b.x_parts = spare[:, 408:408 + 2 * HEADS].rearrange("p (h k) -> p h k", k=2)
            b.u_parts = spare[:, 440:440 + P]
            b.uT_parts = spare[0:3 * HEADS, 600:600 + P]
            b.p = take(HEADS * P)
            b.pT = take(HEADS * P)
            b.xT = take(2, N_IN, rows=HC)
            b.xn = take(C)
            b.t1 = take(C)
            b.on = take(C)
            b.onT = take(2, P, rows=HC)
            b.stats = take(8)
            b.mv = take(4)
            b.mx = take(HEADS)
            b.rec = take(HEADS)
            b.nt = take(HEADS)
            b.n2 = take(HEADS)
            b.stats12 = take(HEADS)
            b.maxdiag = take(HEADS, rows=HEADS)
            b.sv = take(HEADS)
            assert used[0] <= ARENA, used
            bufs.append(b)

        def loaded(eng):
            eng.wait_ge(sem("consts_loaded"), 16)
            eng.wait_ge(sem("masks_ready"), 6)
            eng.wait_ge(sem("pick_ready"), 3)
            eng.wait_ge(sem("pads_ready"), 2 * STREAMS + 1)

        block = ctx.enter_context(nc.Block())


        def dve_stats(dve, part, s, n, i, keep):
            b = bufs[s]
            nc.vector.bn_stats(b.stats[:, 0:6], b.t1).then_inc(sem(f"{part}_stats"), 1)
            nc.vector.tensor_copy(keep, b.t1).then_inc(sem(f"{part}_kept"), 1)
            dve.wait_ge(*after(f"{part}_stats", n))
            nc.vector.tensor_scalar(allstats[:, bass.ds(i + s, 1), :].rearrange("p o c -> p (o c)"),
                                    b.stats[:, 0:6], 1.0, None, ALU.mult).then_inc(sem(f"{part}_mv"), 1)

        def rsqrt_steps(y, v, t):
            yield nc.vector.tensor_scalar(y.bitcast(I32), v.bitcast(I32), -0.5, 1597463007.0, ALU.mult, ALU.add)
            for _ in range(3):
                yield nc.vector.tensor_tensor(t, y, y, ALU.mult)
                yield nc.vector.scalar_tensor_tensor(out=t, in0=t, scalar=-0.5, in1=v, op0=ALU.mult, op1=ALU.mult)
                yield nc.vector.scalar_tensor_tensor(out=y, in0=t, scalar=1.5, in1=y, op0=ALU.add, op1=ALU.mult)

        def dve_normalize(dve, pre, s, n, i, src, dst):
            nc.vector.tensor_scalar(dst, src, meanvar[:, bass.ds(i + s, 1), 0:1].rearrange("p o c -> p (o c)"),
                                    rstd[:, bass.ds(i + s, 1)], ALU.subtract, ALU.mult).then_inc(
                                        sem(f"{pre}_xn"), 1)

        def pe_turn(pe, wait, done, s, n, src, bank):
            pe.wait_ge(*after(wait, n))
            for c in range(2):
                last = nc.tensor.transpose(ps[s][0:HC, bank, c * P:(c + 1) * P],
                                           src[:, c * HC:(c + 1) * HC], ident[:, :])
            last.then_inc(sem(done), 1)

        def act_turned(act, wait, done, s, n, dst, bank, gain=None, bias=None):
            act.wait_ge(*after(wait, n))
            if gain is None:
                nc.scalar.activation(dst, ps[s][0:HC, bank, 0:2 * P].rearrange("p (c n) -> p c n", c=2),
                                     ACT.Copy).then_inc(sem(done), 1)
                return
            for c in range(2):
                last = nc.scalar.activation(dst[:, c, :], ps[s][0:HC, bank, c * P:(c + 1) * P], ACT.Identity,
                                            bias=bias[:, c:c + 1], scale=gain[:, c:c + 1])
            last.then_inc(sem(done), 1)

        def at_pe_qkv(pe, pre, s, n, w):
            pe.wait_ge(*after(f"{pre}_xT", n))
            xT = bufs[s].xT
            for c in range(2):
                nc.tensor.matmul(ps[s][:, 0, 0:2 * C], xT[:, c, 0:P], w[:, c, 0:2 * C],
                                 start=(c == 0), stop=(c == 1))
            for c in range(2):
                last = nc.tensor.matmul(ps[s][:, 1, 0:C], xT[:, c, 0:P], w[:, c, 2 * C:3 * C],
                                        start=(c == 0), stop=(c == 1))
            last.then_inc(sem(f"{pre}_qkv"), 1)

        def at_dve_qkv(dve, pre, s, n, bias):
            b = bufs[s]
            dve.wait_ge(*after(f"{pre}_qkv", n))
            qk = ps[s][:, 0, 0:2 * C].rearrange("p (h d) -> p h d", d=HD)
            v = ps[s][:, 1, 0:C].rearrange("p (h d) -> p h d", d=HD)
            if bias is None:
                nc.vector.tensor_copy(b.qk_pad[:, 0:2 * HEADS, 0:HD], qk)
                last = nc.vector.tensor_copy(b.v_ext[:, 0:HEADS, 0:HD], v)
            else:
                bv = bias.rearrange("p (h d) -> p h d", d=HD)
                nc.vector.tensor_tensor(b.qk_pad[:, 0:2 * HEADS, 0:HD], qk, bv[:, 0:2 * HEADS, :], ALU.add)
                last = nc.vector.tensor_tensor(b.v_ext[:, 0:HEADS, 0:HD], v, bv[:, 2 * HEADS:, :], ALU.add)
            last.then_inc(sem(f"{pre}_pad"), 1)

        def at_pe_turn_qk(pe, pre, s, n):
            pe.wait_ge(*after(f"{pre}_pad", n))
            b = bufs[s]
            for g in range(2 * GROUPS):
                last = nc.tensor.transpose(ps[s][:, g // 4, (g % 4) * P:(g % 4 + 1) * P],
                                           b.qk_pad[:, 4 * g:4 * g + 4, :], ident[:, :])
            last.then_inc(sem(f"{pre}_qkturned"), 1)

        def at_act_qk(act, pre, s, n):
            b = bufs[s]
            act.wait_ge(*after(f"{pre}_qkturned", n))
            flat = ps[s][:, 0:2, :].rearrange("p b n -> p (b n)")
            nc.scalar.activation(b.kT[:, :, 0, :], flat[:, GROUPS * P:2 * GROUPS * P].rearrange(
                "p (g n) -> p g n", g=GROUPS), ACT.Copy)
            nc.scalar.activation(b.qT, flat[:, 0:GROUPS * P].rearrange("p (g n) -> p g n", g=GROUPS),
                                 ACT.Copy).then_inc(sem(f"{pre}_qkT"), 1)

        HEAD_ORDER = [g * 4 + j for g in range(GROUPS) for j in range(4)]

        SUMS = 400
        TOK_PV = 300

        def place(h):
            return (h % 4) * GROUPS + h // 4

        def score_view(s):
            return ps[s][:, :, 0:GROUPS * P].rearrange("p j (g k) -> p j g k", g=GROUPS)

        def at_pe_scores(pe, pre, s, n):
            b = bufs[s]
            pe.wait_ge(*after(f"{pre}_qkT", n))
            for h in HEAD_ORDER:
                g, r = h // 4, 32 * (h % 4)
                last = nc.tensor.matmul(ps[s][:, h % 4, g * P:(g + 1) * P], b.qT[r:r + HD, g, :],
                                        b.kT[r:r + HD, g, 0, :], start=True, stop=True)
            last.then_inc(sem(f"{pre}_scores"), 1)

        def dve_softmax_shift(dve, wait, pre, s, n, sc, a, g, keys):
            b = bufs[s]
            dve.wait_ge(*after(wait, n))
            for k in range(a):
                last = nc.vector.tensor_reduce(b.mx[:, k * g:(k + 1) * g], sc[:, k], X, ALU.max)
            last.then_inc(sem(f"{pre}_max"), 1)
            dve.wait_ge(*after(f"{pre}_max", n))
            p4 = b.p.rearrange("p (a g k) -> p a g k", a=a, g=g)
            for k in range(a):
                last = nc.vector.tensor_tensor(p4[:, k], sc[:, k],
                                               b.mx[:, k * g:(k + 1) * g].unsqueeze(2).to_broadcast([P, g, keys]),
                                               ALU.subtract)
            last.then_inc(sem(f"{pre}_shifted"), 1)

        def act_exp(act, pre, s, n):
            act.wait_ge(*after(f"{pre}_shifted", n))
            nc.scalar.activation(bufs[s].p, bufs[s].p, ACT.Exp, scale=SCALE).then_inc(sem(f"{pre}_probs"), 1)

        def pe_turn_probs(pe, pre, s, n):
            pe.wait_ge(*after(f"{pre}_probs", n))
            for k in range(HEADS):
                last = nc.tensor.transpose(ps[s][:, k // 4, (k % 4) * P:(k % 4 + 1) * P],
                                           bufs[s].p[:, k * P:(k + 1) * P], ident[:, :])
            last.then_inc(sem(f"{pre}_pturned"), 1)

        def act_probs(act, pre, s, n):
            act.wait_ge(*after(f"{pre}_pturned", n))
            nc.scalar.activation(bufs[s].pT[:, 0:8 * P],
                                 ps[s][:, 0:2, :].rearrange("p b n -> p (b n)"),
                                 ACT.Copy).then_inc(sem(f"{pre}_pT_a"), 1)

        def dve_probs(dve, pre, s, n):
            dve.wait_ge(*after(f"{pre}_pturned", n))
            nc.vector.tensor_copy(bufs[s].pT[:, 8 * P:12 * P], ps[s][:, 2, :]).then_inc(sem(f"{pre}_pT_b"), 1)

        def at_pe_pv(pe, pre, s, n):
            b = bufs[s]
            pe.wait_ge(*after(f"{pre}_pT_a", n))
            pe.wait_ge(*after(f"{pre}_pT_b", n))
            for h in range(HEADS):
                last = nc.tensor.matmul(ps[s][:, 3, h * (HD + 1):(h + 1) * (HD + 1)], b.pT[:, place(h) * P:(place(h) + 1) * P],
                                        b.v_ext[:, h, :], start=True, stop=True)
            last.then_inc(sem(f"{pre}_pv"), 1)

        def dve_softmax_norm(dve, pre, s, n, at=0):
            b = bufs[s]
            dve.wait_ge(*after(f"{pre}_pv", n))
            o = ps[s][:, 3, at:at + HEADS * (HD + 1)].rearrange("p (h d) -> p h d", h=HEADS)
            nc.vector.reciprocal(b.rec[:, :], o[:, :, HD]).then_inc(sem(f"{pre}_rec"), 1)
            dve.wait_ge(*after(f"{pre}_rec", n))
            nc.vector.tensor_tensor(b.on.rearrange("p (h d) -> p h d", h=HEADS), o[:, :, 0:HD],
                                    b.rec.unsqueeze(2).to_broadcast([P, HEADS, HD]),
                                    ALU.mult).then_inc(sem(f"{pre}_on"), 1)

        def pe_project(pe, pre, s, n, w):
            pe.wait_ge(*after(f"{pre}_onT", n))
            for c in range(2):
                last = nc.tensor.matmul(ps[s][:, 1, 0:C], bufs[s].onT[:, c, :], w[:, c, :],
                                        start=(c == 0), stop=(c == 1))
            last.then_inc(sem(f"{pre}_proj"), 1)

        def half_steps(i, s, it):
            return i * (2 * SINKHORN_ITERS) + STREAMS * it + s + 1

        def halfs(i, s, it):
            return i * (2 * SINKHORN_ITERS - 1) + STREAMS * it + s + 1

        def both(step, n0, *args):
            for s in range(STREAMS):
                step(s, n0 + s, *args)

        @block.sync
        def _(sp):
            sp.dma_start(consts[:, :], packed[:, :]).then_inc(sem("consts_loaded"), 16)
            for s in range(STREAMS):
                sp.dma_start(bufs[s].xT, x[s]).then_inc(sem(f"tok_x{s}"), 16)
            with sp.Fori(0, B - 2 * STREAMS + 1, STREAMS) as i:
                for s in range(STREAMS):
                    sp.wait_ge(sem("tok_v"), i + s + 1)
                    sp.dma_start(bufs[s].xT, x[bass.ds(i + s + STREAMS, 1), :, :, :].rearrange(
                        "o p c n -> (o p) c n")).then_inc(sem(f"tok_x{s}"), 16)
            for k in range(2):
                sp.dma_start(ew1[k], w1[k]).then_inc(sem(f"moe_w1_{k}"), 16)
                sp.dma_start(ew2[k], w2[k]).then_inc(sem(f"moe_w2_{k}"), 16)
            with sp.Fori(0, EXPERTS - 3, 2) as e:
                for k in range(2):
                    sp.wait_ge(sem("moe_out"), e * B + (k + 1) * B + 8)
                    sp.dma_start(ew1[k], w1[bass.ds(e + k + 2, 1), :, :, :].rearrange(
                        "o p c n -> (o p) c n")).then_inc(sem(f"moe_w1_{k}"), 16)
                    sp.dma_start(ew2[k], w2[bass.ds(e + k + 2, 1), :, :, :].rearrange(
                        "o p c n -> (o p) c n")).then_inc(sem(f"moe_w2_{k}"), 16)
            sp.wait_ge(sem("result"), 1)
            for w in range(WINDOWS):
                sp.dma_start(out.rearrange("b (q w) c -> w q b c", w=WINDOWS)[w],
                             hs[w * WQ:(w + 1) * WQ, :, :]).then_inc(sem("stored"), 16)
            sp.wait_ge(sem("stored"), 16 * WINDOWS)

        flat_arena = arena[:, :, :].rearrange("p s n -> p (s n)")
        he = [flat_arena[:, k * HT * TG:(k + 1) * HT * TG].rearrange("p (m n) -> p m n", m=HT) for k in range(2)]
        gelu_out = flat_arena[:, 0:HT * T].rearrange("p (m n) -> p m n", m=HT)

        def bf(lo, words):
            return flat_arena[:, lo:lo + words].bitcast(BF16)

        q_at = HT * T
        wq1T = bf(q_at, HT * P)[0:HC, :].rearrange("p (c n) -> p c n", c=2)
        wq2T = bf(q_at + HT * P, HT * C // 2).rearrange("p (m n) -> p m n", m=HT)
        q_end = q_at + HT * P + HT * C // 2
        w1_s = flat_arena[:, q_end:q_end + HT * C].rearrange("p (m n) -> p m n", m=HT)
        w1_q = bf(q_end + HT * C, HT * C // 2).rearrange("p (m n) -> p m n", m=HT)
        w2_q = bf(q_end + HT * C + HT * C // 2, HIDDEN)[0:HC, :].rearrange("p (c n) -> p c n", c=2)
        q_end2 = q_end + HT * C + HT * C // 2 + HIDDEN
        csb = flat_arena[0:HC, q_end2:q_end2 + 2 * P].rearrange("p (c n) -> p c n", c=2)
        sw2b = flat_arena[0:HC, q_end2 + 2 * P:q_end2 + 4 * P].rearrange("p (c n) -> p c n", c=2)
        assert q_end2 + 4 * P <= STREAMS * ARENA
        oq = flat_arena[:, q_end:q_end + B * C].rearrange("p (b n) -> p b n", b=B)
        wmax = flat_arena[:, q_end2 + 4 * P:q_end2 + 4 * P + C]
        assert q_end2 + 4 * P + C <= STREAMS * ARENA

        @block.gpsimd
        def _(pool):
            nc.gpsimd.memset(ident[:, :], 0.0).then_inc(sem("mask_zero"), 1)
            nc.gpsimd.memset(identb[:, :], 0.0).then_inc(sem("mask_zero"), 1)
            nc.gpsimd.memset(diag_off[:, :, :], 0.0).then_inc(sem("mask_zero"), 1)
            nc.gpsimd.memset(diag_one[:, :], 0.0).then_inc(sem("mask_zero"), 1)
            nc.gpsimd.memset(pick[:, :, :], 0.0).then_inc(sem("mask_zero"), 1)
            nc.gpsimd.memset(ones[:, :], 1.0).then_inc(sem("masks_ready"), 1)
            pool.wait_ge(sem("mask_zero"), 5)
            for k in range(3):
                nc.gpsimd.affine_select(out=pick[:, :, :], in_=pick[:, :, :], compare_op=ALU.not_equal, fill=1.0,
                                        base=-HEADS * k, pattern=[[-1, HEADS], [0, P]],
                                        channel_multiplier=1).then_inc(sem("pick_ready"), 1)
                pool.wait_ge(sem("pick_ready"), k + 1)
            for m, fill in ((ident, 1.0), (identb, 1.0), (diag_one, float(np.exp(SCALE) - 1.0))):
                nc.gpsimd.affine_select(out=m[:, :], in_=m[:, :], compare_op=ALU.not_equal, fill=fill, base=0,
                                        pattern=[[-1, P]], channel_multiplier=1).then_inc(sem("masks_ready"), 1)
            nc.gpsimd.affine_select(out=diag_off[:, :, :], in_=diag_off[:, :, :], compare_op=ALU.not_equal,
                                    fill=-DIAG_VAL, base=0, pattern=[[0, GROUPS], [-1, P]],
                                    channel_multiplier=1).then_inc(sem("masks_ready"), 1)
            nc.gpsimd.iota(iota8[:, :], pattern=[[1, EXPERTS]], base=0, channel_multiplier=0,
                           allow_small_or_imprecise_dtypes=True).then_inc(sem("masks_ready"), 1)

        def moe_up(pe, e, k, g):
            for m in range(HT):
                q = g * HT + m
                pe.wait_ge(sem("moe_gelu"), e * (NG * HT) + k * NG * HT + q + 1)
                for c in range(2):
                    last = nc.tensor.matmul(ps[0][:, q % 4, :], ew1[k][:, c, m * P:(m + 1) * P],
                                            featT[:, c, g * TG:(g + 1) * TG], start=(c == 0), stop=(c == 1))
                last.then_inc(sem("moe_hidden"), 1)

        def moe_down(pe, e, k, g):
            pe.wait_ge(sem("moe_gelu"), e * (NG * HT) + k * NG * HT + (g + 1) * HT + 4)
            for t in range(4):
                pe.wait_ge(sem("moe_added"), e * B + k * B + g * 4 + t + 1)
                for m in range(HT):
                    last = nc.tensor.matmul(ps[1][:, t, 0:C], he[g % 2][:, m, t * P:(t + 1) * P], ew2[k][:, m, :],
                                            start=(m == 0), stop=(m == HT - 1))
                last.then_inc(sem("moe_out"), 1)

        @block.tensor
        def _(pe):
            loaded(pe)

            tok_w, tok_pw = chunks("tok_w"), chunks("tok_pw")

            def tiles(s, lo, n):
                return ps[s][:, lo:lo + n // 2, :].rearrange("p b n -> p (b n)").rearrange(
                    "p (t n) -> p t n", t=n)

            def tok_qk(s, n, dma):
                pe.wait_ge(sem(f"tok_x{s}"), dma)
                xT = bufs[s].xT
                for part in range(2):
                    o = tiles(s, 2 * part, STRIDE)
                    for t in range(STRIDE):
                        for c in range(2):
                            cols = slice(t, N_IN, STRIDE) if part == 0 else slice(t * P, (t + 1) * P)
                            last = nc.tensor.matmul(o[:, t, 0:C], xT[:, c, cols],
                                                    tok_w[:, c, part * C:(part + 1) * C],
                                                    start=(c == 0), stop=(c == 1))
                    last.then_inc(sem(f"tok_{'qk'[part]}"), 1)

            def tok_v(s, n):
                pe.wait_ge(*after("tok_pooled", n))
                o = tiles(s, 0, 4)
                for t in range(4):
                    for c in range(2):
                        last = nc.tensor.matmul(o[:, t, 0:C], bufs[s].xT[:, c, t * P:(t + 1) * P],
                                                tok_w[:, c, 2 * C:3 * C], start=(c == 0), stop=(c == 1))
                last.then_inc(sem("tok_v"), 1)

            def tok_turn_k(s, n):
                pe.wait_ge(*after("tok_vpad", n))
                b = bufs[s]
                for g in range(GROUPS):
                    for t in range(STRIDE):
                        at = (1 + t) * HEADS + 4 * g
                        nc.tensor.transpose(ps[s][:, g, t * P:(t + 1) * P], b.qk_pad[:, at:at + 4, :], ident[:, :])
                for g in range(GROUPS):
                    last = nc.tensor.transpose(ps[s][:, 3, g * P:(g + 1) * P], b.qk_pad[:, 4 * g:4 * g + 4, :],
                                               ident[:, :])
                last.then_inc(sem("tok_turned"), 1)

            def tok_scores(s, n, half):
                b = bufs[s]
                if half == 0:
                    pe.wait_ge(*after("tok_kT", n))
                    pe.wait_ge(*after("tok_qT", n))
                else:
                    pe.wait_ge(*after("tok0_pT_a", n))
                    pe.wait_ge(*after("tok0_pT_b", n))
                for g in range(GROUPS):
                  for jj in range(2):
                    r = 32 * (2 * half + jj)
                    for w in range(WINDOWS):
                        last = nc.tensor.matmul(
                            ps[s][w * WQ:(w + 1) * WQ, 2 * jj + g // 2, (g % 2) * 256:(g % 2 + 1) * 256],
                            b.qT[r:r + HD, g, w * WQ:(w + 1) * WQ], b.kT[r:r + HD, g, 2 * w:2 * w + 2, :],
                            start=True, stop=True)
                last.then_inc(sem(f"tok{half}_scores"), 1)

            def tok_pv(s, n, half):
                b = bufs[s]
                pe.wait_ge(*after(f"tok{half}_pT_a", n))
                pe.wait_ge(*after(f"tok{half}_pT_b", n))
                pT = b.pT.rearrange("p (l h n) -> p l h n", l=6, h=2)
                for l in range(6):
                    h = 4 * (l % GROUPS) + 2 * half + l // GROUPS
                    at = TOK_PV + h * (HD + 1)
                    for w in range(WINDOWS):
                        for k in range(2):
                            last = nc.tensor.matmul(
                                ps[s][w * WQ:(w + 1) * WQ, 3, at:at + HD + 1],
                                pT[:, l, k, w * WQ:(w + 1) * WQ], b.v_ext[:, (2 * w + k) * HEADS + h, :],
                                start=(k == 0), stop=(k == 1))
                last.then_inc(sem(f"tok{half}_pv" if half == 0 else "tok_pv"), 1)

            with pe.Fori(0, B - STREAMS + 1, STREAMS) as i:
                for s in range(STREAMS):
                    tok_qk(s, i + s + 1, i * (16 // STREAMS) + 16)
                both(tok_v, i + 1)
                both(tok_turn_k, i + 1)
                for half in range(2):
                    both(tok_scores, i + 1, half)
                    both(lambda s, n: pe_turn_probs(pe, f"tok{half}", s, n), i + 1)
                    both(tok_pv, i + 1, half)
                both(lambda s, n: pe_turn(pe, "tok_on", "tok_oturned", s, n, bufs[s].on, 0), i + 1)
                both(lambda s, n: pe_project(pe, "tok", s, n, tok_pw), i + 1)
                pe.wait_ge(sem("tok_h"), i + STREAMS)

            for pre, w, pw in (("at", chunks("at_w"), chunks("at_pw")), ("ff", chunks("ff_w"), chunks("ff_pw"))):
                with pe.Fori(0, B - STREAMS + 1, STREAMS) as i:
                    both(lambda s, n: pe_turn(pe, f"{pre}_xn", f"{pre}_xturned", s, n, bufs[s].xn, 0), i + 1)
                    both(lambda s, n: at_pe_qkv(pe, pre, s, n, w), i + 1)
                    both(lambda s, n: at_pe_turn_qk(pe, pre, s, n), i + 1)
                    both(lambda s, n: at_pe_scores(pe, pre, s, n), i + 1)
                    both(lambda s, n: pe_turn_probs(pe, pre, s, n), i + 1)
                    both(lambda s, n: at_pe_pv(pe, pre, s, n), i + 1)
                    both(lambda s, n: pe_turn(pe, f"{pre}_on", f"{pre}_oturned", s, n, bufs[s].on, 0), i + 1)
                    both(lambda s, n: pe_project(pe, pre, s, n, pw), i + 1)
            with pe.Fori(0, B - STREAMS + 1, STREAMS) as i:
                both(lambda s, n: pe_turn(pe, "ff2_xn", "ff2_xturned", s, n, bufs[s].xn, 0), i + 1)

                def gate(s, n):
                    pe.wait_ge(*after("ff2_xT", n))
                    for c in range(2):
                        last = nc.tensor.matmul(ps[s][:, 1, 0:EXPERTS], bufs[s].xT[:, c, 0:P],
                                                chunks("gate_w")[:, c, :], start=(c == 0), stop=(c == 1))
                    last.then_inc(sem("ff_logits"), 1)
                both(gate, i + 1)

            pe.wait_ge(sem("moe_cw"), 1)
            with pe.Fori(0, B - STREAMS + 1, STREAMS) as i:
                def turn_cw(s, n):
                    pe.wait_ge(*after("moe_cw_copy", n))
                    nc.tensor.transpose(ps[s][0:EXPERTS, 0, 0:P], bufs[s].xn[:, 0:EXPERTS],
                                        ident[:, :]).then_inc(sem("moe_cwturned"), 1)

                def bias2(s, n):
                    pe.wait_ge(*after("moe_cwT", n))
                    nc.tensor.matmul(ps[s][:, 1, 0:C], bufs[s].onT[0:EXPERTS, 0, :], const("b2"),
                                     start=True, stop=True).then_inc(sem("moe_bias2"), 1)
                both(turn_cw, i + 1)
                both(bias2, i + 1)
            pe.wait_ge(sem("moe_start"), 1)
            with pe.Fori(0, EXPERTS - 1, 2) as e:
                for k in range(2):
                    pe.wait_ge(sem(f"moe_w1_{k}"), e * 8 + 16)
                    pe.wait_ge(sem(f"moe_w2_{k}"), e * 8 + 16)
                    for g in range(NG):
                        moe_up(pe, e, k, g)
                        if g > 0:
                            moe_down(pe, e, k, g - 1)
                    moe_down(pe, e, k, NG - 1)

            with pe.Fori(0, B - STREAMS + 1, STREAMS) as i:
                l1_w, l1_pw = chunks("l1_w"), chunks("l1_pw")
                both(lambda s, n: pe_turn(pe, "l1_xn", "l1_xturned", s, n, bufs[s].xn, 0), i + 1)

                def l1_qv(s, n):
                    pe.wait_ge(*after("l1_xT", n))
                    for part in range(2):
                        for c in range(2):
                            last = nc.tensor.matmul(ps[s][:, part, 0:C], bufs[s].xT[:, c, 0:P],
                                                    l1_w[:, c, 2 * part * C:(2 * part + 1) * C],
                                                    start=(c == 0), stop=(c == 1))
                    last.then_inc(sem("l1_qv"), 1)
                both(l1_qv, i + 1)

                def l1_turn_q(s, n):
                    pe.wait_ge(*after("l1_pad", n))
                    for g in range(GROUPS):
                        last = nc.tensor.transpose(ps[s][:, 3, g * P:(g + 1) * P],
                                                   bufs[s].qk_pad[:, 4 * g:4 * g + 4, :], ident[:, :])
                    last.then_inc(sem("l1_qturned"), 1)
                both(l1_turn_q, i + 1)

                def l1_gram(s, n):
                    b = bufs[s]
                    pe.wait_ge(*after("l1_qT", n))
                    for j in range(4):
                        nc.tensor.matmul(ps[s][:, j, 0:GROUPS * P], identb[:, :],
                                         diag_off[:, :, :].rearrange("p a n -> p (a n)"),
                                         start=True, stop=False, skip_group_check=True)
                    for h in HEAD_ORDER:
                        g, r = h // 4, 32 * (h % 4)
                        last = nc.tensor.matmul(ps[s][:, h % 4, g * P:(g + 1) * P], b.qT[r:r + HD, g, :],
                                                b.qT[r:r + HD, g, :], start=False, stop=True,
                                                skip_group_check=True)
                    last.then_inc(sem("l1_gram"), 1)
                both(l1_gram, i + 1)

                def l1_half_step(s, n, i, it):
                    b = bufs[s]
                    if it == 0:
                        pe.wait_ge(*after("l1_kernel_lo", n))
                    else:
                        pe.wait_ge(sem("l1_xlo"), halfs(i, s, it - 1))
                    for k in range(HEADS):
                        for part in (b.hi, b.lo):
                            last = nc.tensor.matmul(ps[s][:, 3, SUMS + 2 * k:SUMS + 2 * k + 2],
                                                    part[:, k * P:(k + 1) * P], b.x_parts[:, k, :],
                                                    start=(part is b.hi), stop=(part is b.lo))
                    last.then_inc(sem("l1_sums"), 1)
                for it in range(2 * SINKHORN_ITERS):
                    both(l1_half_step, i + 1, i, it)

                def l1_turn_u(s, n):
                    pe.wait_ge(*after("l1_uparts", n))
                    nc.tensor.transpose(ps[s][:, 3, 0:P // 2].bitcast(BF16), bufs[s].u_parts,
                                        identb[:, :]).then_inc(sem("l1_uturned"), 1)
                both(l1_turn_u, i + 1)

                def l1_u_rows(s, n):
                    pe.wait_ge(*after("l1_uT", n))
                    for h in range(HEADS):
                        last = nc.tensor.matmul(ps[s][:, h // 4, (h % 4) * P:(h % 4 + 1) * P],
                                                pick[:, h, :], bufs[s].uT_parts, start=True, stop=True)
                    last.then_inc(sem("l1_urows"), 1)
                both(l1_u_rows, i + 1)

                def l1_turn_max(s, n):
                    pe.wait_ge(*after("l1_rowmax", n))
                    nc.tensor.transpose(ps[s][0:HEADS, 3, 0:P], bufs[s].stats12, ident[:, :]).then_inc(
                        sem("l1_maxturned"), 1)
                both(l1_turn_max, i + 1)

                def l1_spread_max(s, n):
                    pe.wait_ge(*after("l1_maxdiag", n))
                    nc.tensor.matmul(ps[s][:, 3, P:P + HEADS], ones[0:HEADS, :], bufs[s].maxdiag,
                                     start=True, stop=True).then_inc(sem("l1_maxspread"), 1)
                both(l1_spread_max, i + 1)

                def l1_pv(s, n):
                    b = bufs[s]
                    pe.wait_ge(*after("l1_probs_lo", n))
                    o = ps[s][:, 3, 0:HEADS * (HD + 1)]
                    nc.tensor.matmul(o, diag_one[:, :], b.v_ext[:, 0:HEADS, :], start=True, stop=False,
                                     skip_group_check=True)
                    for h in range(HEADS):
                        for part in (b.hi, b.lo):
                            for v in (b.v_hi, b.v_lo):
                                last = nc.tensor.matmul(o[:, h * (HD + 1):(h + 1) * (HD + 1)],
                                                        part[:, place(h) * P:(place(h) + 1) * P], v[:, h, :],
                                                        start=False, stop=True, skip_group_check=True)
                    last.then_inc(sem("l1_pv"), 1)
                both(l1_pv, i + 1)
                both(lambda s, n: pe_turn(pe, "l1_on", "l1_oturned", s, n, bufs[s].on, 0), i + 1)
                both(lambda s, n: pe_project(pe, "l1", s, n, l1_pw), i + 1)
            with pe.Fori(0, B - STREAMS + 1, STREAMS) as i:
                both(lambda s, n: pe_turn(pe, "q_xn", "q_xturned", s, n, bufs[s].xn, 0), i + 1)

            p0 = ps[0]
            pe.wait_ge(sem("q_wmax"), 1)
            for c in range(2):
                last = nc.tensor.transpose(p0[0:HC, 3, c * P:(c + 1) * P], wmax[:, c * HC:(c + 1) * HC], ident[:, :])
            last.then_inc(sem("q_wmaxturned"), 1)
            pe.wait_ge(sem("q_cs_rows"), 1)
            for c in range(2):
                last = nc.tensor.matmul(p0[:, 0, c * HC:(c + 1) * HC], csb[:, c, :], ident[0:HC, 0:HC],
                                        start=True, stop=True)
            last.then_inc(sem("q_csrow"), 1)
            pe.wait_ge(sem("q_range"), 1)
            nc.tensor.transpose(p0[0:2, 1, 0:HC], small[0:HC, 20:22], ident[0:HC, 0:HC]).then_inc(
                sem("q_rangeturned"), 1)
            pe.wait_ge(sem("q_rangediag"), 1)
            nc.tensor.matmul(p0[:, 2, 0:2], ones[0:2, :], small[0:2, 24:26], start=True,
                             stop=True).then_inc(sem("q_rangespread"), 1)
            pe.wait_ge(sem("q_w_quant"), 1)
            tb = ps[1][:, :, :].rearrange("p b n -> p (b n)").bitcast(BF16).rearrange("p (b n) -> p b n", b=4)
            for c in range(2):
                for m in range(HT):
                    nc.tensor.transpose(tb[0:HC, c, m * P:(m + 1) * P], w1_q[:, m, c * HC:(c + 1) * HC],
                                        identb[:, :])
            for c in range(2):
                for m in range(HT):
                    last = nc.tensor.transpose(tb[:, 2 + m // 3, (m % 3) * C + c * HC:(m % 3) * C + (c + 1) * HC],
                                               w2_q[:, c, m * P:(m + 1) * P], identb[0:HC, 0:HC])
            last.then_inc(sem("q_wturned"), 1)
            for c in range(2):
                last = nc.tensor.matmul(p0[:, 3, c * HC:(c + 1) * HC], sw2b[:, c, :], ident[0:HC, 0:HC],
                                        start=True, stop=True)
            last.then_inc(sem("q_sw2row"), 1)
            pe.wait_ge(sem("q_xq"), 1)
            pe.wait_ge(sem("q_wT"), 1)
            pe.wait_ge(sem("q_sw2"), 1)
            for g in range(NG):
                for m in range(HT):
                    k = g * HT + m
                    if k >= 8:
                        pe.wait_ge(sem("q_gelu"), k - 7)
                    o = ps[k % 8 // 4][:, k % 4, :]
                    for c in range(2):
                        last = nc.tensor.matmul(o, wq1T[:, c, m * P:(m + 1) * P], xq[:, c, g * TG:(g + 1) * TG],
                                                start=(c == 0), stop=(c == 1))
                    last.then_inc(sem("q_up"), 1)
            pe.wait_ge(sem("q_hmax"), 1)
            nc.tensor.transpose(p0[0:1, 0, 0:P], small[:, 30:31], ident[:, :]).then_inc(sem("q_hmaxturned"), 1)
            pe.wait_ge(sem("q_hmaxone"), 1)
            nc.tensor.matmul(p0[:, 1, 0:1], ones[0:1, :], small[0:1, 31:32], start=True,
                             stop=True).then_inc(sem("q_hmaxspread"), 1)
            pe.wait_ge(sem("q_hscale"), 1)
            for t in range(B):
                if t % 4 == 0:
                    pe.wait_ge(sem("q_hq"), t // 4 + 1)
                if t >= 8:
                    pe.wait_ge(sem("q_down_read"), t - 7)
                o = ps[t % 8 // 4][:, t % 4, 0:C]
                for m in range(HT):
                    last = nc.tensor.matmul(o, hqs[t // 4][:, m, (t % 4) * P:(t % 4 + 1) * P], wq2T[:, m, :],
                                            start=(m == 0), stop=(m == HT - 1))
                last.then_inc(sem("q_down"), 1)
            pe.wait_ge(sem("q_orange"), 1)
            nc.tensor.transpose(p0[0:2, 1, 0:P], small[:, 40:42], ident[:, :]).then_inc(sem("q_orangeturned"), 1)
            pe.wait_ge(sem("q_orangediag"), 1)
            nc.tensor.matmul(p0[:, 2, 0:2], ones[0:2, :], small[0:2, 76:78], start=True,
                             stop=True).then_inc(sem("q_orangespread"), 1)

        @block.scalar
        def _(act):
            loaded(act)

            def tok_kT(s, n):
                act.wait_ge(*after("tok_turned", n))
                nc.scalar.activation(bufs[s].kT.rearrange("p g t n -> p (g t n)"),
                                     ps[s][:, 0:3, :].rearrange("p b n -> p (b n)"),
                                     ACT.Copy).then_inc(sem("tok_kT"), 1)
            with act.Fori(0, B - STREAMS + 1, STREAMS) as i:
                both(tok_kT, i + 1)
                for half in range(2):
                    both(lambda s, n: act_exp(act, f"tok{half}", s, n), i + 1)
                    both(lambda s, n: act_probs(act, f"tok{half}", s, n), i + 1)
                both(lambda s, n: act_turned(act, "tok_oturned", "tok_onT", s, n, bufs[s].onT, 0), i + 1)

            for pre in ("at", "ff"):
                with act.Fori(0, B - STREAMS + 1, STREAMS) as i:
                    gain, bias = (const("ln1_g"), const("ln1_b")) if pre == "ff" else (None, None)
                    both(lambda s, n: act_turned(act, f"{pre}_xturned", f"{pre}_xT", s, n,
                                                 bufs[s].xT[:, :, 0:P], 0, gain, bias), i + 1)
                    both(lambda s, n: at_act_qk(act, pre, s, n), i + 1)
                    both(lambda s, n: act_exp(act, pre, s, n), i + 1)
                    both(lambda s, n: act_probs(act, pre, s, n), i + 1)
                    both(lambda s, n: act_turned(act, f"{pre}_oturned", f"{pre}_onT", s, n, bufs[s].onT, 0), i + 1)
            with act.Fori(0, B - STREAMS + 1, STREAMS) as i:
                both(lambda s, n: act_turned(act, "ff2_xturned", "ff2_xT", s, n, bufs[s].xT[:, :, 0:P], 0,
                                             const("ln2_g"), const("ln2_b")), i + 1)

                def keep(s, n):
                    act.wait_ge(*after("ff2_xT", n))
                    for c in range(2):
                        last = nc.scalar.activation(featT[:, c, bass.ds((i + s) * P, P)],
                                                    bufs[s].xT[:, c, 0:P], ACT.Copy)
                    last.then_inc(sem("ff_featT"), 1)
                both(keep, i + 1)
                act.wait_ge(sem("ff_featT"), i + STREAMS)

            act.wait_ge(sem("moe_gap"), 1)
            nc.scalar.activation(gw[:, :, 1:2], gw[:, :, 3:4], ACT.Exp).then_inc(sem("moe_gapexp"), 1)
            with act.Fori(0, B - STREAMS + 1, STREAMS) as i:
                def cwT(s, n):
                    act.wait_ge(*after("moe_cwturned", n))
                    nc.scalar.activation(bufs[s].onT[0:EXPERTS, 0, :], ps[s][0:EXPERTS, 0, 0:P],
                                         ACT.Copy).then_inc(sem("moe_cwT"), 1)
                both(cwT, i + 1)
            act.wait_ge(sem("moe_start"), 1)
            with act.Fori(0, EXPERTS - 1, 2) as e:
                for k in range(2):
                    nc.scalar.activation(b1cur[:, k, :], const("b1")[:, bass.ds(e * HT + k * HT, HT)],
                                         ACT.Copy).then_inc(sem("moe_b1"), 1)
                    act.wait_ge(sem("moe_b1"), e + k + 1)
                    for g in range(NG):
                        act.wait_ge(sem("moe_out"), e * B + k * B + g * 4 + 4)
                        for m in range(HT):
                            act.wait_ge(sem("moe_hidden"), e * (NG * HT) + k * NG * HT + g * HT + m + 1)
                            nc.scalar.activation(he[g % 2][:, m, :], ps[0][:, (g * HT + m) % 4, :], ACT.Gelu,
                                                 bias=b1cur[:, k, m:m + 1]).then_inc(
                                                     sem("moe_gelu"), 1)

            with act.Fori(0, B - STREAMS + 1, STREAMS) as i:
                both(lambda s, n: act_turned(act, "l1_xturned", "l1_xT", s, n, bufs[s].xT[:, :, 0:P], 0), i + 1)

                def qT(s, n):
                    act.wait_ge(*after("l1_qturned", n))
                    nc.scalar.activation(bufs[s].qT, ps[s][:, 3, 0:GROUPS * P].rearrange(
                        "p (g n) -> p g n", g=GROUPS), ACT.Copy).then_inc(sem("l1_qT"), 1)
                both(qT, i + 1)

                def kernel_exp(s, n):
                    act.wait_ge(*after("l1_gram", n))
                    nc.scalar.activation(bufs[s].hi.rearrange("p (j n) -> p j n", j=4),
                                         ps[s][:, :, 0:GROUPS * P], ACT.Exp,
                                         scale=1.0 / OT_REG, bias=neg_reg[:, 0:1])
                    nc.scalar.activation(bufs[s].p.rearrange("p (j n) -> p j n", j=4),
                                         ps[s][:, :, 0:GROUPS * P], ACT.Exp,
                                         scale=1.0 / OT_REG, bias=neg_reg[:, 0:1]).then_inc(sem("l1_kernel"), 1)
                both(kernel_exp, i + 1)

                def uT(s, n):
                    act.wait_ge(*after("l1_uturned", n))
                    nc.scalar.activation(bufs[s].uT_parts, ps[s][0:3 * HEADS, 3, 0:P // 2].bitcast(BF16),
                                         ACT.Copy).then_inc(sem("l1_uT"), 1)
                both(uT, i + 1)

                def probs(s, n):
                    act.wait_ge(*after("l1_z", n))
                    nc.scalar.activation(bufs[s].hi, bufs[s].pT, ACT.Exp).then_inc(sem("l1_probs_hi"), 1)
                    act.wait_ge(*after("l1_probs_hi", n))
                    nc.scalar.activation(bufs[s].pT, bufs[s].pT, ACT.Exp).then_inc(sem("l1_probs"), 1)
                both(probs, i + 1)
                both(lambda s, n: act_turned(act, "l1_oturned", "l1_onT", s, n, bufs[s].onT, 0), i + 1)

            with act.Fori(0, B - STREAMS + 1, STREAMS) as i:
                def keep(s, n):
                    act.wait_ge(*after("q_xturned", n))
                    for c in range(2):
                        last = nc.scalar.activation(featT[:, c, bass.ds((i + s) * P, P)],
                                                    ps[s][0:HC, 0, c * P:(c + 1) * P], ACT.Copy)
                    last.then_inc(sem("q_featT"), 1)
                both(keep, i + 1)

            act.wait_ge(sem("q_hidden_scale"), 1)
            for g in range(NG):
                for m in range(HT):
                    k = g * HT + m
                    act.wait_ge(sem("q_up"), k + 1)
                    nc.scalar.activation(gelu_out[:, m, g * TG:(g + 1) * TG], ps[k % 8 // 4][:, k % 4, :],
                                         ACT.Gelu, bias=const("q_b1")[:, m:m + 1],
                                         scale=small[:, 48 + m:49 + m]).then_inc(sem("q_gelu"), 1)

        @block.vector
        def _(dve):
            for s in range(STREAMS):
                nc.vector.memset(bufs[s].qk_pad, 0.0).then_inc(sem("pads_ready"), 1)
                nc.vector.memset(bufs[s].v_ext, 1.0).then_inc(sem("pads_ready"), 1)
            nc.vector.memset(neg_reg[:, :], -1.0 / OT_REG).then_inc(sem("pads_ready"), 1)
            loaded(dve)

            chain = [0]

            def link(ins):
                chain[0] += 1
                ins.then_inc(sem("dve_chain"), 1)
                dve.wait_ge(sem("dve_chain"), chain[0])

            def row(i, s, src=None):
                return (hs if src is None else src)[:, bass.ds(i + s, 1), :].rearrange("p o c -> p (o c)")

            def residual(pre, s, n, h, bias):
                dve.wait_ge(*after(f"{pre}_proj", n))
                nc.vector.tensor_tensor(bufs[s].t1, ps[s][:, 1, 0:C], bias, ALU.add).then_inc(sem(f"{pre}_biased"), 1)
                dve.wait_ge(*after(f"{pre}_biased", n))
                nc.vector.tensor_tensor(bufs[s].t1, h, bufs[s].t1, ALU.add).then_inc(sem(f"{pre}_h"), 1)

            tok_b = const("tok_b")

            def tok_pool(s, n):
                dve.wait_ge(*after("tok_q", n))
                q4 = ps[s][:, 0:2, :].rearrange("p b n -> p (b n)").rearrange("p (t n) -> p n t", t=STRIDE)
                nc.vector.tensor_reduce(bufs[s].xn, q4[:, 0:C, :], X, ALU.max).then_inc(sem("tok_pooled"), 1)

            def tok_qk_pad(s, n):
                b = bufs[s]
                dve.wait_ge(*after("tok_pooled", n))
                nc.vector.tensor_tensor(b.qk_pad[:, 0:HEADS, 0:HD], b.xn.rearrange("p (h d) -> p h d", d=HD),
                                        tok_b[:, 0:C].rearrange("p (h d) -> p h d", d=HD), ALU.add)
                dve.wait_ge(*after("tok_k", n))
                k4 = ps[s][:, 2:4, :].rearrange("p b n -> p (b n)").rearrange("p (t n) -> p t n", t=STRIDE)
                for t in range(STRIDE):
                    last = nc.vector.tensor_tensor(
                        b.qk_pad[:, (1 + t) * HEADS:(2 + t) * HEADS, 0:HD],
                        k4[:, t, 0:C].rearrange("p (h d) -> p h d", d=HD),
                        tok_b[:, C:2 * C].rearrange("p (h d) -> p h d", d=HD), ALU.add)

            def tok_v_pad(s, n):
                b = bufs[s]
                dve.wait_ge(*after("tok_v", n))
                v4 = ps[s][:, 0:2, :].rearrange("p b n -> p (b n)").rearrange("p (t n) -> p t n", t=4)
                for t in range(4):
                    last = nc.vector.tensor_tensor(
                        b.v_ext[:, t * HEADS:(t + 1) * HEADS, 0:HD],
                        v4[:, t, 0:C].rearrange("p (h d) -> p h d", d=HD),
                        tok_b[:, 2 * C:3 * C].rearrange("p (h d) -> p h d", d=HD), ALU.add)
                last.then_inc(sem("tok_vpad"), 1)

            def tok_qT(s, n):
                dve.wait_ge(*after("tok_turned", n))
                nc.vector.tensor_copy(bufs[s].qT, ps[s][:, 3, 0:GROUPS * P].rearrange(
                    "p (g n) -> p g n", g=GROUPS)).then_inc(sem("tok_qT"), 1)

            with dve.Fori(0, B - STREAMS + 1, STREAMS) as i:
                both(tok_pool, i + 1)
                both(tok_qk_pad, i + 1)
                both(tok_v_pad, i + 1)

                both(tok_qT, i + 1)
                for half in range(2):
                    both(lambda s, n: dve_softmax_shift(dve, f"tok{half}_scores", f"tok{half}", s, n, ps[s][:, :, :].rearrange(
                        "p (a b) n -> p a (b n)", a=2)[:, :, 0:768].rearrange("p a (g k) -> p a g k", g=GROUPS),
                        2, GROUPS, 256), i + 1)
                    both(lambda s, n: dve_probs(dve, f"tok{half}", s, n), i + 1)
                both(lambda s, n: dve_softmax_norm(dve, "tok", s, n, TOK_PV), i + 1)

                def tok_out(s, n):
                    dve.wait_ge(*after("tok_proj", n))
                    nc.vector.tensor_tensor(bufs[s].t1, ps[s][:, 1, 0:C], const("tok_pb"), ALU.add).then_inc(sem("tok_h"), 1)
                    dve.wait_ge(*after("tok_h", n))
                    dve_stats(dve, "n0", s, n, i, row(i, s))
                both(tok_out, i + 1)

            def rstd_all(part):
                dve.wait_ge(*after(f"{part}_mv", B))
                for t in range(B):
                    ins = nc.vector.bn_aggr(meanvar[:, t, :], allstats[:, t, :])
                link(ins)
                link(nc.vector.tensor_scalar(varp[:, :], meanvar[:, :, 1], LN_EPS, None, ALU.add))
                for ins in rsqrt_steps(rstd[:, :], varp[:, :], newton[:, :]):
                    link(ins)

            rstd_all("n0")
            with dve.Fori(0, B - STREAMS + 1, STREAMS) as i:
                both(lambda s, n: dve_normalize(dve, "at", s, n, i, row(i, s), bufs[s].xn), i + 1)
                both(lambda s, n: at_dve_qkv(dve, "at", s, n, const("at_b")), i + 1)
                both(lambda s, n: dve_softmax_shift(dve, "at_scores", "at", s, n, score_view(s), 4, GROUPS, P), i + 1)
                both(lambda s, n: dve_probs(dve, "at", s, n), i + 1)
                both(lambda s, n: dve_softmax_norm(dve, "at", s, n), i + 1)

                def at_out(s, n):
                    residual("at", s, n, row(i, s), const("at_pb"))
                    dve.wait_ge(*after("at_h", n))
                    dve_stats(dve, "n1", s, n, i, row(i, s))
                both(at_out, i + 1)

            rstd_all("n1")
            with dve.Fori(0, B - STREAMS + 1, STREAMS) as i:
                def own_residual(s, n):
                    nc.vector.tensor_scalar(bufs[s].t1, row(i, s),
                                            meanvar[:, bass.ds(i + s, 1), 0:1].rearrange("p o c -> p (o c)"),
                                            rstd[:, bass.ds(i + s, 1)], ALU.subtract, ALU.mult).then_inc(
                                                sem("ff_x3"), 1)
                    dve.wait_ge(*after("ff_x3", n))
                    dve_stats(dve, "n2", s, n, i, row(i, s, x3))
                both(own_residual, i + 1)
            rstd_all("n2")
            with dve.Fori(0, B - STREAMS + 1, STREAMS) as i:
                both(lambda s, n: dve_normalize(dve, "ff", s, n, i, row(i, s, x3), bufs[s].xn), i + 1)
                both(lambda s, n: at_dve_qkv(dve, "ff", s, n, None), i + 1)
                both(lambda s, n: dve_softmax_shift(dve, "ff_scores", "ff", s, n, score_view(s), 4, GROUPS, P), i + 1)
                both(lambda s, n: dve_probs(dve, "ff", s, n), i + 1)
                both(lambda s, n: dve_softmax_norm(dve, "ff", s, n), i + 1)

                def ff_out(s, n):
                    residual("ff", s, n, row(i, s, x3), const("ff_pb"))
                    dve.wait_ge(*after("ff_h", n))
                    dve_stats(dve, "n3", s, n, i, row(i, s, x3))
                    nc.vector.tensor_tensor(row(i, s), row(i, s), bufs[s].t1, ALU.add).then_inc(sem("ff_sum"), 1)
                both(ff_out, i + 1)
            rstd_all("n3")
            with dve.Fori(0, B - STREAMS + 1, STREAMS) as i:
                both(lambda s, n: dve_normalize(dve, "ff2", s, n, i, row(i, s, x3), bufs[s].xn), i + 1)

                def take_logits(s, n):
                    dve.wait_ge(*after("ff_logits", n))
                    nc.vector.tensor_tensor(logits[:, bass.ds(i + s, 1), :].rearrange("p o c -> p (o c)"),
                                            ps[s][:, 1, 0:EXPERTS], const("gate_b"), ALU.add).then_inc(
                                                sem("ff_logits_kept"), 1)
                both(take_logits, i + 1)

            dve.wait_ge(sem("ff_logits_kept"), B)
            dve.wait_ge(sem("ff_sum"), B)
            for t in range(B):
                ins = nc.vector.max(top8[:, t, :], logits[:, t, :])
            link(ins)
            for t in range(B):
                ins = nc.vector.max_index(idx8[:, t, :], top8[:, t, :], logits[:, t, :])
            link(ins)
            link(nc.vector.tensor_copy(gidx[:, :, :], idx8[:, :, 0:2]))
            link(nc.vector.tensor_tensor(gw[:, :, 0:1], top8[:, :, 1:2], top8[:, :, 0:1], ALU.subtract))
            nc.vector.tensor_copy(gw[:, :, 3:4], gw[:, :, 0:1]).then_inc(sem("moe_gap"), 1)
            dve.wait_ge(sem("moe_gapexp"), 1)
            link(nc.vector.tensor_scalar(gw[:, :, 2:3], gw[:, :, 1:2], 1.0, None, ALU.add))
            link(nc.vector.reciprocal(gw[:, :, 2:3], gw[:, :, 2:3]))
            link(nc.vector.tensor_tensor(gw[:, :, 1:2], gw[:, :, 1:2], gw[:, :, 2:3], ALU.mult))
            ia = iota8[:, :].unsqueeze(1).to_broadcast([P, B, EXPERTS])
            link(nc.vector.tensor_tensor(cw[:, :, :], ia, gidx[:, :, 0:1].to_broadcast([P, B, EXPERTS]), ALU.is_equal))
            link(nc.vector.tensor_tensor(logits[:, :, :], ia, gidx[:, :, 1:2].to_broadcast([P, B, EXPERTS]),
                                         ALU.is_equal))
            link(nc.vector.tensor_tensor(cw[:, :, :], cw[:, :, :], gw[:, :, 2:3].to_broadcast([P, B, EXPERTS]),
                                         ALU.mult))
            link(nc.vector.tensor_tensor(logits[:, :, :], logits[:, :, :],
                                         gw[:, :, 1:2].to_broadcast([P, B, EXPERTS]), ALU.mult))
            nc.vector.tensor_tensor(cw[:, :, :], cw[:, :, :], logits[:, :, :], ALU.add).then_inc(sem("moe_cw"), 1)
            dve.wait_ge(sem("moe_cw"), 1)

            with dve.Fori(0, B - STREAMS + 1, STREAMS) as i:
                def cw_copy(s, n):
                    nc.vector.tensor_copy(bufs[s].xn[:, 0:EXPERTS],
                                          cw[:, bass.ds(i + s, 1), :].rearrange("p o c -> p (o c)")).then_inc(
                                              sem("moe_cw_copy"), 1)
                both(cw_copy, i + 1)

                def add_bias2(s, n):
                    dve.wait_ge(*after("moe_bias2", n))
                    nc.vector.tensor_tensor(row(i, s), row(i, s), ps[s][:, 1, 0:C], ALU.add).then_inc(
                        sem("moe_b2_added"), 1)
                both(add_bias2, i + 1)
            dve.wait_ge(sem("moe_b2_added"), B)
            nc.vector.memset(small[:, 0:1], 0.0).then_inc(sem("moe_gelu"), 4)
            nc.vector.memset(small[:, 1:2], 0.0).then_inc(sem("moe_added"), 4)
            nc.vector.memset(small[:, 2:3], 0.0).then_inc(sem("moe_out"), 8)
            nc.vector.memset(small[:, 3:4], 0.0).then_inc(sem("moe_start"), 1)

            with dve.Fori(0, EXPERTS - 1, 2) as e:
                for k in range(2):
                    nc.vector.tensor_copy(cwcur[:, k, :].unsqueeze(2), cw[:, :, bass.ds(e + k, 1)]).then_inc(
                        sem("moe_cwcur"), 1)
                    dve.wait_ge(sem("moe_cwcur"), e + k + 1)
                    for t in range(B):
                        dve.wait_ge(sem("moe_out"), e * B + k * B + t + 1 + 8)
                        nc.vector.scalar_tensor_tensor(
                            out=hs[:, t, :], in0=ps[1][:, t % 4, 0:C], scalar=cwcur[:, k, t:t + 1],
                            in1=hs[:, t, :], op0=ALU.mult, op1=ALU.add).then_inc(sem("moe_added"), 1)
            dve.wait_ge(sem("moe_added"), EXPERTS * B + 4)
            nc.vector.memset(bufs[0].qk_pad, 0.0)
            nc.vector.memset(bufs[0].v_ext[:, 0:HEADS, :], 1.0)
            for t in range(B):
                nc.vector.bn_stats(allstats[:, t, :], hs[:, t, :]).then_inc(sem("n4_mv"), 1)
            rstd_all("n4")

            with dve.Fori(0, B - STREAMS + 1, STREAMS) as i:
                both(lambda s, n: dve_normalize(dve, "l1", s, n, i, row(i, s), bufs[s].xn), i + 1)

                def unit_q(s, n):
                    b = bufs[s]
                    dve.wait_ge(*after("l1_qv", n))
                    on3 = b.on.rearrange("p (h d) -> p h d", d=HD)
                    nc.vector.tensor_copy(b.v_ext[:, 0:HEADS, 0:HD],
                                          ps[s][:, 1, 0:C].rearrange("p (h d) -> p h d", d=HD))
                    nc.vector.tensor_copy(b.on, ps[s][:, 0, 0:C]).then_inc(sem("l1_q"), 1)
                    dve.wait_ge(*after("l1_q", n))
                    nc.vector.tensor_tensor(b.t1, b.on, b.on, ALU.mult).then_inc(sem("l1_squares"), 1)
                    dve.wait_ge(*after("l1_squares", n))
                    nc.vector.tensor_reduce(b.n2, b.t1.rearrange("p (h d) -> p h d", d=HD), X,
                                            ALU.add).then_inc(sem("l1_norm2"), 1)
                    dve.wait_ge(*after("l1_norm2", n))
                    for k, ins in enumerate(rsqrt_steps(b.sv, b.n2, b.nt)):
                        ins.then_inc(sem("l1_newton"), 1)
                        dve.wait_ge(sem("l1_newton"), i * 10 + (10 * s + k + 1))
                    nc.vector.tensor_tensor(b.sv, b.sv, b.n2, ALU.mult).then_inc(sem("l1_root"), 1)
                    dve.wait_ge(*after("l1_root", n))
                    nc.vector.tensor_scalar(b.sv, b.sv, Q_EPS, None, ALU.add).then_inc(sem("l1_norm"), 1)
                    dve.wait_ge(*after("l1_norm", n))
                    nc.vector.reciprocal(b.sv, b.sv).then_inc(sem("l1_rnorm"), 1)
                    nc.vector.memset(b.x_parts[:, :, 0:1], 1.0)
                    nc.vector.memset(b.x_parts[:, :, 1:2], 0.0)
                    nc.vector.tensor_copy(b.v_hi, b.v_ext[:, 0:HEADS, :]).then_inc(sem("l1_vhi"), 1)
                    dve.wait_ge(*after("l1_vhi", n))
                    nc.vector.tensor_tensor(b.v_lo, b.v_ext[:, 0:HEADS, :], b.v_hi, ALU.subtract)
                    dve.wait_ge(*after("l1_rnorm", n))
                    nc.vector.tensor_tensor(b.qk_pad[:, 0:HEADS, 0:HD], on3,
                                            b.sv.unsqueeze(2).to_broadcast([P, HEADS, HD]),
                                            ALU.mult).then_inc(sem("l1_pad"), 1)
                both(unit_q, i + 1)

                def kernel_lo(s, n):
                    b = bufs[s]
                    dve.wait_ge(*after("l1_kernel", n))
                    nc.vector.tensor_tensor(b.lo, b.p, b.hi, ALU.subtract).then_inc(sem("l1_kernel_lo"), 1)
                both(kernel_lo, i + 1)

                def rescale(s, n, i, it):
                    b = bufs[s]
                    x = b.rec if it % 2 == 0 else b.mx
                    step = half_steps(i, s, it)
                    dve.wait_ge(sem("l1_sums"), step)
                    nc.vector.tensor_reduce(b.n2, ps[s][:, 3, SUMS:SUMS + 2 * HEADS].rearrange(
                        "p (h k) -> p h k", k=2), X, ALU.add).then_inc(sem("l1_summed"), 1)
                    dve.wait_ge(sem("l1_summed"), step)
                    nc.vector.reciprocal(x, b.n2).then_inc(sem("l1_scaled"), 1)
                    dve.wait_ge(sem("l1_scaled"), step)
                    if it == 2 * SINKHORN_ITERS - 1:
                        return
                    nc.vector.tensor_copy(b.x_parts[:, :, 0], x).then_inc(sem("l1_xhi"), 1)
                    dve.wait_ge(sem("l1_xhi"), halfs(i, s, it))
                    nc.vector.tensor_tensor(b.x_parts[:, :, 1], x, b.x_parts[:, :, 0],
                                            ALU.subtract).then_inc(sem("l1_xlo"), 1)
                for it in range(2 * SINKHORN_ITERS):
                    both(rescale, i + 1, i, it)

                def split_u(s, n):
                    b = bufs[s]
                    nc.vector.tensor_copy(b.u_parts[:, 0:HEADS], b.rec).then_inc(sem("l1_u0"), 1)
                    dve.wait_ge(*after("l1_u0", n))
                    nc.vector.tensor_tensor(b.nt, b.rec, b.u_parts[:, 0:HEADS], ALU.subtract).then_inc(
                        sem("l1_ur"), 1)
                    dve.wait_ge(*after("l1_ur", n))
                    nc.vector.tensor_copy(b.u_parts[:, HEADS:2 * HEADS], b.nt).then_inc(sem("l1_u1"), 1)
                    dve.wait_ge(*after("l1_u1", n))
                    nc.vector.tensor_tensor(b.u_parts[:, 2 * HEADS:3 * HEADS], b.nt, b.u_parts[:, HEADS:2 * HEADS],
                                            ALU.subtract).then_inc(sem("l1_uparts"), 1)
                both(split_u, i + 1)

                def transport(s, n):
                    b = bufs[s]
                    dve.wait_ge(*after("l1_urows", n))
                    nc.vector.tensor_tensor(b.pT, b.p, ps[s][:, 0:3, :].rearrange("p b n -> p (b n)"),
                                            ALU.mult).then_inc(sem("l1_ku"), 1)
                    dve.wait_ge(*after("l1_ku", n))
                    nc.vector.tensor_reduce(b.stats12, b.pT.rearrange("p (h n) -> p h n", h=HEADS), X,
                                            ALU.max).then_inc(sem("l1_kumax"), 1)
                    dve.wait_ge(*after("l1_kumax", n))
                    nc.vector.tensor_tensor(b.stats12, b.stats12, b.mx, ALU.mult).then_inc(sem("l1_rowmax"), 1)
                both(transport, i + 1)

                def head_max(s, n):
                    b = bufs[s]
                    dve.wait_ge(*after("l1_maxturned", n))
                    nc.vector.tensor_reduce(b.stats[0:HEADS, 0:1], ps[s][0:HEADS, 3, 0:P], X,
                                            ALU.max).then_inc(sem("l1_headmax"), 1)
                    dve.wait_ge(*after("l1_headmax", n))
                    nc.vector.reciprocal(b.stats[0:HEADS, 1:2], b.stats[0:HEADS, 0:1]).then_inc(
                        sem("l1_headrec"), 1)
                    dve.wait_ge(*after("l1_headrec", n))
                    nc.vector.tensor_scalar(b.maxdiag, ident[0:HEADS, 0:HEADS], b.stats[0:HEADS, 1:2], SCALE,
                                            ALU.mult, ALU.mult).then_inc(sem("l1_maxdiag"), 1)
                both(head_max, i + 1)

                def scaled_z(s, n):
                    b = bufs[s]
                    dve.wait_ge(*after("l1_maxspread", n))
                    nc.vector.tensor_tensor(b.sv, b.mx, ps[s][:, 3, P:P + HEADS], ALU.mult).then_inc(
                        sem("l1_sv"), 1)
                    dve.wait_ge(*after("l1_sv", n))
                    pT3 = b.pT.rearrange("p (h n) -> p h n", h=HEADS)
                    nc.vector.tensor_tensor(pT3, pT3, b.sv.unsqueeze(2).to_broadcast([P, HEADS, P]),
                                            ALU.mult).then_inc(sem("l1_z"), 1)
                both(scaled_z, i + 1)

                def probs_lo(s, n):
                    b = bufs[s]
                    dve.wait_ge(*after("l1_probs", n))
                    nc.vector.tensor_tensor(b.lo, b.pT, b.hi, ALU.subtract).then_inc(sem("l1_probs_lo"), 1)
                both(probs_lo, i + 1)
                both(lambda s, n: dve_softmax_norm(dve, "l1", s, n), i + 1)

                def l1_out(s, n):
                    residual("l1", s, n, row(i, s), const("l1_pb"))
                    dve.wait_ge(*after("l1_h", n))
                    dve_stats(dve, "n5", s, n, i, row(i, s))
                both(l1_out, i + 1)
            rstd_all("n5")
            with dve.Fori(0, B - STREAMS + 1, STREAMS) as i:
                both(lambda s, n: dve_normalize(dve, "q", s, n, i, row(i, s), bufs[s].xn), i + 1)
                dve.wait_ge(sem("q_featT"), i + STREAMS)

            dve.wait_ge(sem("q_featT"), B)
            A96 = slice(0, HC)
            hi2, lo2, abs2 = small[A96, 0:2], small[A96, 2:4], small[A96, 4:6]
            wm2, cs2, pw2, up2 = small[A96, 6:8], small[A96, 8:10], small[A96, 10:12], small[A96, 12:14]
            rc2 = small[A96, 16:18]
            w1n = const("q_w1").rearrange("p (m n) -> p m n", m=HT)
            w2n = const("q_w2").rearrange("p (c n) -> p c n", c=2)

            def absmax(dst, src):
                return nc.vector.tensor_reduce(dst, src, X, ALU.max, apply_absolute_value=True)

            nc.vector.tensor_reduce(wmax, w1n.rearrange("p m n -> p n m"), X, ALU.max,
                                    apply_absolute_value=True).then_inc(sem("q_wmax"), 1)
            nc.vector.tensor_reduce(hi2, featT[:, :, :], X, ALU.max)
            link(nc.vector.tensor_reduce(lo2, featT[:, :, :], X, ALU.min))
            link(nc.vector.tensor_scalar(lo2, lo2, -1.0, None, ALU.mult))
            link(nc.vector.tensor_tensor(abs2, hi2, lo2, ALU.max))
            dve.wait_ge(sem("q_wmaxturned"), 1)
            link(nc.vector.tensor_reduce(wm2, ps[0][A96, 3, 0:2 * P].rearrange("p (c n) -> p c n", c=2), X, ALU.max))
            link(nc.vector.reciprocal(wm2, wm2))
            link(nc.vector.tensor_tensor(wm2, abs2, wm2, ALU.mult))
            for ins in rsqrt_steps(abs2, wm2, pw2):
                link(ins)
            link(nc.vector.tensor_tensor(abs2, abs2, wm2, ALU.mult))
            link(nc.vector.tensor_scalar(pw2.bitcast(I32), abs2.bitcast(I32), 0x7F800000, None, ALU.bitwise_and))
            link(nc.vector.tensor_scalar(up2, pw2, 1.5, None, ALU.mult))
            link(nc.vector.tensor_tensor(up2, abs2, up2, ALU.is_gt))
            link(nc.vector.tensor_scalar(up2, up2, 1.0, None, ALU.add))
            link(nc.vector.tensor_tensor(cs2, pw2, up2, ALU.mult))
            for c in range(2):
                last = nc.vector.tensor_scalar(csb[:, c, :], ones[A96, :], cs2[:, c:c + 1], None, ALU.mult)
            last.then_inc(sem("q_cs_rows"), 1)
            link(nc.vector.reciprocal(rc2, cs2))
            nc.vector.tensor_tensor(hi2, hi2, rc2, ALU.mult)
            link(nc.vector.tensor_tensor(lo2, lo2, rc2, ALU.mult))
            nc.vector.tensor_tensor(small[A96, 20:21], hi2[:, 0:1], hi2[:, 1:2], ALU.max)
            nc.vector.tensor_tensor(small[A96, 21:22], lo2[:, 0:1], lo2[:, 1:2], ALU.max).then_inc(
                sem("q_range"), 1)

            def quant_range(pre, rows, at):
                dve.wait_ge(sem(f"{pre}turned"), 1)
                link(nc.vector.tensor_reduce(small[0:2, at:at + 1], ps[0][0:2, 1, 0:rows], X, ALU.max))
                link(nc.vector.tensor_scalar(small[0:2, at:at + 1], small[0:2, at:at + 1], 0.0, None, ALU.max))
                nc.vector.tensor_scalar(small[0:2, at + 1:at + 3], ident[0:2, 0:2], small[0:2, at:at + 1], None,
                                        ALU.mult).then_inc(sem(f"{pre}diag"), 1)
                dve.wait_ge(sem(f"{pre}spread"), 1)
                link(nc.vector.tensor_copy(small[:, at + 8:at + 10], ps[0][:, 2, 0:2]))
                sc, lo, hi, rs = (small[:, at + k:at + k + 1] for k in (4, 5, 6, 10))
                link(nc.vector.tensor_tensor(sc, small[:, at + 8:at + 9], small[:, at + 9:at + 10], ALU.add))
                link(nc.vector.tensor_scalar(sc, sc, 1.0 / 255.0, 1e-8, ALU.mult, ALU.max))
                link(nc.vector.reciprocal(rs, sc))
                link(nc.vector.tensor_scalar(lo, small[:, at + 9:at + 10], rs, ROUND, ALU.mult, ALU.add))
                link(nc.vector.tensor_scalar(lo, lo, ROUND, -1.0, ALU.subtract, ALU.mult))
                link(nc.vector.tensor_scalar(hi, lo, 255.0, None, ALU.add))
                return sc, lo, hi, rs

            sx, xlo, xhi, rsx = quant_range("q_range", HC, 23)
            for c in range(2):
                link(nc.vector.tensor_scalar(featT[:, c, :], featT[:, c, :], rc2[:, c:c + 1], rsx[A96],
                                             ALU.mult, ALU.mult))
                link(nc.vector.tensor_scalar(featT[:, c, :], featT[:, c, :], ROUND, ROUND, ALU.add, ALU.subtract))
                last = nc.vector.tensor_scalar(xq[:, c, :], featT[:, c, :], xlo[A96], xhi[A96], ALU.max, ALU.min)
            last.then_inc(sem("q_xq"), 1)

            s1, s2 = small[:, 54:60], small[A96, 60:62]
            dve.wait_ge(sem("q_csrow"), 1)
            link(nc.vector.tensor_tensor(w1_s, w1n, ps[0][:, 0, 0:C].unsqueeze(1).to_broadcast([P, HT, C]), ALU.mult))
            absmax(s1, w1_s)
            link(absmax(s2, w2n))
            r1, r2 = small[:, 86:92], small[A96, 92:94]
            nc.vector.tensor_scalar(s1, s1, 1.0 / 127.0, 1e-8, ALU.mult, ALU.max)
            link(nc.vector.tensor_scalar(s2, s2, 1.0 / 127.0, 1e-8, ALU.mult, ALU.max))
            nc.vector.reciprocal(r1, s1)
            link(nc.vector.reciprocal(r2, s2))
            nc.vector.tensor_tensor(w1_s, w1_s, r1.unsqueeze(2).to_broadcast([P, HT, C]), ALU.mult)
            link(nc.vector.tensor_tensor(w2n, w2n, r2.unsqueeze(2).to_broadcast([HC, 2, HIDDEN]), ALU.mult))
            nc.vector.tensor_scalar(w1_s, w1_s, ROUND, ROUND, ALU.add, ALU.subtract)
            link(nc.vector.tensor_scalar(w2n, w2n, ROUND, ROUND, ALU.add, ALU.subtract))
            nc.vector.tensor_scalar(w1_q, w1_s, -128.0, 127.0, ALU.max, ALU.min)
            nc.vector.tensor_scalar(w2_q, w2n, -128.0, 127.0, ALU.max, ALU.min)
            for c in range(2):
                last = nc.vector.tensor_scalar(sw2b[:, c, :], ones[A96, :], s2[:, c:c + 1], None, ALU.mult)
            last.then_inc(sem("q_w_quant"), 1)
            nc.vector.tensor_scalar(small[:, 48:54], s1, sx, None, ALU.mult).then_inc(sem("q_hidden_scale"), 1)
            dve.wait_ge(sem("q_wturned"), 1)
            tb = ps[1][:, :, :].rearrange("p b n -> p (b n)").bitcast(BF16).rearrange("p (b n) -> p b n", b=4)
            nc.vector.tensor_copy(wq1T, tb[0:HC, 0:2, 0:HIDDEN])
            nc.vector.tensor_copy(wq2T.rearrange("p (b m) n -> p b (m n)", b=2), tb[:, 2:4, 0:3 * C]).then_inc(
                sem("q_wT"), 1)
            dve.wait_ge(sem("q_sw2row"), 1)
            nc.vector.tensor_copy(sw2row[:, :], ps[0][:, 3, 0:C]).then_inc(sem("q_sw2"), 1)

            for g in range(NG):
                dve.wait_ge(sem("q_gelu"), (g + 1) * HT)
                ins = nc.vector.tensor_reduce(small[:, 64 + g:65 + g], gelu_out[:, :, g * TG:(g + 1) * TG],
                                              mybir.AxisListType.XY, ALU.max, apply_absolute_value=True)
            link(ins)
            nc.vector.tensor_reduce(small[:, 30:31], small[:, 64:64 + NG], X, ALU.max).then_inc(sem("q_hmax"), 1)
            dve.wait_ge(sem("q_hmaxturned"), 1)
            nc.vector.tensor_reduce(small[0:1, 31:32], ps[0][0:1, 0, 0:P], X, ALU.max).then_inc(sem("q_hmaxone"), 1)
            dve.wait_ge(sem("q_hmaxspread"), 1)
            sh = small[:, 70:71]
            rsh = small[:, 71:72]
            link(nc.vector.tensor_scalar(sh, ps[0][:, 1, 0:1], 1.0 / 127.0, 1e-8, ALU.mult, ALU.max))
            link(nc.vector.reciprocal(rsh, sh))
            nc.vector.tensor_scalar(sw2row[:, :], sw2row[:, :], sh, None, ALU.mult).then_inc(sem("q_hscale"), 1)
            for g in range(NG):
                part = gelu_out[:, :, g * TG:(g + 1) * TG]
                link(nc.vector.tensor_scalar(part, part, rsh, ROUND, ALU.mult, ALU.add))
                nc.vector.tensor_scalar(hqs[g], part, ROUND, 127.0, ALU.subtract, ALU.min).then_inc(sem("q_hq"), 1)
            for t in range(B):
                dve.wait_ge(sem("q_down"), t + 1)
                nc.vector.tensor_tensor(oq[:, t, :], ps[t % 8 // 4][:, t % 4, 0:C], sw2row[:, :],
                                        ALU.mult).then_inc(sem("q_down_read"), 1)
            dve.wait_ge(sem("q_down_read"), B)
            link(nc.vector.tensor_tensor(oq, oq, const("q_b2").unsqueeze(1).to_broadcast([P, B, C]), ALU.add))
            nc.vector.tensor_reduce(small[:, 40:41], oq, mybir.AxisListType.XY, ALU.max)
            link(nc.vector.tensor_reduce(small[:, 42:43], oq, mybir.AxisListType.XY, ALU.min))
            nc.vector.tensor_scalar(small[:, 41:42], small[:, 42:43], -1.0, None, ALU.mult).then_inc(
                sem("q_orange"), 1)
            so, olo, ohi, rso = quant_range("q_orange", P, 75)
            link(nc.vector.tensor_scalar(oq, oq, rso, ROUND, ALU.mult, ALU.add))
            link(nc.vector.tensor_scalar(oq, oq, ROUND, olo, ALU.subtract, ALU.max))
            link(nc.vector.tensor_scalar(oq, oq, ohi, so, ALU.min, ALU.mult))
            nc.vector.tensor_tensor(hs[:, :, :], hs[:, :, :], oq, ALU.add).then_inc(sem("result"), 1)


def kernel(**inputs):
    import concourse.bacc as bacc
    from concourse.bass_utils import run_bass_kernel_spmd

    a = {k: np.asarray(v) for k, v in inputs.items()}

    def chunked(w):
        return w.reshape(2, HC, -1).transpose(1, 0, 2).reshape(HC, -1)

    def rows(v):
        return np.broadcast_to(v.reshape(1, -1), (P, v.size))

    parts = {
        "tok_w": chunked(a["L0_tok_w_qkv"].T), "tok_b": rows(a["L0_tok_b_qkv"]),
        "tok_pw": chunked(a["L0_tok_w_proj"].T), "tok_pb": rows(a["L0_tok_b_proj"]),
        "at_w": chunked(a["L0_attn_qkv_w"].T), "at_b": rows(a["L0_attn_qkv_b"]),
        "at_pw": chunked(a["L0_attn_proj_w"].T), "at_pb": rows(a["L0_attn_proj_b"]),
        "ff_w": chunked(a["L0_ffn_qkv_w"]), "ff_pw": chunked(a["L0_ffn_proj_w"]), "ff_pb": rows(a["L0_ffn_proj_b"]),
        "ln1_g": chunked(a["L0_ffn_ln1_g"]), "ln1_b": chunked(a["L0_ffn_ln1_b"]),
        "ln2_g": chunked(a["L0_ffn_ln2_g"]), "ln2_b": chunked(a["L0_ffn_ln2_b"]),
        "gate_w": chunked(a["L0_ffn_gate_w"]), "gate_b": rows(a["L0_ffn_gate_b"]),
        "b1": a["L0_ffn_b1"].reshape(EXPERTS, HT, P).transpose(2, 0, 1).reshape(P, -1), "b2": a["L0_ffn_b2"],
        "l1_w": chunked(a["L1_attn_w_qkv"].T), "l1_pw": chunked(a["L1_attn_w_proj"].T),
        "l1_pb": rows(a["L1_attn_b_proj"]),
        "q_b1": a["L1_ffn_b1"].reshape(HT, P).T, "q_b2": rows(a["L1_ffn_b2"]),
        "q_w1": a["L1_ffn_w1"].reshape(HT, P, C).transpose(1, 0, 2).reshape(P, -1),
        "q_w2": a["L1_ffn_w2"].reshape(2, HC, HIDDEN).transpose(1, 0, 2).reshape(HC, -1),
    }
    packed = np.zeros((P, PACKED), np.float32)
    for name, (at, n, cols) in OFFSET.items():
        packed[0:n, at:at + cols] = parts[name]
    x = a["x"].reshape(B, STRIDE, WQ, WINDOWS, 2, HC).transpose(0, 5, 4, 3, 2, 1).reshape(B, HC, 2, N_IN)
    w1 = a["L0_ffn_w1"].reshape(EXPERTS, 2, HC, HIDDEN).transpose(0, 2, 1, 3)
    w2 = a["L0_ffn_w2"].reshape(EXPERTS, HT, P, C).transpose(0, 2, 1, 3)

    nc = bacc.Bacc("TRN2", target_bir_lowering=False, num_devices=1)
    arrays = {"x_dram": x, "packed_dram": packed, "w1_dram": w1, "w2_dram": w2}
    arrays = {k: np.ascontiguousarray(v) for k, v in arrays.items()}
    args = [nc.dram_tensor(k, v.shape, F32, kind="ExternalInput").ap() for k, v in arrays.items()]
    out = nc.dram_tensor("out_dram", (B, P, C), F32, kind="ExternalOutput").ap()
    build(nc, *args, out)
    r = run_bass_kernel_spmd(nc, [arrays], core_ids=[0])
    return r.results[0]["out_dram"]
```

```python
from contextlib import ExitStack

import numpy as np

import concourse.bass as bass
from concourse import mybir
from concourse.alu_op_type import AluOpType as ALU

ACT = mybir.ActivationFunctionType
F32 = mybir.dt.float32
BF16 = mybir.dt.bfloat16
I32 = mybir.dt.int32
U32 = mybir.dt.uint32
X = mybir.AxisListType.X

P = 128
B = 16
N_IN = 512
C = 192
HEADS = 12
HD = C // HEADS
STRIDE = 4
WINDOWS = 2
WQ = 64
HC = C // 2
GROUPS = 3
EXPERTS = 8
HIDDEN = 768
HT = HIDDEN // P
T = B * P
TG = 512
NG = T // TG
LN_EPS = 1e-5
SCALE = float(HD) ** -0.5
OT_REG = 0.1
SINKHORN_ITERS = 10
DIAG_VAL = 1000.0
Q_EPS = 1e-8
ROUND = 12582912.0
STREAMS = 2

SHARED = {
    **{k: [("n0", "n1", "n2", "n3", "n5")] for k in ("stats", "kept")},
    "mv": [("n0", "n1", "n2", "n3", "n4", "n5")],
    **{k: [("at", "ff", "ff2", "l1", "q")] for k in ("xn", "xturned")},
    "xT": [("at", "ff", "ff2", "l1")],
    **{k: [("at", "ff")] for k in ("qkv", "pad", "qkturned", "qkT")},
    **{k: [("tok1", "at", "ff")] for k in ("scores", "max", "shifted", "pturned")},
    **{k: [("at", "ff")] for k in ("pT_hi", "pT_lo")},
    "vhi": [("at", "ff", "l1")],
    "probs": [("tok1", "at", "ff", "l1")],
    **{k: [("tok", "at", "ff", "l1")] for k in ("pv", "rec", "on", "oturned", "onT", "proj")},
    **{k: [("at", "ff", "l1")] for k in ("biased", "h")},
}

LAYOUT = [
    ("tok_w", HC, 2 * 3 * C), ("tok_b", P, 3 * C), ("tok_pw", HC, 2 * C), ("tok_pb", P, C),
    ("at_w", HC, 2 * 3 * C), ("at_b", P, 3 * C), ("at_pw", HC, 2 * C), ("at_pb", P, C),
    ("ff_w", HC, 2 * 3 * C), ("ff_pw", HC, 2 * C), ("ff_pb", P, C), ("ln1_g", HC, 2), ("ln1_b", HC, 2),
    ("ln2_g", HC, 2), ("ln2_b", HC, 2), ("gate_w", HC, 2 * EXPERTS), ("gate_b", P, EXPERTS),
    ("b1", P, EXPERTS * HT), ("b2", EXPERTS, C),
    ("l1_w", HC, 2 * 3 * C), ("l1_pw", HC, 2 * C), ("l1_pb", P, C),
    ("q_b1", P, HT), ("q_b2", P, C), ("q_w1", P, HT * C), ("q_w2", HC, 2 * HIDDEN),
]
OFFSET = {}
_at = 0
for _name, _rows, _cols in LAYOUT:
    OFFSET[_name] = (_at, _rows, _cols)
    _at += _cols
PACKED = _at


def build(nc, x, packed, w1, w2, out):
    with ExitStack() as ctx:
        def sb(name, shape, dt=F32):
            return ctx.enter_context(nc.sbuf_tensor(name, shape, dt))

        sems = {}

        def shared(name):
            part, _, stage = name.partition("_")
            parts = SHARED.get(stage, ())
            for group in parts:
                if part in group:
                    return stage + "_" * parts.index(group), group.index(part)
            return name, 0

        def after(name, n):
            return sem(name), n + B * shared(name)[1]

        def sem(name):
            name = shared(name)[0]
            if name not in sems:
                sems[name] = ctx.enter_context(nc.semaphore(name))
            return sems[name]

        ps = [ctx.enter_context(nc.psum_tensor(f"ps{s}", [P, 4, 512], F32)) for s in range(STREAMS)]

        consts = sb("consts", [P, PACKED])

        def const(name):
            at, rows, cols = OFFSET[name]
            return consts[0:rows, at:at + cols]

        def chunks(name):
            return const(name).rearrange("p (c n) -> p c n", c=2)

        ident = sb("ident", [P, P])
        identb = sb("identb", [P, P], BF16)
        diag_off = sb("diag_off", [P, GROUPS, P], BF16)
        diag_one = sb("diag_one", [P, P])
        ones = sb("ones", [P, P])
        pick = sb("pick", [3 * HEADS, HEADS, P], BF16)
        iota8 = sb("iota8", [P, EXPERTS])

        hs = sb("hs", [P, B, C])
        featT = sb("featT", [HC, 2, T])
        logits = sb("logits", [P, B, EXPERTS])
        cw = sb("cw", [P, B, EXPERTS])

        ARENA = 9984
        arena = sb("arena", [P, STREAMS, ARENA])

        ffw = sb("ffw", [P, HT * T // 2])
        ew1 = [ffw[0:HC, k * 2 * HIDDEN:(k + 1) * 2 * HIDDEN].rearrange("p (c n) -> p c n", c=2) for k in range(2)]
        ew2 = [ffw[:, 4 * HIDDEN + k * HT * C:4 * HIDDEN + (k + 1) * HT * C].rearrange("p (m n) -> p m n", m=HT)
               for k in range(2)]
        hqs = [ffw[:, g * HT * TG // 2:(g + 1) * HT * TG // 2].bitcast(BF16).rearrange("p (m n) -> p m n", m=HT)
               for g in range(NG)]
        small = sb("small", [P, 96])
        allstats = sb("allstats", [P, B, 6])
        meanvar = sb("meanvar", [P, B, 2])
        rstd = sb("rstd", [P, B])
        newton = sb("newton", [P, B])
        varp = sb("varp", [P, B])
        x3 = sb("x3", [P, B, C])
        b1cur = sb("b1cur", [P, 2, HT])
        cwcur = sb("cwcur", [P, 2, B])
        neg_reg = sb("neg_reg", [P, 1])
        idx8 = sb("idx8", [P, B, 8], U32)
        top8 = sb("top8", [P, B, 8])
        gidx = sb("gidx", [P, B, 2])
        gw = sb("gw", [P, B, 4])
        sw2row = sb("sw2row", [P, C])
        xq = sb("xq", [HC, 2, T], BF16)

        class Buffers:
            pass

        bufs = []
        for s in range(STREAMS):
            b = Buffers()
            used = [0]

            def take(*dims, rows=P):
                n = int(np.prod(dims))
                v = arena[0:rows, s, used[0]:used[0] + n]
                used[0] += n
                if len(dims) == 2:
                    return v.rearrange("p (a b) -> p a b", a=dims[0])
                if len(dims) == 3:
                    return v.rearrange("p (a b c) -> p a b c", a=dims[0], b=dims[1])
                return v

            b.qk_pad = take(5 * HEADS, 32)
            b.v_ext = take(4 * HEADS, HD + 1)
            b.qT = take(GROUPS, P)
            b.kT = take(GROUPS, STRIDE, P)
            parts = b.kT.rearrange("p g t n -> p (g t n)").bitcast(BF16)
            b.hi, b.lo = parts[:, 0:HEADS * P], parts[:, HEADS * P:2 * HEADS * P]
            spare = b.qk_pad.rearrange("p h d -> p (h d)")[:, 2 * HEADS * 32:5 * HEADS * 32].bitcast(BF16)
            b.v_hi = spare[:, 0:204].rearrange("p (h d) -> p h d", h=HEADS)
            b.v_lo = spare[:, 204:408].rearrange("p (h d) -> p h d", h=HEADS)
            b.x_parts = spare[:, 408:408 + 2 * HEADS].rearrange("p (h k) -> p h k", k=2)
            b.u_parts = spare[:, 440:440 + P]
            b.uT_parts = spare[0:3 * HEADS, 600:600 + P]
            b.p = take(HEADS * P)
            b.pT = take(HEADS * P)
            b.pT_hi = b.pT.bitcast(BF16)[:, 0:HEADS * P]
            b.pT_lo = b.pT.bitcast(BF16)[:, HEADS * P:2 * HEADS * P]
            b.xT = take(2, N_IN, rows=HC)
            b.xn = take(C)
            b.t1 = take(C)
            b.on = take(C)
            b.onT = take(2, P, rows=HC)
            b.stats = take(8)
            b.mv = take(4)
            b.mx = take(HEADS)
            b.rec = take(HEADS)
            b.nt = take(HEADS)
            b.n2 = take(HEADS)
            b.stats12 = take(HEADS)
            b.maxdiag = take(HEADS, rows=HEADS)
            b.sv = take(HEADS)
            assert used[0] <= ARENA, used
            bufs.append(b)

        def loaded(eng):
            eng.wait_ge(sem("consts_loaded"), 16)
            eng.wait_ge(sem("masks_ready"), 6)
            eng.wait_ge(sem("pick_ready"), 3)
            eng.wait_ge(sem("pads_ready"), 2 * STREAMS + 1)

        block = ctx.enter_context(nc.Block())


        def dve_stats(dve, part, s, n, keep):
            b = bufs[s]
            nc.vector.bn_stats(b.stats[:, 0:6], b.t1).then_inc(sem(f"{part}_stats"), 1)
            nc.vector.tensor_copy(keep, b.t1).then_inc(sem(f"{part}_kept"), 1)
            dve.wait_ge(*after(f"{part}_stats", n))
            nc.vector.tensor_scalar(allstats[:, bass.ds(n - 1, 1), :].rearrange("p o c -> p (o c)"),
                                    b.stats[:, 0:6], 1.0, None, ALU.mult).then_inc(sem(f"{part}_mv"), 1)

        def rsqrt_steps(y, v, t):
            yield lambda: nc.vector.tensor_scalar(y.bitcast(I32), v.bitcast(I32), -0.5, 1597463007.0,
                                                  ALU.mult, ALU.add)
            for _ in range(3):
                yield lambda: nc.vector.tensor_tensor(t, y, y, ALU.mult)
                yield lambda: nc.vector.scalar_tensor_tensor(out=t, in0=t, scalar=-0.5, in1=v, op0=ALU.mult,
                                                             op1=ALU.mult)
                yield lambda: nc.vector.scalar_tensor_tensor(out=y, in0=t, scalar=1.5, in1=y, op0=ALU.add,
                                                             op1=ALU.mult)

        def dve_normalize(dve, pre, s, n, src, dst):
            nc.vector.tensor_scalar(dst, src, meanvar[:, bass.ds(n - 1, 1), 0:1].rearrange("p o c -> p (o c)"),
                                    rstd[:, bass.ds(n - 1, 1)], ALU.subtract, ALU.mult).then_inc(
                                        sem(f"{pre}_xn"), 1)

        def pe_turn(pe, wait, done, s, n, src, bank):
            pe.wait_ge(*after(wait, n))
            for c in range(2):
                last = nc.tensor.transpose(ps[s][0:HC, bank, c * P:(c + 1) * P],
                                           src[:, c * HC:(c + 1) * HC], ident[:, :])
            last.then_inc(sem(done), 1)

        def act_turned(act, wait, done, s, n, dst, bank, gain=None, bias=None):
            act.wait_ge(*after(wait, n))
            if gain is None:
                nc.scalar.activation(dst, ps[s][0:HC, bank, 0:2 * P].rearrange("p (c n) -> p c n", c=2),
                                     ACT.Copy).then_inc(sem(done), 1)
                return
            for c in range(2):
                last = nc.scalar.activation(dst[:, c, :], ps[s][0:HC, bank, c * P:(c + 1) * P], ACT.Identity,
                                            bias=bias[:, c:c + 1], scale=gain[:, c:c + 1])
            last.then_inc(sem(done), 1)

        def at_pe_qkv(pe, pre, s, n, w):
            pe.wait_ge(*after(f"{pre}_xT", n))
            xT = bufs[s].xT
            for c in range(2):
                nc.tensor.matmul(ps[s][:, 0, 0:2 * C], xT[:, c, 0:P], w[:, c, 0:2 * C],
                                 start=(c == 0), stop=(c == 1))
            for c in range(2):
                last = nc.tensor.matmul(ps[s][:, 1, 0:C], xT[:, c, 0:P], w[:, c, 2 * C:3 * C],
                                        start=(c == 0), stop=(c == 1))
            last.then_inc(sem(f"{pre}_qkv"), 1)

        def dve_split_v(dve, pre, s, n):
            b = bufs[s]
            nc.vector.tensor_copy(b.v_hi, b.v_ext[:, 0:HEADS, :]).then_inc(sem(f"{pre}_vhi"), 1)
            dve.wait_ge(*after(f"{pre}_vhi", n))
            nc.vector.tensor_tensor(b.v_lo, b.v_ext[:, 0:HEADS, :], b.v_hi, ALU.subtract)

        def at_dve_qkv(dve, pre, s, n, bias):
            b = bufs[s]
            dve.wait_ge(*after(f"{pre}_qkv", n))
            qk = ps[s][:, 0, 0:2 * C].rearrange("p (h d) -> p h d", d=HD)
            v = ps[s][:, 1, 0:C].rearrange("p (h d) -> p h d", d=HD)
            if bias is None:
                nc.vector.tensor_copy(b.qk_pad[:, 0:2 * HEADS, 0:HD], qk)
                last = nc.vector.tensor_copy(b.v_ext[:, 0:HEADS, 0:HD], v)
            else:
                bv = bias.rearrange("p (h d) -> p h d", d=HD)
                nc.vector.tensor_tensor(b.qk_pad[:, 0:2 * HEADS, 0:HD], qk, bv[:, 0:2 * HEADS, :], ALU.add)
                last = nc.vector.tensor_tensor(b.v_ext[:, 0:HEADS, 0:HD], v, bv[:, 2 * HEADS:, :], ALU.add)
            last.then_inc(sem(f"{pre}_pad"), 1)
            dve.wait_ge(*after(f"{pre}_pad", n))
            dve_split_v(dve, pre, s, n)

        def at_pe_turn_qk(pe, pre, s, n):
            pe.wait_ge(*after(f"{pre}_pad", n))
            b = bufs[s]
            for g in range(2 * GROUPS):
                last = nc.tensor.transpose(ps[s][:, g // 4, (g % 4) * P:(g % 4 + 1) * P],
                                           b.qk_pad[:, 4 * g:4 * g + 4, :], ident[:, :])
            last.then_inc(sem(f"{pre}_qkturned"), 1)

        def at_act_qk(act, pre, s, n):
            b = bufs[s]
            act.wait_ge(*after(f"{pre}_qkturned", n))
            flat = ps[s][:, 0:2, :].rearrange("p b n -> p (b n)")
            nc.scalar.activation(b.kT[:, :, 0, :], flat[:, GROUPS * P:2 * GROUPS * P].rearrange(
                "p (g n) -> p g n", g=GROUPS), ACT.Copy)
            nc.scalar.activation(b.qT, flat[:, 0:GROUPS * P].rearrange("p (g n) -> p g n", g=GROUPS),
                                 ACT.Copy).then_inc(sem(f"{pre}_qkT"), 1)

        HEAD_ORDER = [g * 4 + j for g in range(GROUPS) for j in range(4)]

        SUMS = 400
        BANK_ORDER = (0, 2, 3, 1)
        TOK_PV = 300

        def place(h):
            return (h % 4) * GROUPS + h // 4

        def score_view(s):
            return ps[s][:, :, 0:GROUPS * P].rearrange("p j (g k) -> p j g k", g=GROUPS)

        def at_pe_scores(pe, pre, s, n):
            b = bufs[s]
            pe.wait_ge(*after(f"{pre}_qkT", n))
            for h in HEAD_ORDER:
                g, r = h // 4, 32 * (h % 4)
                last = nc.tensor.matmul(ps[s][:, h % 4, g * P:(g + 1) * P], b.qT[r:r + HD, g, :],
                                        b.kT[r:r + HD, g, 0, :], start=True, stop=True)
            last.then_inc(sem(f"{pre}_scores"), 1)

        def dve_softmax_shift(dve, wait, pre, s, n, sc, a, g, keys):
            b = bufs[s]
            dve.wait_ge(*after(wait, n))
            for k in range(a):
                last = nc.vector.tensor_reduce(b.mx[:, k * g:(k + 1) * g], sc[:, k], X, ALU.max)
            last.then_inc(sem(f"{pre}_max"), 1)
            dve.wait_ge(*after(f"{pre}_max", n))
            p4 = b.p.rearrange("p (a g k) -> p a g k", a=a, g=g)
            for k in range(a):
                last = nc.vector.tensor_tensor(p4[:, k], sc[:, k],
                                               b.mx[:, k * g:(k + 1) * g].unsqueeze(2).to_broadcast([P, g, keys]),
                                               ALU.subtract)
            last.then_inc(sem(f"{pre}_shifted"), 1)

        def act_exp(act, pre, s, n):
            act.wait_ge(*after(f"{pre}_shifted", n))
            nc.scalar.activation(bufs[s].p, bufs[s].p, ACT.Exp, scale=SCALE).then_inc(sem(f"{pre}_probs"), 1)

        def pe_turn_probs(pe, pre, s, n):
            pe.wait_ge(*after(f"{pre}_probs", n))
            for k in range(HEADS):
                last = nc.tensor.transpose(ps[s][:, k // 4, (k % 4) * P:(k % 4 + 1) * P],
                                           bufs[s].p[:, k * P:(k + 1) * P], ident[:, :])
            last.then_inc(sem(f"{pre}_pturned"), 1)

        def act_probs(act, pre, s, n):
            act.wait_ge(*after(f"{pre}_pturned", n))
            nc.scalar.activation(bufs[s].pT[:, 0:8 * P],
                                 ps[s][:, 0:2, :].rearrange("p b n -> p (b n)"),
                                 ACT.Copy).then_inc(sem(f"{pre}_pT_a"), 1)

        def dve_probs(dve, pre, s, n):
            dve.wait_ge(*after(f"{pre}_pturned", n))
            nc.vector.tensor_copy(bufs[s].pT[:, 8 * P:12 * P], ps[s][:, 2, :]).then_inc(sem(f"{pre}_pT_b"), 1)

        def at_act_probs(act, pre, s, n):
            act.wait_ge(*after(f"{pre}_pturned", n))
            nc.scalar.activation(bufs[s].pT_hi, ps[s][:, 0:3, :].rearrange("p b n -> p (b n)"),
                                 ACT.Copy).then_inc(sem(f"{pre}_pT_hi"), 1)

        def at_dve_probs(dve, pre, s, n):
            dve.wait_ge(*after(f"{pre}_pT_hi", n))
            nc.vector.tensor_tensor(bufs[s].pT_lo, ps[s][:, 0:3, :].rearrange("p b n -> p (b n)"),
                                    bufs[s].pT_hi, ALU.subtract).then_inc(sem(f"{pre}_pT_lo"), 1)

        def at_pe_pv(pe, pre, s, n):
            b = bufs[s]
            pe.wait_ge(*after(f"{pre}_pT_lo", n))
            for h in range(HEADS):
                for part in (b.pT_hi, b.pT_lo):
                    for v in (b.v_hi, b.v_lo):
                        last = nc.tensor.matmul(ps[s][:, 3, h * (HD + 1):(h + 1) * (HD + 1)],
                                                part[:, place(h) * P:(place(h) + 1) * P], v[:, h, :],
                                                start=(part is b.pT_hi and v is b.v_hi),
                                                stop=(part is b.pT_lo and v is b.v_lo))
            last.then_inc(sem(f"{pre}_pv"), 1)

        def dve_softmax_norm(dve, pre, s, n, at=0):
            b = bufs[s]
            dve.wait_ge(*after(f"{pre}_pv", n))
            o = ps[s][:, 3, at:at + HEADS * (HD + 1)].rearrange("p (h d) -> p h d", h=HEADS)
            nc.vector.reciprocal(b.rec[:, :], o[:, :, HD]).then_inc(sem(f"{pre}_rec"), 1)
            dve.wait_ge(*after(f"{pre}_rec", n))
            nc.vector.tensor_tensor(b.on.rearrange("p (h d) -> p h d", h=HEADS), o[:, :, 0:HD],
                                    b.rec.unsqueeze(2).to_broadcast([P, HEADS, HD]),
                                    ALU.mult).then_inc(sem(f"{pre}_on"), 1)

        def pe_project(pe, pre, s, n, w):
            pe.wait_ge(*after(f"{pre}_onT", n))
            for c in range(2):
                last = nc.tensor.matmul(ps[s][:, 1, 0:C], bufs[s].onT[:, c, :], w[:, c, :],
                                        start=(c == 0), stop=(c == 1))
            last.then_inc(sem(f"{pre}_proj"), 1)

        def half_steps(n, it):
            return n * (2 * SINKHORN_ITERS) + (it + 1 - 2 * SINKHORN_ITERS)

        def halfs(n, it):
            return n * (2 * SINKHORN_ITERS - 1) + (it + 2 - 2 * SINKHORN_ITERS)

        def sinkhorn_stages(eng, stage):
            stage(None, None, (0, 1))
            stage(None, (0, 1), (1, 2))
            with eng.Fori(0, B - 3, 2) as i:
                stage((0, i + 1), (1, i + 2), (0, i + 3))
                stage((1, i + 2), (0, i + 3), (1, i + 4))
            stage((0, B - 1), (1, B), None)
            stage((1, B), None, None)

        def both(step, n0, *args):
            for s in range(STREAMS):
                step(s, n0 + s, *args)

        @block.sync
        def _(sp):
            sp.dma_start(consts[:, :], packed[:, :]).then_inc(sem("consts_loaded"), 16)
            for s in range(STREAMS):
                sp.dma_start(bufs[s].xT, x[s]).then_inc(sem(f"tok_x{s}"), 16)
            with sp.Fori(0, B - 2 * STREAMS + 1, STREAMS) as i:
                for s in range(STREAMS):
                    sp.wait_ge(sem("tok_v"), i + s + 1)
                    sp.dma_start(bufs[s].xT, x[bass.ds(i + s + STREAMS, 1), :, :, :].rearrange(
                        "o p c n -> (o p) c n")).then_inc(sem(f"tok_x{s}"), 16)
            for k in range(2):
                sp.dma_start(ew1[k], w1[k]).then_inc(sem(f"moe_w1_{k}"), 16)
                sp.dma_start(ew2[k], w2[k]).then_inc(sem(f"moe_w2_{k}"), 16)
            with sp.Fori(0, EXPERTS - 3, 2) as e:
                for k in range(2):
                    sp.wait_ge(sem("moe_w_lo"), e + k + 1)
                    sp.dma_start(ew1[k], w1[bass.ds(e + k + 2, 1), :, :, :].rearrange(
                        "o p c n -> (o p) c n")).then_inc(sem(f"moe_w1_{k}"), 16)
                    sp.dma_start(ew2[k], w2[bass.ds(e + k + 2, 1), :, :, :].rearrange(
                        "o p c n -> (o p) c n")).then_inc(sem(f"moe_w2_{k}"), 16)
            sp.wait_ge(sem("result"), 1)
            for w in range(WINDOWS):
                sp.dma_start(out.rearrange("b (q w) c -> w q b c", w=WINDOWS)[w],
                             hs[w * WQ:(w + 1) * WQ, :, :]).then_inc(sem("stored"), 16)
            sp.wait_ge(sem("stored"), 16 * WINDOWS)

        flat_arena = arena[:, :, :].rearrange("p s n -> p (s n)")
        gelu_out = flat_arena[:, 0:HT * T].rearrange("p (m n) -> p m n", m=HT)

        def bf(lo, words):
            return flat_arena[:, lo:lo + words].bitcast(BF16)

        he = flat_arena[:, 0:HT * TG].rearrange("p (m n) -> p m n", m=HT)
        he_hi, he_lo = ([bf(HT * TG * (1 + k) + part * HT * TG // 2, HT * TG // 2).rearrange(
            "p (m n) -> p m n", m=HT) for k in range(2)] for part in range(2))
        W_SET = 2 * HIDDEN + HT * C
        w_at = 3 * HT * TG
        w1_parts = [[bf(w_at + k * W_SET + part * HIDDEN, HIDDEN)[0:HC, :].rearrange("p (c n) -> p c n", c=2)
                     for part in range(2)] for k in range(2)]
        w2_parts = [[bf(w_at + k * W_SET + 2 * HIDDEN + part * HT * C // 2, HT * C // 2).rearrange(
            "p (m n) -> p m n", m=HT) for part in range(2)] for k in range(2)]
        assert w_at + 2 * W_SET <= STREAMS * ARENA
        feat_hi, feat_lo = (featT[:, :, :].rearrange("p c n -> p (c n)").bitcast(BF16)[
            :, part * 2 * T:(part + 1) * 2 * T].rearrange("p (c n) -> p c n", c=2) for part in range(2))

        q_at = HT * T
        wq1T = bf(q_at, HT * P)[0:HC, :].rearrange("p (c n) -> p c n", c=2)
        wq2T = bf(q_at + HT * P, HT * C // 2).rearrange("p (m n) -> p m n", m=HT)
        q_end = q_at + HT * P + HT * C // 2
        w1_s = flat_arena[:, q_end:q_end + HT * C].rearrange("p (m n) -> p m n", m=HT)
        w1_q = bf(q_end + HT * C, HT * C // 2).rearrange("p (m n) -> p m n", m=HT)
        w2_q = bf(q_end + HT * C + HT * C // 2, HIDDEN)[0:HC, :].rearrange("p (c n) -> p c n", c=2)
        q_end2 = q_end + HT * C + HT * C // 2 + HIDDEN
        csb = flat_arena[0:HC, q_end2:q_end2 + 2 * P].rearrange("p (c n) -> p c n", c=2)
        sw2b = flat_arena[0:HC, q_end2 + 2 * P:q_end2 + 4 * P].rearrange("p (c n) -> p c n", c=2)
        assert q_end2 + 4 * P <= STREAMS * ARENA
        oq = flat_arena[:, q_end:q_end + B * C].rearrange("p (b n) -> p b n", b=B)
        wmax = flat_arena[:, q_end2 + 4 * P:q_end2 + 4 * P + C]
        assert q_end2 + 4 * P + C <= STREAMS * ARENA

        @block.gpsimd
        def _(pool):
            nc.gpsimd.memset(ident[:, :], 0.0).then_inc(sem("mask_zero"), 1)
            nc.gpsimd.memset(identb[:, :], 0.0).then_inc(sem("mask_zero"), 1)
            nc.gpsimd.memset(diag_off[:, :, :], 0.0).then_inc(sem("mask_zero"), 1)
            nc.gpsimd.memset(diag_one[:, :], 0.0).then_inc(sem("mask_zero"), 1)
            nc.gpsimd.memset(pick[:, :, :], 0.0).then_inc(sem("mask_zero"), 1)
            nc.gpsimd.memset(ones[:, :], 1.0).then_inc(sem("masks_ready"), 1)
            pool.wait_ge(sem("mask_zero"), 5)
            for k in range(3):
                nc.gpsimd.affine_select(out=pick[:, :, :], in_=pick[:, :, :], compare_op=ALU.not_equal, fill=1.0,
                                        base=-HEADS * k, pattern=[[-1, HEADS], [0, P]],
                                        channel_multiplier=1).then_inc(sem("pick_ready"), 1)
                pool.wait_ge(sem("pick_ready"), k + 1)
            for m, fill in ((ident, 1.0), (identb, 1.0), (diag_one, float(np.exp(SCALE) - 1.0))):
                nc.gpsimd.affine_select(out=m[:, :], in_=m[:, :], compare_op=ALU.not_equal, fill=fill, base=0,
                                        pattern=[[-1, P]], channel_multiplier=1).then_inc(sem("masks_ready"), 1)
            nc.gpsimd.affine_select(out=diag_off[:, :, :], in_=diag_off[:, :, :], compare_op=ALU.not_equal,
                                    fill=-DIAG_VAL, base=0, pattern=[[0, GROUPS], [-1, P]],
                                    channel_multiplier=1).then_inc(sem("masks_ready"), 1)
            nc.gpsimd.iota(iota8[:, :], pattern=[[1, EXPERTS]], base=0, channel_multiplier=0,
                           allow_small_or_imprecise_dtypes=True).then_inc(sem("masks_ready"), 1)

        def moe_up(pe, e, k, g):
            for m in range(HT):
                q = g * HT + m
                pe.wait_ge(sem("moe_gelu"), e * (NG * HT) + k * NG * HT + q + 1)
                for c in range(2):
                    for w, x in ((0, feat_hi), (0, feat_lo), (1, feat_hi)):
                        last = nc.tensor.matmul(ps[0][:, q % 4, :], w1_parts[k][w][:, c, m * P:(m + 1) * P],
                                                x[:, c, g * TG:(g + 1) * TG], start=(c == 0 and w == 0 and x is feat_hi),
                                                stop=(c == 1 and w == 1))
                last.then_inc(sem("moe_hidden"), 1)

        def moe_down(pe, e, k, g):
            pe.wait_ge(sem("moe_he_lo"), e * (NG * HT) + k * NG * HT + (g + 1) * HT + HT)
            for t in range(4):
                pe.wait_ge(sem("moe_added"), e * B + k * B + g * 4 + t + 1)
                for m in range(HT):
                    for h, w in ((he_hi, 0), (he_hi, 1), (he_lo, 0)):
                        last = nc.tensor.matmul(ps[1][:, t, 0:C], h[g % 2][:, m, t * P:(t + 1) * P],
                                                w2_parts[k][w][:, m, :], start=(m == 0 and w == 0 and h is he_hi),
                                                stop=(m == HT - 1 and h is he_lo))
                last.then_inc(sem("moe_out"), 1)

        def experts(eng, expert):
            with eng.Fori(0, EXPERTS - 3, 2) as e:
                expert(e, 0, True)
                expert(e, 1, True)
            expert(EXPERTS - 2, 0, True)
            expert(EXPERTS - 2, 1, False)

        @block.tensor
        def _(pe):
            loaded(pe)

            tok_w, tok_pw = chunks("tok_w"), chunks("tok_pw")

            def tiles(s, lo, n):
                return ps[s][:, lo:lo + n // 2, :].rearrange("p b n -> p (b n)").rearrange(
                    "p (t n) -> p t n", t=n)

            def tok_qk(s, n, dma):
                pe.wait_ge(sem(f"tok_x{s}"), dma)
                xT = bufs[s].xT
                for part in range(2):
                    o = tiles(s, 2 * part, STRIDE)
                    for t in range(STRIDE):
                        for c in range(2):
                            cols = slice(t, N_IN, STRIDE) if part == 0 else slice(t * P, (t + 1) * P)
                            last = nc.tensor.matmul(o[:, t, 0:C], xT[:, c, cols],
                                                    tok_w[:, c, part * C:(part + 1) * C],
                                                    start=(c == 0), stop=(c == 1))
                    last.then_inc(sem(f"tok_{'qk'[part]}"), 1)

            def tok_v(s, n):
                pe.wait_ge(*after("tok_pooled", n))
                o = tiles(s, 0, 4)
                for t in range(4):
                    for c in range(2):
                        last = nc.tensor.matmul(o[:, t, 0:C], bufs[s].xT[:, c, t * P:(t + 1) * P],
                                                tok_w[:, c, 2 * C:3 * C], start=(c == 0), stop=(c == 1))
                last.then_inc(sem("tok_v"), 1)

            def tok_turn_k(s, n):
                pe.wait_ge(*after("tok_vpad", n))
                b = bufs[s]
                for g in range(GROUPS):
                    for t in range(STRIDE):
                        at = (1 + t) * HEADS + 4 * g
                        nc.tensor.transpose(ps[s][:, g, t * P:(t + 1) * P], b.qk_pad[:, at:at + 4, :], ident[:, :])
                for g in range(GROUPS):
                    last = nc.tensor.transpose(ps[s][:, 3, g * P:(g + 1) * P], b.qk_pad[:, 4 * g:4 * g + 4, :],
                                               ident[:, :])
                last.then_inc(sem("tok_turned"), 1)

            def tok_scores(s, n, half):
                b = bufs[s]
                if half == 0:
                    pe.wait_ge(*after("tok_kT", n))
                    pe.wait_ge(*after("tok_qT", n))
                else:
                    pe.wait_ge(*after("tok0_pT_a", n))
                    pe.wait_ge(*after("tok0_pT_b", n))
                for g in range(GROUPS):
                  for jj in range(2):
                    r = 32 * (2 * half + jj)
                    for w in range(WINDOWS):
                        last = nc.tensor.matmul(
                            ps[s][w * WQ:(w + 1) * WQ, 2 * jj + g // 2, (g % 2) * 256:(g % 2 + 1) * 256],
                            b.qT[r:r + HD, g, w * WQ:(w + 1) * WQ], b.kT[r:r + HD, g, 2 * w:2 * w + 2, :],
                            start=True, stop=True)
                last.then_inc(sem(f"tok{half}_scores"), 1)

            def tok_pv(s, n, half):
                b = bufs[s]
                pe.wait_ge(*after(f"tok{half}_pT_a", n))
                pe.wait_ge(*after(f"tok{half}_pT_b", n))
                pT = b.pT.rearrange("p (l h n) -> p l h n", l=6, h=2)
                for l in range(6):
                    h = 4 * (l % GROUPS) + 2 * half + l // GROUPS
                    at = TOK_PV + h * (HD + 1)
                    for w in range(WINDOWS):
                        for k in range(2):
                            last = nc.tensor.matmul(
                                ps[s][w * WQ:(w + 1) * WQ, 3, at:at + HD + 1],
                                pT[:, l, k, w * WQ:(w + 1) * WQ], b.v_ext[:, (2 * w + k) * HEADS + h, :],
                                start=(k == 0), stop=(k == 1))
                last.then_inc(sem(f"tok{half}_pv" if half == 0 else "tok_pv"), 1)

            with pe.Fori(0, B - STREAMS + 1, STREAMS) as i:
                for s in range(STREAMS):
                    tok_qk(s, i + s + 1, i * (16 // STREAMS) + 16)
                both(tok_v, i + 1)
                both(tok_turn_k, i + 1)
                for half in range(2):
                    both(tok_scores, i + 1, half)
                    both(lambda s, n: pe_turn_probs(pe, f"tok{half}", s, n), i + 1)
                    both(tok_pv, i + 1, half)
                both(lambda s, n: pe_turn(pe, "tok_on", "tok_oturned", s, n, bufs[s].on, 0), i + 1)
                both(lambda s, n: pe_project(pe, "tok", s, n, tok_pw), i + 1)
                pe.wait_ge(sem("tok_h"), i + STREAMS)

            for pre, w, pw in (("at", chunks("at_w"), chunks("at_pw")), ("ff", chunks("ff_w"), chunks("ff_pw"))):
                with pe.Fori(0, B - STREAMS + 1, STREAMS) as i:
                    both(lambda s, n: pe_turn(pe, f"{pre}_xn", f"{pre}_xturned", s, n, bufs[s].xn, 0), i + 1)
                    both(lambda s, n: at_pe_qkv(pe, pre, s, n, w), i + 1)
                    both(lambda s, n: at_pe_turn_qk(pe, pre, s, n), i + 1)
                    both(lambda s, n: at_pe_scores(pe, pre, s, n), i + 1)
                    both(lambda s, n: pe_turn_probs(pe, pre, s, n), i + 1)
                    both(lambda s, n: at_pe_pv(pe, pre, s, n), i + 1)
                    both(lambda s, n: pe_turn(pe, f"{pre}_on", f"{pre}_oturned", s, n, bufs[s].on, 0), i + 1)
                    both(lambda s, n: pe_project(pe, pre, s, n, pw), i + 1)
            with pe.Fori(0, B - STREAMS + 1, STREAMS) as i:
                both(lambda s, n: pe_turn(pe, "ff2_xn", "ff2_xturned", s, n, bufs[s].xn, 0), i + 1)

                def gate(s, n):
                    pe.wait_ge(*after("ff2_xT", n))
                    for c in range(2):
                        last = nc.tensor.matmul(ps[s][:, 1, 0:EXPERTS], bufs[s].xT[:, c, 0:P],
                                                chunks("gate_w")[:, c, :], start=(c == 0), stop=(c == 1))
                    last.then_inc(sem("ff_logits"), 1)
                both(gate, i + 1)

            pe.wait_ge(sem("moe_cw"), 1)
            with pe.Fori(0, B - STREAMS + 1, STREAMS) as i:
                def turn_cw(s, n):
                    pe.wait_ge(*after("moe_cw_copy", n))
                    nc.tensor.transpose(ps[s][0:EXPERTS, 0, 0:P], bufs[s].xn[:, 0:EXPERTS],
                                        ident[:, :]).then_inc(sem("moe_cwturned"), 1)

                def bias2(s, n):
                    pe.wait_ge(*after("moe_cwT", n))
                    nc.tensor.matmul(ps[s][:, 1, 0:C], bufs[s].onT[0:EXPERTS, 0, :], const("b2"),
                                     start=True, stop=True).then_inc(sem("moe_bias2"), 1)
                both(turn_cw, i + 1)
                both(bias2, i + 1)
            pe.wait_ge(sem("moe_start"), 1)

            def expert(e, k, more):
                pe.wait_ge(sem("moe_w_lo"), e + k + 1)
                for g in range(NG):
                    moe_up(pe, e, k, g)
                    if g > 0:
                        moe_down(pe, e, k, g - 1)
                moe_down(pe, e, k, NG - 1)
            experts(pe, expert)

            l1_w, l1_pw = chunks("l1_w"), chunks("l1_pw")

            def l1_qv(s, n, part, c):
                if part == 0 and c == 0:
                    pe.wait_ge(*after("l1_xT", n))
                last = nc.tensor.matmul(ps[s][:, 2 - part, part * C:(part + 1) * C], bufs[s].xT[:, c, 0:P],
                                        l1_w[:, c, 2 * part * C:(2 * part + 1) * C],
                                        start=(c == 0), stop=(c == 1))
                if c == 1:
                    last.then_inc(sem("l1_" + "qv"[part]), 1)

            def l1_turn_q(s, n):
                pe.wait_ge(*after("l1_pad", n))
                for g in range(GROUPS):
                    last = nc.tensor.transpose(ps[s][:, 0, g * P:(g + 1) * P],
                                               bufs[s].qk_pad[:, 4 * g:4 * g + 4, :], ident[:, :])
                last.then_inc(sem("l1_qturned"), 1)

            def l1_gram(s, n, j, g):
                b = bufs[s]
                if g == 0:
                    nc.tensor.matmul(ps[s][:, j, 0:GROUPS * P], identb[:, :],
                                     diag_off[:, :, :].rearrange("p a n -> p (a n)"),
                                     start=True, stop=False, skip_group_check=True)
                last = nc.tensor.matmul(ps[s][:, j, g * P:(g + 1) * P], b.qT[32 * j:32 * j + HD, g, :],
                                        b.qT[32 * j:32 * j + HD, g, :], start=False, stop=True,
                                        skip_group_check=True)
                if g == GROUPS - 1:
                    last.then_inc(sem("l1_gram"), 1)

            def l1_half_step(s, n, it):
                b = bufs[s]
                if it == 0:
                    pe.wait_ge(*after("l1_kernel_lo", n))
                else:
                    pe.wait_ge(sem("l1_xlo"), halfs(n, it - 1))
                for k in range(HEADS):
                    for part in (b.hi, b.lo):
                        last = nc.tensor.matmul(ps[s][:, 3, SUMS + 2 * k:SUMS + 2 * k + 2],
                                                part[:, k * P:(k + 1) * P], b.x_parts[:, k, :],
                                                start=(part is b.hi), stop=(part is b.lo))
                last.then_inc(sem("l1_sums"), 1)

            def l1_turn_u(s, n):
                pe.wait_ge(*after("l1_uparts", n))
                nc.tensor.transpose(ps[s][:, 3, 0:P // 2].bitcast(BF16), bufs[s].u_parts,
                                    identb[:, :]).then_inc(sem("l1_uturned"), 1)

            def l1_u_rows(s, n, half):
                if half == 0:
                    pe.wait_ge(*after("l1_uT", n))
                for h in range(8 * half, 8 + 4 * half):
                    last = nc.tensor.matmul(ps[s][:, h // 4, (h % 4) * P:(h % 4 + 1) * P],
                                            pick[:, h, :], bufs[s].uT_parts, start=True, stop=True)
                last.then_inc(sem("l1_urows"), 1)

            def l1_turn_max(s, n):
                pe.wait_ge(*after("l1_rowmax", n))
                nc.tensor.transpose(ps[s][0:HEADS, 3, 0:P], bufs[s].stats12, ident[:, :]).then_inc(
                    sem("l1_maxturned"), 1)

            def l1_spread_max(s, n):
                pe.wait_ge(*after("l1_maxdiag", n))
                nc.tensor.matmul(ps[s][:, 3, P:P + HEADS], ones[0:HEADS, :], bufs[s].maxdiag,
                                 start=True, stop=True).then_inc(sem("l1_maxspread"), 1)

            def l1_pv_diagonal(s, n):
                pe.wait_ge(*after("l1_sv", n))
                nc.tensor.matmul(ps[s][:, 3, 0:HEADS * (HD + 1)], diag_one[:, :], bufs[s].v_ext[:, 0:HEADS, :],
                                 start=True, stop=False, skip_group_check=True)

            def l1_pv(s, n, half):
                b = bufs[s]
                o = ps[s][:, 3, 0:HEADS * (HD + 1)]
                if half == 0:
                    pe.wait_ge(*after("l1_probs_lo", n))
                for h in range(HEADS // 2 * half, HEADS // 2 * (half + 1)):
                    for part in (b.hi, b.lo):
                        for v in (b.v_hi, b.v_lo):
                            last = nc.tensor.matmul(o[:, h * (HD + 1):(h + 1) * (HD + 1)],
                                                    part[:, place(h) * P:(place(h) + 1) * P], v[:, h, :],
                                                    start=False, stop=True, skip_group_check=True)
                if half == 1:
                    last.then_inc(sem("l1_pv"), 1)

            def l1_project(s, n, c):
                if c == 0:
                    pe.wait_ge(*after("l1_onT", n))
                last = nc.tensor.matmul(ps[s][:, 1, 0:C], bufs[s].onT[:, c, :], l1_pw[:, c, :],
                                        start=(c == 0), stop=(c == 1))
                if c == 1:
                    last.then_inc(sem("l1_proj"), 1)

            def l1_stage(post, half, pre):
                for it in range(2 * SINKHORN_ITERS):
                    if half:
                        l1_half_step(*half, it)
                    if pre and it == 14:
                        pe.wait_ge(*after("l1_vcopy", pre[1]))
                    if post:
                        if it == 1:
                            l1_turn_u(*post)
                        if it in (2, 3):
                            l1_u_rows(*post, it - 2)
                        if it == 6:
                            l1_turn_max(*post)
                        if it == 7:
                            l1_spread_max(*post)
                        if it == 9:
                            l1_pv_diagonal(*post)
                        if it in (11, 12):
                            l1_pv(*post, it - 11)
                        if it == 13:
                            pe_turn(pe, "l1_on", "l1_oturned", *post, bufs[post[0]].on, 3)
                        if it in (14, 15):
                            l1_project(*post, it - 14)
                    if pre:
                        if it == 4:
                            pe_turn(pe, "l1_xn", "l1_xturned", *pre, bufs[pre[0]].xn, 2)
                        if it in (5, 6):
                            l1_qv(*pre, 0, it - 5)
                        if it in (8, 10):
                            l1_qv(*pre, 1, (it - 8) // 2)
                        if it == 13:
                            l1_turn_q(*pre)
                        if it == 14:
                            pe.wait_ge(*after("l1_qT", pre[1]))
                            l1_gram(*pre, 0, 0)
                            l1_gram(*pre, 0, 1)
                        if it == 15:
                            l1_gram(*pre, 0, 2)
                            l1_gram(*pre, 2, 0)
                        if it == 16:
                            l1_gram(*pre, 2, 1)
                            l1_gram(*pre, 2, 2)
                        if it == 17:
                            l1_gram(*pre, 3, 0)
                            l1_gram(*pre, 3, 1)
                        if it == 18:
                            l1_gram(*pre, 3, 2)
                            if post:
                                pe.wait_ge(*after("l1_biased", post[1]))
                            l1_gram(*pre, 1, 0)
                        if it == 19:
                            l1_gram(*pre, 1, 1)
                            l1_gram(*pre, 1, 2)
            sinkhorn_stages(pe, l1_stage)
            with pe.Fori(0, B - STREAMS + 1, STREAMS) as i:
                both(lambda s, n: pe_turn(pe, "q_xn", "q_xturned", s, n, bufs[s].xn, 0), i + 1)

            p0 = ps[0]
            pe.wait_ge(sem("q_wmax"), 1)
            for c in range(2):
                last = nc.tensor.transpose(p0[0:HC, 3, c * P:(c + 1) * P], wmax[:, c * HC:(c + 1) * HC], ident[:, :])
            last.then_inc(sem("q_wmaxturned"), 1)
            pe.wait_ge(sem("q_cs_rows"), 1)
            for c in range(2):
                last = nc.tensor.matmul(p0[:, 0, c * HC:(c + 1) * HC], csb[:, c, :], ident[0:HC, 0:HC],
                                        start=True, stop=True)
            last.then_inc(sem("q_csrow"), 1)
            pe.wait_ge(sem("q_range"), 1)
            nc.tensor.transpose(p0[0:2, 1, 0:HC], small[0:HC, 20:22], ident[0:HC, 0:HC]).then_inc(
                sem("q_rangeturned"), 1)
            pe.wait_ge(sem("q_rangediag"), 1)
            nc.tensor.matmul(p0[:, 2, 0:2], ones[0:2, :], small[0:2, 24:26], start=True,
                             stop=True).then_inc(sem("q_rangespread"), 1)
            pe.wait_ge(sem("q_w_quant"), 1)
            tb = ps[1][:, :, :].rearrange("p b n -> p (b n)").bitcast(BF16).rearrange("p (b n) -> p b n", b=4)
            for c in range(2):
                for m in range(HT):
                    nc.tensor.transpose(tb[0:HC, c, m * P:(m + 1) * P], w1_q[:, m, c * HC:(c + 1) * HC],
                                        identb[:, :])
            for c in range(2):
                for m in range(HT):
                    last = nc.tensor.transpose(tb[:, 2 + m // 3, (m % 3) * C + c * HC:(m % 3) * C + (c + 1) * HC],
                                               w2_q[:, c, m * P:(m + 1) * P], identb[0:HC, 0:HC])
            last.then_inc(sem("q_wturned"), 1)
            for c in range(2):
                last = nc.tensor.matmul(p0[:, 3, c * HC:(c + 1) * HC], sw2b[:, c, :], ident[0:HC, 0:HC],
                                        start=True, stop=True)
            last.then_inc(sem("q_sw2row"), 1)
            pe.wait_ge(sem("q_xq"), 1)
            pe.wait_ge(sem("q_wT"), 1)
            pe.wait_ge(sem("q_sw2"), 1)
            for g in range(NG):
                for m in range(HT):
                    k = g * HT + m
                    if k >= 8:
                        pe.wait_ge(sem("q_gelu"), k - 7)
                    o = ps[k % 8 // 4][:, k % 4, :]
                    for c in range(2):
                        last = nc.tensor.matmul(o, wq1T[:, c, m * P:(m + 1) * P], xq[:, c, g * TG:(g + 1) * TG],
                                                start=(c == 0), stop=(c == 1))
                    last.then_inc(sem("q_up"), 1)
            pe.wait_ge(sem("q_hmax"), 1)
            nc.tensor.transpose(p0[0:1, 0, 0:P], small[:, 30:31], ident[:, :]).then_inc(sem("q_hmaxturned"), 1)
            pe.wait_ge(sem("q_hmaxone"), 1)
            nc.tensor.matmul(p0[:, 1, 0:1], ones[0:1, :], small[0:1, 31:32], start=True,
                             stop=True).then_inc(sem("q_hmaxspread"), 1)
            pe.wait_ge(sem("q_hscale"), 1)
            for t in range(B):
                if t % 4 == 0:
                    pe.wait_ge(sem("q_hq"), t // 4 + 1)
                if t >= 8:
                    pe.wait_ge(sem("q_down_read"), t - 7)
                o = ps[t % 8 // 4][:, t % 4, 0:C]
                for m in range(HT):
                    last = nc.tensor.matmul(o, hqs[t // 4][:, m, (t % 4) * P:(t % 4 + 1) * P], wq2T[:, m, :],
                                            start=(m == 0), stop=(m == HT - 1))
                last.then_inc(sem("q_down"), 1)
            pe.wait_ge(sem("q_orange"), 1)
            nc.tensor.transpose(p0[0:2, 1, 0:P], small[:, 40:42], ident[:, :]).then_inc(sem("q_orangeturned"), 1)
            pe.wait_ge(sem("q_orangediag"), 1)
            nc.tensor.matmul(p0[:, 2, 0:2], ones[0:2, :], small[0:2, 76:78], start=True,
                             stop=True).then_inc(sem("q_orangespread"), 1)

        @block.scalar
        def _(act):
            loaded(act)

            def tok_kT(s, n):
                act.wait_ge(*after("tok_turned", n))
                nc.scalar.activation(bufs[s].kT.rearrange("p g t n -> p (g t n)"),
                                     ps[s][:, 0:3, :].rearrange("p b n -> p (b n)"),
                                     ACT.Copy).then_inc(sem("tok_kT"), 1)
            with act.Fori(0, B - STREAMS + 1, STREAMS) as i:
                both(tok_kT, i + 1)
                for half in range(2):
                    both(lambda s, n: act_exp(act, f"tok{half}", s, n), i + 1)
                    both(lambda s, n: act_probs(act, f"tok{half}", s, n), i + 1)
                both(lambda s, n: act_turned(act, "tok_oturned", "tok_onT", s, n, bufs[s].onT, 0), i + 1)

            for pre in ("at", "ff"):
                with act.Fori(0, B - STREAMS + 1, STREAMS) as i:
                    gain, bias = (const("ln1_g"), const("ln1_b")) if pre == "ff" else (None, None)
                    both(lambda s, n: act_turned(act, f"{pre}_xturned", f"{pre}_xT", s, n,
                                                 bufs[s].xT[:, :, 0:P], 0, gain, bias), i + 1)
                    both(lambda s, n: at_act_qk(act, pre, s, n), i + 1)
                    both(lambda s, n: act_exp(act, pre, s, n), i + 1)
                    both(lambda s, n: at_act_probs(act, pre, s, n), i + 1)
                    both(lambda s, n: act_turned(act, f"{pre}_oturned", f"{pre}_onT", s, n, bufs[s].onT, 0), i + 1)
            with act.Fori(0, B - STREAMS + 1, STREAMS) as i:
                both(lambda s, n: act_turned(act, "ff2_xturned", "ff2_xT", s, n, bufs[s].xT[:, :, 0:P], 0,
                                             const("ln2_g"), const("ln2_b")), i + 1)

                def keep(s, n):
                    act.wait_ge(*after("ff2_xT", n))
                    for c in range(2):
                        last = nc.scalar.activation(feat_hi[:, c, bass.ds((n - 1) * P, P)],
                                                    bufs[s].xT[:, c, 0:P], ACT.Copy)
                    last.then_inc(sem("ff_feat_hi"), 1)
                both(keep, i + 1)
                act.wait_ge(sem("ff_feat_lo"), i + STREAMS)

            act.wait_ge(sem("moe_gap"), 1)
            nc.scalar.activation(gw[:, :, 1:2], gw[:, :, 3:4], ACT.Exp).then_inc(sem("moe_gapexp"), 1)
            with act.Fori(0, B - STREAMS + 1, STREAMS) as i:
                def cwT(s, n):
                    act.wait_ge(*after("moe_cwturned", n))
                    nc.scalar.activation(bufs[s].onT[0:EXPERTS, 0, :], ps[s][0:EXPERTS, 0, 0:P],
                                         ACT.Copy).then_inc(sem("moe_cwT"), 1)
                both(cwT, i + 1)
            act.wait_ge(sem("moe_start"), 1)

            def split_weights(k, n):
                act.wait_ge(sem(f"moe_w1_{k}"), (n - (1 + k)) * 8 + 16)
                act.wait_ge(sem(f"moe_w2_{k}"), (n - (1 + k)) * 8 + 16)
                nc.scalar.activation(w1_parts[k][0], ew1[k], ACT.Copy)
                nc.scalar.activation(w2_parts[k][0], ew2[k], ACT.Copy).then_inc(sem("moe_w_hi"), 1)
            split_weights(0, 1)

            def expert(e, k, more):
                nc.scalar.activation(b1cur[:, k, :], const("b1")[:, bass.ds(e * HT + k * HT, HT)],
                                     ACT.Copy).then_inc(sem("moe_b1"), 1)
                act.wait_ge(sem("moe_b1"), e + k + 1)
                for g in range(NG):
                    act.wait_ge(sem("moe_out"), e * B + k * B + g * 4 + 4)
                    for m in range(HT):
                        at = g * HT + m + 1
                        act.wait_ge(sem("moe_hidden"), e * (NG * HT) + k * NG * HT + at)
                        bias = b1cur[:, k, m:m + 1]
                        nc.scalar.activation(he_hi[g % 2][:, m, :], ps[0][:, (at - 1) % 4, :], ACT.Gelu, bias=bias)
                        act.wait_ge(sem("moe_he_lo"), e * (NG * HT) + k * NG * HT + at)
                        nc.scalar.activation(he[:, m, :], ps[0][:, (at - 1) % 4, :], ACT.Gelu,
                                             bias=bias).then_inc(sem("moe_gelu"), 1)
                    if g == 1 and more:
                        split_weights(1 - k, e + k + 2)
            experts(act, expert)

            def qT(s, n):
                act.wait_ge(*after("l1_qturned", n))
                nc.scalar.activation(bufs[s].qT, ps[s][:, 0, 0:GROUPS * P].rearrange(
                    "p (g n) -> p g n", g=GROUPS), ACT.Copy).then_inc(sem("l1_qT"), 1)

            def kernel_exp(s, n, k):
                b = bufs[s]
                j = BANK_ORDER[k]
                act.wait_ge(sem("l1_gram"), n * 4 + (k + 1 - 4))
                for dst in (b.hi, b.p):
                    last = nc.scalar.activation(dst[:, j * GROUPS * P:(j + 1) * GROUPS * P],
                                                ps[s][:, j, 0:GROUPS * P], ACT.Exp,
                                                scale=1.0 / OT_REG, bias=neg_reg[:, 0:1])
                last.then_inc(sem("l1_kernel"), 1)

            def uT(s, n):
                act.wait_ge(*after("l1_uturned", n))
                nc.scalar.activation(bufs[s].uT_parts, ps[s][0:3 * HEADS, 3, 0:P // 2].bitcast(BF16),
                                     ACT.Copy).then_inc(sem("l1_uT"), 1)

            def probs(s, n):
                act.wait_ge(*after("l1_z", n))
                nc.scalar.activation(bufs[s].hi, bufs[s].pT, ACT.Exp).then_inc(sem("l1_probs_hi"), 1)
                act.wait_ge(*after("l1_probs_hi", n))
                nc.scalar.activation(bufs[s].pT, bufs[s].pT, ACT.Exp).then_inc(sem("l1_probs"), 1)

            def l1_stage(post, half, pre):
                if post:
                    uT(*post)
                if pre:
                    act_turned(act, "l1_xturned", "l1_xT", *pre, bufs[pre[0]].xT[:, :, 0:P], 2)
                if post:
                    probs(*post)
                    act_turned(act, "l1_oturned", "l1_onT", *post, bufs[post[0]].onT, 3)
                if pre:
                    qT(*pre)
                    for k in range(4):
                        kernel_exp(*pre, k)
            sinkhorn_stages(act, l1_stage)

            with act.Fori(0, B - STREAMS + 1, STREAMS) as i:
                def keep(s, n):
                    act.wait_ge(*after("q_xturned", n))
                    for c in range(2):
                        last = nc.scalar.activation(featT[:, c, bass.ds((i + s) * P, P)],
                                                    ps[s][0:HC, 0, c * P:(c + 1) * P], ACT.Copy)
                    last.then_inc(sem("q_featT"), 1)
                both(keep, i + 1)

            act.wait_ge(sem("q_hidden_scale"), 1)
            for g in range(NG):
                for m in range(HT):
                    k = g * HT + m
                    act.wait_ge(sem("q_up"), k + 1)
                    nc.scalar.activation(gelu_out[:, m, g * TG:(g + 1) * TG], ps[k % 8 // 4][:, k % 4, :],
                                         ACT.Gelu, bias=const("q_b1")[:, m:m + 1],
                                         scale=small[:, 48 + m:49 + m]).then_inc(sem("q_gelu"), 1)

        @block.vector
        def _(dve):
            for s in range(STREAMS):
                nc.vector.memset(bufs[s].qk_pad, 0.0).then_inc(sem("pads_ready"), 1)
                nc.vector.memset(bufs[s].v_ext, 1.0).then_inc(sem("pads_ready"), 1)
            nc.vector.memset(neg_reg[:, :], -1.0 / OT_REG).then_inc(sem("pads_ready"), 1)
            loaded(dve)

            chain = [0]

            def link(ins):
                chain[0] += 1
                ins.then_inc(sem("dve_chain"), 1)
                dve.wait_ge(sem("dve_chain"), chain[0])

            def row(n, src=None):
                return (hs if src is None else src)[:, bass.ds(n - 1, 1), :].rearrange("p o c -> p (o c)")

            def residual(pre, s, n, h, bias):
                dve.wait_ge(*after(f"{pre}_proj", n))
                nc.vector.tensor_tensor(bufs[s].t1, ps[s][:, 1, 0:C], bias, ALU.add).then_inc(sem(f"{pre}_biased"), 1)
                dve.wait_ge(*after(f"{pre}_biased", n))
                nc.vector.tensor_tensor(bufs[s].t1, h, bufs[s].t1, ALU.add).then_inc(sem(f"{pre}_h"), 1)

            tok_b = const("tok_b")

            def tok_pool(s, n):
                dve.wait_ge(*after("tok_q", n))
                q4 = ps[s][:, 0:2, :].rearrange("p b n -> p (b n)").rearrange("p (t n) -> p n t", t=STRIDE)
                nc.vector.tensor_reduce(bufs[s].xn, q4[:, 0:C, :], X, ALU.max).then_inc(sem("tok_pooled"), 1)

            def tok_qk_pad(s, n):
                b = bufs[s]
                dve.wait_ge(*after("tok_pooled", n))
                nc.vector.tensor_tensor(b.qk_pad[:, 0:HEADS, 0:HD], b.xn.rearrange("p (h d) -> p h d", d=HD),
                                        tok_b[:, 0:C].rearrange("p (h d) -> p h d", d=HD), ALU.add)
                dve.wait_ge(*after("tok_k", n))
                k4 = ps[s][:, 2:4, :].rearrange("p b n -> p (b n)").rearrange("p (t n) -> p t n", t=STRIDE)
                for t in range(STRIDE):
                    last = nc.vector.tensor_tensor(
                        b.qk_pad[:, (1 + t) * HEADS:(2 + t) * HEADS, 0:HD],
                        k4[:, t, 0:C].rearrange("p (h d) -> p h d", d=HD),
                        tok_b[:, C:2 * C].rearrange("p (h d) -> p h d", d=HD), ALU.add)

            def tok_v_pad(s, n):
                b = bufs[s]
                dve.wait_ge(*after("tok_v", n))
                v4 = ps[s][:, 0:2, :].rearrange("p b n -> p (b n)").rearrange("p (t n) -> p t n", t=4)
                for t in range(4):
                    last = nc.vector.tensor_tensor(
                        b.v_ext[:, t * HEADS:(t + 1) * HEADS, 0:HD],
                        v4[:, t, 0:C].rearrange("p (h d) -> p h d", d=HD),
                        tok_b[:, 2 * C:3 * C].rearrange("p (h d) -> p h d", d=HD), ALU.add)
                last.then_inc(sem("tok_vpad"), 1)

            def tok_qT(s, n):
                dve.wait_ge(*after("tok_turned", n))
                nc.vector.tensor_copy(bufs[s].qT, ps[s][:, 3, 0:GROUPS * P].rearrange(
                    "p (g n) -> p g n", g=GROUPS)).then_inc(sem("tok_qT"), 1)

            with dve.Fori(0, B - STREAMS + 1, STREAMS) as i:
                both(tok_pool, i + 1)
                both(tok_qk_pad, i + 1)
                both(tok_v_pad, i + 1)

                both(tok_qT, i + 1)
                for half in range(2):
                    both(lambda s, n: dve_softmax_shift(dve, f"tok{half}_scores", f"tok{half}", s, n, ps[s][:, :, :].rearrange(
                        "p (a b) n -> p a (b n)", a=2)[:, :, 0:768].rearrange("p a (g k) -> p a g k", g=GROUPS),
                        2, GROUPS, 256), i + 1)
                    both(lambda s, n: dve_probs(dve, f"tok{half}", s, n), i + 1)
                both(lambda s, n: dve_softmax_norm(dve, "tok", s, n, TOK_PV), i + 1)

                def tok_out(s, n):
                    dve.wait_ge(*after("tok_proj", n))
                    nc.vector.tensor_tensor(bufs[s].t1, ps[s][:, 1, 0:C], const("tok_pb"), ALU.add).then_inc(sem("tok_h"), 1)
                    dve.wait_ge(*after("tok_h", n))
                    dve_stats(dve, "n0", s, n, row(n))
                both(tok_out, i + 1)

            def rstd_all(part):
                dve.wait_ge(*after(f"{part}_mv", B))
                for t in range(B):
                    ins = nc.vector.bn_aggr(meanvar[:, t, :], allstats[:, t, :])
                link(ins)
                link(nc.vector.tensor_scalar(varp[:, :], meanvar[:, :, 1], LN_EPS, None, ALU.add))
                for step in rsqrt_steps(rstd[:, :], varp[:, :], newton[:, :]):
                    link(step())

            rstd_all("n0")
            with dve.Fori(0, B - STREAMS + 1, STREAMS) as i:
                both(lambda s, n: dve_normalize(dve, "at", s, n, row(n), bufs[s].xn), i + 1)
                both(lambda s, n: at_dve_qkv(dve, "at", s, n, const("at_b")), i + 1)
                both(lambda s, n: dve_softmax_shift(dve, "at_scores", "at", s, n, score_view(s), 4, GROUPS, P), i + 1)
                both(lambda s, n: at_dve_probs(dve, "at", s, n), i + 1)
                both(lambda s, n: dve_softmax_norm(dve, "at", s, n), i + 1)

                def at_out(s, n):
                    residual("at", s, n, row(n), const("at_pb"))
                    dve.wait_ge(*after("at_h", n))
                    dve_stats(dve, "n1", s, n, row(n))
                both(at_out, i + 1)

            rstd_all("n1")
            with dve.Fori(0, B - STREAMS + 1, STREAMS) as i:
                def own_residual(s, n):
                    nc.vector.tensor_scalar(bufs[s].t1, row(n),
                                            meanvar[:, bass.ds(n - 1, 1), 0:1].rearrange("p o c -> p (o c)"),
                                            rstd[:, bass.ds(n - 1, 1)], ALU.subtract, ALU.mult).then_inc(
                                                sem("ff_x3"), 1)
                    dve.wait_ge(*after("ff_x3", n))
                    dve_stats(dve, "n2", s, n, row(n, x3))
                both(own_residual, i + 1)
            rstd_all("n2")
            with dve.Fori(0, B - STREAMS + 1, STREAMS) as i:
                both(lambda s, n: dve_normalize(dve, "ff", s, n, row(n, x3), bufs[s].xn), i + 1)
                both(lambda s, n: at_dve_qkv(dve, "ff", s, n, None), i + 1)
                both(lambda s, n: dve_softmax_shift(dve, "ff_scores", "ff", s, n, score_view(s), 4, GROUPS, P), i + 1)
                both(lambda s, n: at_dve_probs(dve, "ff", s, n), i + 1)
                both(lambda s, n: dve_softmax_norm(dve, "ff", s, n), i + 1)

                def ff_out(s, n):
                    residual("ff", s, n, row(n, x3), const("ff_pb"))
                    dve.wait_ge(*after("ff_h", n))
                    dve_stats(dve, "n3", s, n, row(n, x3))
                    nc.vector.tensor_tensor(row(n), row(n), bufs[s].t1, ALU.add).then_inc(sem("ff_sum"), 1)
                both(ff_out, i + 1)
            rstd_all("n3")
            with dve.Fori(0, B - STREAMS + 1, STREAMS) as i:
                both(lambda s, n: dve_normalize(dve, "ff2", s, n, row(n, x3), bufs[s].xn), i + 1)

                def feat_rest(s, n):
                    dve.wait_ge(sem("ff_feat_hi"), n)
                    last = nc.vector.tensor_tensor(feat_lo[:, :, bass.ds((n - 1) * P, P)], bufs[s].xT[:, :, 0:P],
                                                   feat_hi[:, :, bass.ds((n - 1) * P, P)], ALU.subtract)
                    last.then_inc(sem("ff_feat_lo"), 1)
                both(feat_rest, i + 1)

                def take_logits(s, n):
                    dve.wait_ge(*after("ff_logits", n))
                    nc.vector.tensor_tensor(logits[:, bass.ds(i + s, 1), :].rearrange("p o c -> p (o c)"),
                                            ps[s][:, 1, 0:EXPERTS], const("gate_b"), ALU.add).then_inc(
                                                sem("ff_logits_kept"), 1)
                both(take_logits, i + 1)

            dve.wait_ge(sem("ff_logits_kept"), B)
            dve.wait_ge(sem("ff_sum"), B)
            for t in range(B):
                ins = nc.vector.max(top8[:, t, :], logits[:, t, :])
            link(ins)
            for t in range(B):
                ins = nc.vector.max_index(idx8[:, t, :], top8[:, t, :], logits[:, t, :])
            link(ins)
            link(nc.vector.tensor_copy(gidx[:, :, :], idx8[:, :, 0:2]))
            link(nc.vector.tensor_tensor(gw[:, :, 0:1], top8[:, :, 1:2], top8[:, :, 0:1], ALU.subtract))
            nc.vector.tensor_copy(gw[:, :, 3:4], gw[:, :, 0:1]).then_inc(sem("moe_gap"), 1)
            dve.wait_ge(sem("moe_gapexp"), 1)
            link(nc.vector.tensor_scalar(gw[:, :, 2:3], gw[:, :, 1:2], 1.0, None, ALU.add))
            link(nc.vector.reciprocal(gw[:, :, 2:3], gw[:, :, 2:3]))
            link(nc.vector.tensor_tensor(gw[:, :, 1:2], gw[:, :, 1:2], gw[:, :, 2:3], ALU.mult))
            ia = iota8[:, :].unsqueeze(1).to_broadcast([P, B, EXPERTS])
            link(nc.vector.tensor_tensor(cw[:, :, :], ia, gidx[:, :, 0:1].to_broadcast([P, B, EXPERTS]), ALU.is_equal))
            link(nc.vector.tensor_tensor(logits[:, :, :], ia, gidx[:, :, 1:2].to_broadcast([P, B, EXPERTS]),
                                         ALU.is_equal))
            link(nc.vector.tensor_tensor(cw[:, :, :], cw[:, :, :], gw[:, :, 2:3].to_broadcast([P, B, EXPERTS]),
                                         ALU.mult))
            link(nc.vector.tensor_tensor(logits[:, :, :], logits[:, :, :],
                                         gw[:, :, 1:2].to_broadcast([P, B, EXPERTS]), ALU.mult))
            nc.vector.tensor_tensor(cw[:, :, :], cw[:, :, :], logits[:, :, :], ALU.add).then_inc(sem("moe_cw"), 1)
            dve.wait_ge(sem("moe_cw"), 1)

            with dve.Fori(0, B - STREAMS + 1, STREAMS) as i:
                def cw_copy(s, n):
                    nc.vector.tensor_copy(bufs[s].xn[:, 0:EXPERTS],
                                          cw[:, bass.ds(i + s, 1), :].rearrange("p o c -> p (o c)")).then_inc(
                                              sem("moe_cw_copy"), 1)
                both(cw_copy, i + 1)

                def add_bias2(s, n):
                    dve.wait_ge(*after("moe_bias2", n))
                    nc.vector.tensor_tensor(row(n), row(n), ps[s][:, 1, 0:C], ALU.add).then_inc(
                        sem("moe_b2_added"), 1)
                both(add_bias2, i + 1)
            dve.wait_ge(sem("moe_b2_added"), B)
            nc.vector.memset(small[:, 0:1], 0.0).then_inc(sem("moe_gelu"), 4)
            nc.vector.memset(small[:, 1:2], 0.0).then_inc(sem("moe_added"), 4)
            nc.vector.memset(small[:, 2:3], 0.0).then_inc(sem("moe_out"), 8)
            nc.vector.memset(small[:, 4:5], 0.0).then_inc(sem("moe_he_lo"), HT)
            nc.vector.memset(small[:, 3:4], 0.0).then_inc(sem("moe_start"), 1)

            def split_weights(k, n):
                dve.wait_ge(sem("moe_w_hi"), n)
                nc.vector.tensor_tensor(w1_parts[k][1], ew1[k], w1_parts[k][0], ALU.subtract)
                nc.vector.tensor_tensor(w2_parts[k][1], ew2[k], w2_parts[k][0], ALU.subtract).then_inc(
                    sem("moe_w_lo"), 1)
            split_weights(0, 1)

            def add_outputs(e, k, g):
                for t in range(4 * g, 4 * g + 4):
                    dve.wait_ge(sem("moe_out"), e * B + k * B + t + 1 + 8)
                    nc.vector.scalar_tensor_tensor(
                        out=hs[:, t, :], in0=ps[1][:, t % 4, 0:C], scalar=cwcur[:, k, t:t + 1],
                        in1=hs[:, t, :], op0=ALU.mult, op1=ALU.add).then_inc(sem("moe_added"), 1)

            def expert(e, k, more):
                nc.vector.tensor_copy(cwcur[:, k, :].unsqueeze(2), cw[:, :, bass.ds(e + k, 1)]).then_inc(
                    sem("moe_cwcur"), 1)
                dve.wait_ge(sem("moe_cwcur"), e + k + 1)
                for g in range(NG):
                    for m in range(HT):
                        dve.wait_ge(sem("moe_gelu"), e * (NG * HT) + k * NG * HT + g * HT + m + 1 + 4)
                        nc.vector.tensor_tensor(he_lo[g % 2][:, m, :], he[:, m, :], he_hi[g % 2][:, m, :],
                                                ALU.subtract).then_inc(sem("moe_he_lo"), 1)
                    if g == 1 and more:
                        split_weights(1 - k, e + k + 2)
                    if g > 0:
                        add_outputs(e, k, g - 1)
                add_outputs(e, k, NG - 1)
            experts(dve, expert)
            dve.wait_ge(sem("moe_added"), EXPERTS * B + 4)
            for s in range(STREAMS):
                nc.vector.memset(bufs[s].qk_pad, 0.0)
                nc.vector.memset(bufs[s].v_ext[:, 0:HEADS, :], 1.0)
            for t in range(B):
                nc.vector.bn_stats(allstats[:, t, :], hs[:, t, :]).then_inc(sem("n4_mv"), 1)
            rstd_all("n4")


            def q_squares(s, n):
                b = bufs[s]
                q, q2 = b.p[:, 0:C], b.p[:, C:2 * C]
                dve.wait_ge(*after("l1_q", n))
                nc.vector.tensor_copy(q, ps[s][:, 2, 0:C]).then_inc(sem("l1_qcopy"), 1)
                dve.wait_ge(*after("l1_qcopy", n))
                nc.vector.tensor_tensor(q2, q, q, ALU.mult).then_inc(sem("l1_squares"), 1)
                dve.wait_ge(*after("l1_squares", n))
                nc.vector.tensor_reduce(b.n2, q2.rearrange("p (h d) -> p h d", d=HD), X,
                                        ALU.add).then_inc(sem("l1_norm2"), 1)
                dve.wait_ge(*after("l1_norm2", n))

            def q_newton(s, n, lo, hi):
                b = bufs[s]
                for k, step in enumerate(rsqrt_steps(b.stats12, b.n2, b.nt)):
                    if lo <= k < hi:
                        step().then_inc(sem("l1_newton"), 1)
                        dve.wait_ge(sem("l1_newton"), n * 10 + (k + 1 - 10))

            def q_unit(s, n):
                b = bufs[s]
                length = b.stats12
                nc.vector.tensor_tensor(length, length, b.n2, ALU.mult).then_inc(sem("l1_root"), 1)
                dve.wait_ge(*after("l1_root", n))
                nc.vector.tensor_scalar(length, length, Q_EPS, None, ALU.add).then_inc(sem("l1_norm"), 1)
                dve.wait_ge(*after("l1_norm", n))
                nc.vector.reciprocal(length, length).then_inc(sem("l1_rnorm"), 1)
                dve.wait_ge(*after("l1_rnorm", n))
                nc.vector.tensor_tensor(b.qk_pad[:, 0:HEADS, 0:HD], b.p[:, 0:C].rearrange("p (h d) -> p h d", d=HD),
                                        length.unsqueeze(2).to_broadcast([P, HEADS, HD]),
                                        ALU.mult).then_inc(sem("l1_pad"), 1)
                nc.vector.memset(b.x_parts[:, :, 0:1], 1.0)
                nc.vector.memset(b.x_parts[:, :, 1:2], 0.0)

            def take_v(s, n):
                dve.wait_ge(*after("l1_v", n))
                nc.vector.tensor_copy(bufs[s].v_ext[:, 0:HEADS, 0:HD],
                                      ps[s][:, 1, C:2 * C].rearrange("p (h d) -> p h d", d=HD)).then_inc(
                                          sem("l1_vcopy"), 1)
                dve.wait_ge(*after("l1_vcopy", n))
                dve_split_v(dve, "l1", s, n)

            def kernel_lo(s, n, k):
                b = bufs[s]
                cols = slice(BANK_ORDER[k] * GROUPS * P, (BANK_ORDER[k] + 1) * GROUPS * P)
                dve.wait_ge(sem("l1_kernel"), n * 4 + (k + 1 - 4))
                last = nc.vector.tensor_tensor(b.lo[:, cols], b.p[:, cols], b.hi[:, cols], ALU.subtract)
                if k == 3:
                    last.then_inc(sem("l1_kernel_lo"), 1)

            HALF = HEADS // 2 * P

            def rescale(s, n, it):
                b = bufs[s]
                x = b.rec if it % 2 == 0 else b.mx
                dve.wait_ge(sem("l1_sums"), half_steps(n, it))
                nc.vector.tensor_reduce(b.n2, ps[s][:, 3, SUMS:SUMS + 2 * HEADS].rearrange(
                    "p (h k) -> p h k", k=2), X, ALU.add).then_inc(sem("l1_summed"), 1)
                dve.wait_ge(sem("l1_summed"), half_steps(n, it))
                if it < 2 * SINKHORN_ITERS - 1:
                    with nc.allow_low_precision(reason="the second part holds what this one leaves"):
                        nc.vector.reciprocal(b.x_parts[:, :, 0], b.n2)
                nc.vector.reciprocal(x, b.n2).then_inc(sem("l1_scaled"), 1)
                dve.wait_ge(sem("l1_scaled"), half_steps(n, it))
                if it < 2 * SINKHORN_ITERS - 1:
                    nc.vector.tensor_tensor(b.x_parts[:, :, 1], x, b.x_parts[:, :, 0],
                                            ALU.subtract).then_inc(sem("l1_xlo"), 1)

            def split_u(s, n):
                b = bufs[s]
                nc.vector.tensor_copy(b.u_parts[:, 0:HEADS], b.rec).then_inc(sem("l1_u0"), 1)
                dve.wait_ge(*after("l1_u0", n))
                nc.vector.tensor_tensor(b.nt, b.rec, b.u_parts[:, 0:HEADS], ALU.subtract).then_inc(
                    sem("l1_ur"), 1)
                dve.wait_ge(*after("l1_ur", n))
                nc.vector.tensor_copy(b.u_parts[:, HEADS:2 * HEADS], b.nt).then_inc(sem("l1_u1"), 1)
                dve.wait_ge(*after("l1_u1", n))
                nc.vector.tensor_tensor(b.u_parts[:, 2 * HEADS:3 * HEADS], b.nt, b.u_parts[:, HEADS:2 * HEADS],
                                        ALU.subtract).then_inc(sem("l1_uparts"), 1)

            def transport(s, n, half):
                b = bufs[s]
                cols = slice(8 * P * half, (8 + 4 * half) * P)
                dve.wait_ge(*after("l1_urows", 2 * n + (half - 1)))
                nc.vector.tensor_tensor(b.pT[:, cols], b.p[:, cols],
                                        ps[s][:, 0:3, :].rearrange("p b n -> p (b n)")[:, cols],
                                        ALU.mult).then_inc(sem("l1_ku"), 1)

            def row_max(s, n, half):
                b = bufs[s]
                dve.wait_ge(*after("l1_ku", 2 * n + (half - 1)))
                nc.vector.tensor_reduce(b.stats12[:, 6 * half:6 * half + 6],
                                        b.pT[:, half * HALF:(half + 1) * HALF].rearrange("p (h n) -> p h n", n=P),
                                        X, ALU.max).then_inc(sem("l1_kumax"), 1)
                if half == 1:
                    dve.wait_ge(*after("l1_kumax", 2 * n))
                    nc.vector.tensor_tensor(b.stats12, b.stats12, b.mx, ALU.mult).then_inc(sem("l1_rowmax"), 1)

            def head_max(s, n):
                b = bufs[s]
                dve.wait_ge(*after("l1_maxturned", n))
                nc.vector.tensor_reduce(b.stats[0:HEADS, 0:1], ps[s][0:HEADS, 3, 0:P], X,
                                        ALU.max).then_inc(sem("l1_headmax"), 1)
                dve.wait_ge(*after("l1_headmax", n))
                nc.vector.reciprocal(b.stats[0:HEADS, 1:2], b.stats[0:HEADS, 0:1]).then_inc(
                    sem("l1_headrec"), 1)
                dve.wait_ge(*after("l1_headrec", n))
                nc.vector.tensor_scalar(b.maxdiag, ident[0:HEADS, 0:HEADS], b.stats[0:HEADS, 1:2], SCALE,
                                        ALU.mult, ALU.mult).then_inc(sem("l1_maxdiag"), 1)

            def z_rows(s, n):
                dve.wait_ge(*after("l1_maxspread", n))
                nc.vector.tensor_tensor(bufs[s].sv, bufs[s].mx, ps[s][:, 3, P:P + HEADS], ALU.mult).then_inc(
                    sem("l1_sv"), 1)
                dve.wait_ge(*after("l1_sv", n))

            def scaled_z(s, n, half):
                b = bufs[s]
                z = b.pT[:, half * HALF:(half + 1) * HALF].rearrange("p (h n) -> p h n", n=P)
                last = nc.vector.tensor_tensor(
                    z, z, b.sv[:, 6 * half:6 * half + 6].unsqueeze(2).to_broadcast([P, 6, P]), ALU.mult)
                if half == 1:
                    last.then_inc(sem("l1_z"), 1)

            def probs_lo(s, n, half):
                b = bufs[s]
                cols = slice(half * HALF, (half + 1) * HALF)
                if half == 0:
                    dve.wait_ge(*after("l1_probs", n))
                last = nc.vector.tensor_tensor(b.lo[:, cols], b.pT[:, cols], b.hi[:, cols], ALU.subtract)
                if half == 1:
                    last.then_inc(sem("l1_probs_lo"), 1)

            def l1_out(s, n):
                residual("l1", s, n, row(n), const("l1_pb"))
                dve.wait_ge(*after("l1_h", n))
                dve_stats(dve, "n5", s, n, row(n))

            def l1_stage(post, half, pre):
                for it in range(2 * SINKHORN_ITERS):
                    if half:
                        rescale(*half, it)
                    if post:
                        if it == 0:
                            split_u(*post)
                        if it in (2, 3):
                            transport(*post, it - 2)
                        if it in (4, 5):
                            row_max(*post, it - 4)
                        if it == 6:
                            head_max(*post)
                        if it == 7:
                            z_rows(*post)
                        if it in (7, 8):
                            scaled_z(*post, it - 7)
                        if it in (10, 11):
                            probs_lo(*post, it - 10)
                        if it == 12:
                            dve_softmax_norm(dve, "l1", *post)
                        if it == 15:
                            l1_out(*post)
                    if pre:
                        if it == 3:
                            dve_normalize(dve, "l1", *pre, row(pre[1]), bufs[pre[0]].xn)
                        if it == 6:
                            q_squares(*pre)
                        if it in (7, 8):
                            q_newton(*pre, it - 7, it - 6)
                        if it == 9:
                            q_newton(*pre, 2, 6)
                        if it in (10, 11):
                            q_newton(*pre, 2 * it - 14, 2 * it - 12)
                        if it == 12:
                            q_unit(*pre)
                        if it == 13:
                            take_v(*pre)
                        if it == 17:
                            kernel_lo(*pre, 0)
                        if it == 18:
                            kernel_lo(*pre, 1)
                        if it == 19:
                            kernel_lo(*pre, 2)
                            kernel_lo(*pre, 3)
            sinkhorn_stages(dve, l1_stage)
            rstd_all("n5")
            with dve.Fori(0, B - STREAMS + 1, STREAMS) as i:
                both(lambda s, n: dve_normalize(dve, "q", s, n, row(n), bufs[s].xn), i + 1)
                dve.wait_ge(sem("q_featT"), i + STREAMS)

            dve.wait_ge(sem("q_featT"), B)
            A96 = slice(0, HC)
            hi2, lo2, abs2 = small[A96, 0:2], small[A96, 2:4], small[A96, 4:6]
            wm2, cs2, pw2, up2 = small[A96, 6:8], small[A96, 8:10], small[A96, 10:12], small[A96, 12:14]
            rc2 = small[A96, 16:18]
            w1n = const("q_w1").rearrange("p (m n) -> p m n", m=HT)
            w2n = const("q_w2").rearrange("p (c n) -> p c n", c=2)

            def absmax(dst, src):
                return nc.vector.tensor_reduce(dst, src, X, ALU.max, apply_absolute_value=True)

            nc.vector.tensor_reduce(wmax, w1n.rearrange("p m n -> p n m"), X, ALU.max,
                                    apply_absolute_value=True).then_inc(sem("q_wmax"), 1)
            nc.vector.tensor_reduce(hi2, featT[:, :, :], X, ALU.max)
            link(nc.vector.tensor_reduce(lo2, featT[:, :, :], X, ALU.min))
            link(nc.vector.tensor_scalar(lo2, lo2, -1.0, None, ALU.mult))
            link(nc.vector.tensor_tensor(abs2, hi2, lo2, ALU.max))
            dve.wait_ge(sem("q_wmaxturned"), 1)
            link(nc.vector.tensor_reduce(wm2, ps[0][A96, 3, 0:2 * P].rearrange("p (c n) -> p c n", c=2), X, ALU.max))
            link(nc.vector.reciprocal(wm2, wm2))
            link(nc.vector.tensor_tensor(wm2, abs2, wm2, ALU.mult))
            for step in rsqrt_steps(abs2, wm2, pw2):
                link(step())
            link(nc.vector.tensor_tensor(abs2, abs2, wm2, ALU.mult))
            link(nc.vector.tensor_scalar(pw2.bitcast(I32), abs2.bitcast(I32), 0x7F800000, None, ALU.bitwise_and))
            link(nc.vector.tensor_scalar(up2, pw2, 1.5, None, ALU.mult))
            link(nc.vector.tensor_tensor(up2, abs2, up2, ALU.is_gt))
            link(nc.vector.tensor_scalar(up2, up2, 1.0, None, ALU.add))
            link(nc.vector.tensor_tensor(cs2, pw2, up2, ALU.mult))
            for c in range(2):
                last = nc.vector.tensor_scalar(csb[:, c, :], ones[A96, :], cs2[:, c:c + 1], None, ALU.mult)
            last.then_inc(sem("q_cs_rows"), 1)
            link(nc.vector.reciprocal(rc2, cs2))
            nc.vector.tensor_tensor(hi2, hi2, rc2, ALU.mult)
            link(nc.vector.tensor_tensor(lo2, lo2, rc2, ALU.mult))
            nc.vector.tensor_tensor(small[A96, 20:21], hi2[:, 0:1], hi2[:, 1:2], ALU.max)
            nc.vector.tensor_tensor(small[A96, 21:22], lo2[:, 0:1], lo2[:, 1:2], ALU.max).then_inc(
                sem("q_range"), 1)

            def quant_range(pre, rows, at):
                dve.wait_ge(sem(f"{pre}turned"), 1)
                link(nc.vector.tensor_reduce(small[0:2, at:at + 1], ps[0][0:2, 1, 0:rows], X, ALU.max))
                link(nc.vector.tensor_scalar(small[0:2, at:at + 1], small[0:2, at:at + 1], 0.0, None, ALU.max))
                nc.vector.tensor_scalar(small[0:2, at + 1:at + 3], ident[0:2, 0:2], small[0:2, at:at + 1], None,
                                        ALU.mult).then_inc(sem(f"{pre}diag"), 1)
                dve.wait_ge(sem(f"{pre}spread"), 1)
                link(nc.vector.tensor_copy(small[:, at + 8:at + 10], ps[0][:, 2, 0:2]))
                sc, lo, hi, rs = (small[:, at + k:at + k + 1] for k in (4, 5, 6, 10))
                link(nc.vector.tensor_tensor(sc, small[:, at + 8:at + 9], small[:, at + 9:at + 10], ALU.add))
                link(nc.vector.tensor_scalar(sc, sc, 1.0 / 255.0, 1e-8, ALU.mult, ALU.max))
                link(nc.vector.reciprocal(rs, sc))
                link(nc.vector.tensor_scalar(lo, small[:, at + 9:at + 10], rs, ROUND, ALU.mult, ALU.add))
                link(nc.vector.tensor_scalar(lo, lo, ROUND, -1.0, ALU.subtract, ALU.mult))
                link(nc.vector.tensor_scalar(hi, lo, 255.0, None, ALU.add))
                return sc, lo, hi, rs

            sx, xlo, xhi, rsx = quant_range("q_range", HC, 23)
            for c in range(2):
                link(nc.vector.tensor_scalar(featT[:, c, :], featT[:, c, :], rc2[:, c:c + 1], rsx[A96],
                                             ALU.mult, ALU.mult))
                link(nc.vector.tensor_scalar(featT[:, c, :], featT[:, c, :], ROUND, ROUND, ALU.add, ALU.subtract))
                last = nc.vector.tensor_scalar(xq[:, c, :], featT[:, c, :], xlo[A96], xhi[A96], ALU.max, ALU.min)
            last.then_inc(sem("q_xq"), 1)

            s1, s2 = small[:, 54:60], small[A96, 60:62]
            dve.wait_ge(sem("q_csrow"), 1)
            link(nc.vector.tensor_tensor(w1_s, w1n, ps[0][:, 0, 0:C].unsqueeze(1).to_broadcast([P, HT, C]), ALU.mult))
            absmax(s1, w1_s)
            link(absmax(s2, w2n))
            r1, r2 = small[:, 86:92], small[A96, 92:94]
            nc.vector.tensor_scalar(s1, s1, 1.0 / 127.0, 1e-8, ALU.mult, ALU.max)
            link(nc.vector.tensor_scalar(s2, s2, 1.0 / 127.0, 1e-8, ALU.mult, ALU.max))
            nc.vector.reciprocal(r1, s1)
            link(nc.vector.reciprocal(r2, s2))
            nc.vector.tensor_tensor(w1_s, w1_s, r1.unsqueeze(2).to_broadcast([P, HT, C]), ALU.mult)
            link(nc.vector.tensor_tensor(w2n, w2n, r2.unsqueeze(2).to_broadcast([HC, 2, HIDDEN]), ALU.mult))
            nc.vector.tensor_scalar(w1_s, w1_s, ROUND, ROUND, ALU.add, ALU.subtract)
            link(nc.vector.tensor_scalar(w2n, w2n, ROUND, ROUND, ALU.add, ALU.subtract))
            nc.vector.tensor_scalar(w1_q, w1_s, -128.0, 127.0, ALU.max, ALU.min)
            nc.vector.tensor_scalar(w2_q, w2n, -128.0, 127.0, ALU.max, ALU.min)
            for c in range(2):
                last = nc.vector.tensor_scalar(sw2b[:, c, :], ones[A96, :], s2[:, c:c + 1], None, ALU.mult)
            last.then_inc(sem("q_w_quant"), 1)
            nc.vector.tensor_scalar(small[:, 48:54], s1, sx, None, ALU.mult).then_inc(sem("q_hidden_scale"), 1)
            dve.wait_ge(sem("q_wturned"), 1)
            tb = ps[1][:, :, :].rearrange("p b n -> p (b n)").bitcast(BF16).rearrange("p (b n) -> p b n", b=4)
            nc.vector.tensor_copy(wq1T, tb[0:HC, 0:2, 0:HIDDEN])
            nc.vector.tensor_copy(wq2T.rearrange("p (b m) n -> p b (m n)", b=2), tb[:, 2:4, 0:3 * C]).then_inc(
                sem("q_wT"), 1)
            dve.wait_ge(sem("q_sw2row"), 1)
            nc.vector.tensor_copy(sw2row[:, :], ps[0][:, 3, 0:C]).then_inc(sem("q_sw2"), 1)

            for g in range(NG):
                dve.wait_ge(sem("q_gelu"), (g + 1) * HT)
                ins = nc.vector.tensor_reduce(small[:, 64 + g:65 + g], gelu_out[:, :, g * TG:(g + 1) * TG],
                                              mybir.AxisListType.XY, ALU.max, apply_absolute_value=True)
            link(ins)
            nc.vector.tensor_reduce(small[:, 30:31], small[:, 64:64 + NG], X, ALU.max).then_inc(sem("q_hmax"), 1)
            dve.wait_ge(sem("q_hmaxturned"), 1)
            nc.vector.tensor_reduce(small[0:1, 31:32], ps[0][0:1, 0, 0:P], X, ALU.max).then_inc(sem("q_hmaxone"), 1)
            dve.wait_ge(sem("q_hmaxspread"), 1)
            sh = small[:, 70:71]
            rsh = small[:, 71:72]
            link(nc.vector.tensor_scalar(sh, ps[0][:, 1, 0:1], 1.0 / 127.0, 1e-8, ALU.mult, ALU.max))
            link(nc.vector.reciprocal(rsh, sh))
            nc.vector.tensor_scalar(sw2row[:, :], sw2row[:, :], sh, None, ALU.mult).then_inc(sem("q_hscale"), 1)
            for g in range(NG):
                part = gelu_out[:, :, g * TG:(g + 1) * TG]
                link(nc.vector.tensor_scalar(part, part, rsh, ROUND, ALU.mult, ALU.add))
                nc.vector.tensor_scalar(hqs[g], part, ROUND, 127.0, ALU.subtract, ALU.min).then_inc(sem("q_hq"), 1)
            for t in range(B):
                dve.wait_ge(sem("q_down"), t + 1)
                nc.vector.tensor_tensor(oq[:, t, :], ps[t % 8 // 4][:, t % 4, 0:C], sw2row[:, :],
                                        ALU.mult).then_inc(sem("q_down_read"), 1)
            dve.wait_ge(sem("q_down_read"), B)
            link(nc.vector.tensor_tensor(oq, oq, const("q_b2").unsqueeze(1).to_broadcast([P, B, C]), ALU.add))
            nc.vector.tensor_reduce(small[:, 40:41], oq, mybir.AxisListType.XY, ALU.max)
            link(nc.vector.tensor_reduce(small[:, 42:43], oq, mybir.AxisListType.XY, ALU.min))
            nc.vector.tensor_scalar(small[:, 41:42], small[:, 42:43], -1.0, None, ALU.mult).then_inc(
                sem("q_orange"), 1)
            so, olo, ohi, rso = quant_range("q_orange", P, 75)
            link(nc.vector.tensor_scalar(oq, oq, rso, ROUND, ALU.mult, ALU.add))
            link(nc.vector.tensor_scalar(oq, oq, ROUND, olo, ALU.subtract, ALU.max))
            link(nc.vector.tensor_scalar(oq, oq, ohi, so, ALU.min, ALU.mult))
            nc.vector.tensor_tensor(hs[:, :, :], hs[:, :, :], oq, ALU.add).then_inc(sem("result"), 1)


def kernel(**inputs):
    import concourse.bacc as bacc
    from concourse.bass_utils import run_bass_kernel_spmd

    a = {k: np.asarray(v) for k, v in inputs.items()}

    def chunked(w):
        return w.reshape(2, HC, -1).transpose(1, 0, 2).reshape(HC, -1)

    def rows(v):
        return np.broadcast_to(v.reshape(1, -1), (P, v.size))

    parts = {
        "tok_w": chunked(a["L0_tok_w_qkv"].T), "tok_b": rows(a["L0_tok_b_qkv"]),
        "tok_pw": chunked(a["L0_tok_w_proj"].T), "tok_pb": rows(a["L0_tok_b_proj"]),
        "at_w": chunked(a["L0_attn_qkv_w"].T), "at_b": rows(a["L0_attn_qkv_b"]),
        "at_pw": chunked(a["L0_attn_proj_w"].T), "at_pb": rows(a["L0_attn_proj_b"]),
        "ff_w": chunked(a["L0_ffn_qkv_w"]), "ff_pw": chunked(a["L0_ffn_proj_w"]), "ff_pb": rows(a["L0_ffn_proj_b"]),
        "ln1_g": chunked(a["L0_ffn_ln1_g"]), "ln1_b": chunked(a["L0_ffn_ln1_b"]),
        "ln2_g": chunked(a["L0_ffn_ln2_g"]), "ln2_b": chunked(a["L0_ffn_ln2_b"]),
        "gate_w": chunked(a["L0_ffn_gate_w"]), "gate_b": rows(a["L0_ffn_gate_b"]),
        "b1": a["L0_ffn_b1"].reshape(EXPERTS, HT, P).transpose(2, 0, 1).reshape(P, -1), "b2": a["L0_ffn_b2"],
        "l1_w": chunked(a["L1_attn_w_qkv"].T), "l1_pw": chunked(a["L1_attn_w_proj"].T),
        "l1_pb": rows(a["L1_attn_b_proj"]),
        "q_b1": a["L1_ffn_b1"].reshape(HT, P).T, "q_b2": rows(a["L1_ffn_b2"]),
        "q_w1": a["L1_ffn_w1"].reshape(HT, P, C).transpose(1, 0, 2).reshape(P, -1),
        "q_w2": a["L1_ffn_w2"].reshape(2, HC, HIDDEN).transpose(1, 0, 2).reshape(HC, -1),
    }
    packed = np.zeros((P, PACKED), np.float32)
    for name, (at, n, cols) in OFFSET.items():
        packed[0:n, at:at + cols] = parts[name]
    x = a["x"].reshape(B, STRIDE, WQ, WINDOWS, 2, HC).transpose(0, 5, 4, 3, 2, 1).reshape(B, HC, 2, N_IN)
    w1 = a["L0_ffn_w1"].reshape(EXPERTS, 2, HC, HIDDEN).transpose(0, 2, 1, 3)
    w2 = a["L0_ffn_w2"].reshape(EXPERTS, HT, P, C).transpose(0, 2, 1, 3)

    nc = bacc.Bacc("TRN2", target_bir_lowering=False, num_devices=1)
    arrays = {"x_dram": x, "packed_dram": packed, "w1_dram": w1, "w2_dram": w2}
    arrays = {k: np.ascontiguousarray(v) for k, v in arrays.items()}
    args = [nc.dram_tensor(k, v.shape, F32, kind="ExternalInput").ap() for k, v in arrays.items()]
    out = nc.dram_tensor("out_dram", (B, P, C), F32, kind="ExternalOutput").ap()
    build(nc, *args, out)
    r = run_bass_kernel_spmd(nc, [arrays], core_ids=[0])
    return r.results[0]["out_dram"]
```

```python
from contextlib import ExitStack

import numpy as np

import concourse.bass as bass
from concourse import mybir
from concourse.alu_op_type import AluOpType as ALU

ACT = mybir.ActivationFunctionType
F32 = mybir.dt.float32
BF16 = mybir.dt.bfloat16
I32 = mybir.dt.int32
U32 = mybir.dt.uint32
X = mybir.AxisListType.X

P = 128
B = 16
N_IN = 512
C = 192
HEADS = 12
HD = C // HEADS
STRIDE = 4
WINDOWS = 2
WQ = 64
HC = C // 2
GROUPS = 3
EXPERTS = 8
HIDDEN = 768
HT = HIDDEN // P
T = B * P
TG = 512
NG = T // TG
LN_EPS = 1e-5
SCALE = float(HD) ** -0.5
OT_REG = 0.1
SINKHORN_ITERS = 10
DIAG_VAL = 1000.0
Q_EPS = 1e-8
ROUND = 12582912.0
STREAMS = 2

SHARED = {
    **{k: [("n0", "n1", "n3", "n5")] for k in ("stats", "kept")},
    "mv": [("n0", "n1", "n2", "n3", "n4", "n5")],
    **{k: [("at", "ff", "l1")] for k in ("xn", "xturned", "xT")},
    **{k: [("at", "ff")] for k in ("qkv", "pad", "qkturned", "qkT")},
    **{k: [("tok1", "at", "ff")] for k in ("scores", "max", "shifted", "pturned")},
    **{k: [("at", "ff")] for k in ("pT_hi", "pT_lo")},
    "vhi": [("at", "ff", "l1")],
    "probs": [("tok1", "at", "ff", "l1")],
    **{k: [("tok", "at", "ff", "l1")] for k in ("pv", "rec", "on", "oturned", "onT", "proj")},
    **{k: [("at", "ff", "l1")] for k in ("biased", "h")},
}

LAYOUT = [
    ("tok_w", HC, 2 * 3 * C), ("tok_b", P, 3 * C), ("tok_pw", HC, 2 * C), ("tok_pb", P, C),
    ("at_w", HC, 2 * 3 * C), ("at_b", P, 3 * C), ("at_pw", HC, 2 * C), ("at_pb", P, C),
    ("ff_w", HC, 2 * 3 * C), ("ff_pw", HC, 2 * C), ("ff_pb", P, C), ("ln1_g", HC, 2), ("ln1_b", HC, 2),
    ("ln2_g", HC, 2), ("ln2_b", HC, 2), ("gate_w", HC, 2 * EXPERTS), ("gate_b", P, EXPERTS),
    ("b1", P, EXPERTS * HT), ("b2", EXPERTS, C),
    ("l1_w", HC, 2 * 3 * C), ("l1_pw", HC, 2 * C), ("l1_pb", P, C),
    ("q_b1", P, HT), ("q_b2", P, C), ("q_w1", P, HT * C), ("q_w2", HC, 2 * HIDDEN),
]
OFFSET = {}
_at = 0
for _name, _rows, _cols in LAYOUT:
    OFFSET[_name] = (_at, _rows, _cols)
    _at += _cols
PACKED = _at
TOK_CONSTS = OFFSET["at_w"][0]


def build(nc, x, packed, w1, w2, out):
    with ExitStack() as ctx:
        def sb(name, shape, dt=F32):
            return ctx.enter_context(nc.sbuf_tensor(name, shape, dt))

        sems = {}

        def shared(name):
            part, _, stage = name.partition("_")
            parts = SHARED.get(stage, ())
            for group in parts:
                if part in group:
                    return stage + "_" * parts.index(group), group.index(part)
            return name, 0

        def after(name, n):
            return sem(name), n + B * shared(name)[1]

        def sem(name):
            name = shared(name)[0]
            if name not in sems:
                sems[name] = ctx.enter_context(nc.semaphore(name))
            return sems[name]

        ps = [ctx.enter_context(nc.psum_tensor(f"ps{s}", [P, 4, 512], F32)) for s in range(STREAMS)]

        consts = sb("consts", [P, PACKED])

        def const(name):
            at, rows, cols = OFFSET[name]
            return consts[0:rows, at:at + cols]

        def chunks(name):
            return const(name).rearrange("p (c n) -> p c n", c=2)

        ident = sb("ident", [P, P])
        identb = sb("identb", [P, P], BF16)
        diag_off = sb("diag_off", [P, GROUPS, P], BF16)
        diag_one = sb("diag_one", [P, P])
        ones = sb("ones", [P, P])
        pick = sb("pick", [3 * HEADS, HEADS, P], BF16)
        iota8 = sb("iota8", [P, EXPERTS])

        hs = sb("hs", [P, B, C])
        featT = sb("featT", [HC, 2, T])
        logits = sb("logits", [P, B, EXPERTS])
        cw = sb("cw", [P, B, EXPERTS])

        ARENA = 9984
        arena = sb("arena", [P, STREAMS, ARENA])

        ffw = sb("ffw", [P, HT * T // 2])
        ew1 = [ffw[0:HC, k * 2 * HIDDEN:(k + 1) * 2 * HIDDEN].rearrange("p (c n) -> p c n", c=2) for k in range(2)]
        ew2 = [ffw[:, 4 * HIDDEN + k * HT * C:4 * HIDDEN + (k + 1) * HT * C].rearrange("p (m n) -> p m n", m=HT)
               for k in range(2)]
        hqs = [ffw[:, g * HT * TG // 2:(g + 1) * HT * TG // 2].bitcast(BF16).rearrange("p (m n) -> p m n", m=HT)
               for g in range(NG)]
        small = sb("small", [P, 96])
        allstats = sb("allstats", [P, B, 6])
        meanvar = sb("meanvar", [P, B, 2])
        rstd = sb("rstd", [P, B])
        newton = sb("newton", [P, B])
        varp = sb("varp", [P, B])
        x3 = sb("x3", [P, B, C])
        b1cur = sb("b1cur", [P, 2, HT])
        cwcur = sb("cwcur", [P, 2, B])
        neg_reg = sb("neg_reg", [P, 1])
        idx8 = sb("idx8", [P, B, 8], U32)
        top8 = sb("top8", [P, B, 8])
        gidx = sb("gidx", [P, B, 2])
        gw = sb("gw", [P, B, 4])
        sw2row = sb("sw2row", [P, C])
        xq = sb("xq", [HC, 2, T], BF16)

        class Buffers:
            pass

        bufs = []
        for s in range(STREAMS):
            b = Buffers()
            used = [0]

            def take(*dims, rows=P):
                n = int(np.prod(dims))
                v = arena[0:rows, s, used[0]:used[0] + n]
                used[0] += n
                if len(dims) == 2:
                    return v.rearrange("p (a b) -> p a b", a=dims[0])
                if len(dims) == 3:
                    return v.rearrange("p (a b c) -> p a b c", a=dims[0], b=dims[1])
                return v

            b.qk_pad = take(5 * HEADS, 32)
            b.v_ext = take(4 * HEADS, HD + 1)
            b.qT = take(GROUPS, P)
            b.kT = take(GROUPS, STRIDE, P)
            parts = b.kT.rearrange("p g t n -> p (g t n)").bitcast(BF16)
            b.hi, b.lo = parts[:, 0:HEADS * P], parts[:, HEADS * P:2 * HEADS * P]
            spare = b.qk_pad.rearrange("p h d -> p (h d)")[:, 2 * HEADS * 32:5 * HEADS * 32].bitcast(BF16)
            b.v_hi = spare[:, 0:204].rearrange("p (h d) -> p h d", h=HEADS)
            b.v_lo = spare[:, 204:408].rearrange("p (h d) -> p h d", h=HEADS)
            b.x_parts = spare[:, 408:408 + 2 * HEADS].rearrange("p (h k) -> p h k", k=2)
            b.u_parts = spare[:, 440:440 + P]
            b.uT_parts = spare[0:3 * HEADS, 600:600 + P]
            b.p = take(HEADS * P)
            b.pT = take(HEADS * P)
            b.pT_hi = b.pT.bitcast(BF16)[:, 0:HEADS * P]
            b.pT_lo = b.pT.bitcast(BF16)[:, HEADS * P:2 * HEADS * P]
            b.xT = take(2, N_IN, rows=HC)
            b.xn = take(C)
            b.t1 = take(C)
            b.on = take(C)
            b.onT = take(2, P, rows=HC)
            b.stats = take(8)
            b.mx = take(HEADS)
            b.rec = take(HEADS)
            b.nt = take(HEADS)
            b.n2 = take(HEADS)
            b.stats12 = take(HEADS)
            b.maxdiag = take(HEADS, rows=HEADS)
            b.sv = take(HEADS)
            b.length = take(HEADS)
            assert used[0] <= ARENA, used
            bufs.append(b)

        def loaded(eng):
            eng.wait_ge(sem("tok_consts_loaded"), 16)
            eng.wait_ge(sem("masks_ready"), 6)
            eng.wait_ge(sem("pick_ready"), 3)
            eng.wait_ge(sem("pads_ready"), 2 * STREAMS + 1)

        block = ctx.enter_context(nc.Block())


        def dve_stats(dve, part, s, n, keep):
            b = bufs[s]
            nc.vector.bn_stats(b.stats[:, 0:6], b.t1).then_inc(sem(f"{part}_stats"), 1)
            nc.vector.tensor_copy(keep, b.t1).then_inc(sem(f"{part}_kept"), 1)
            dve.wait_ge(*after(f"{part}_stats", n))
            nc.vector.tensor_scalar(allstats[:, bass.ds(n - 1, 1), :].rearrange("p o c -> p (o c)"),
                                    b.stats[:, 0:6], 1.0, None, ALU.mult).then_inc(sem(f"{part}_mv"), 1)

        def rsqrt_steps(y, v, t):
            yield lambda: nc.vector.tensor_scalar(y.bitcast(I32), v.bitcast(I32), -0.5, 1597463007.0,
                                                  ALU.mult, ALU.add)
            for _ in range(3):
                yield lambda: nc.vector.tensor_tensor(t, y, y, ALU.mult)
                yield lambda: nc.vector.scalar_tensor_tensor(out=t, in0=t, scalar=-0.5, in1=v, op0=ALU.mult,
                                                             op1=ALU.mult)
                yield lambda: nc.vector.scalar_tensor_tensor(out=y, in0=t, scalar=1.5, in1=y, op0=ALU.add,
                                                             op1=ALU.mult)

        def dve_normalize(dve, pre, s, n, src, dst):
            nc.vector.tensor_scalar(dst, src, meanvar[:, bass.ds(n - 1, 1), 0:1].rearrange("p o c -> p (o c)"),
                                    rstd[:, bass.ds(n - 1, 1)], ALU.subtract, ALU.mult).then_inc(
                                        sem(f"{pre}_xn"), 1)

        def pe_turn(pe, wait, done, s, n, src, bank, at=0):
            pe.wait_ge(*after(wait, n))
            for c in range(2):
                last = nc.tensor.transpose(ps[s][0:HC, bank, at + c * P:at + (c + 1) * P],
                                           src[:, c * HC:(c + 1) * HC], ident[:, :])
            last.then_inc(sem(done), 1)

        def act_turned(act, wait, done, s, n, dst, bank, gain=None, bias=None, at=0):
            act.wait_ge(*after(wait, n))
            if gain is None:
                nc.scalar.activation(dst, ps[s][0:HC, bank, at:at + 2 * P].rearrange("p (c n) -> p c n", c=2),
                                     ACT.Copy).then_inc(sem(done), 1)
                return
            for c in range(2):
                last = nc.scalar.activation(dst[:, c, :], ps[s][0:HC, bank, c * P:(c + 1) * P], ACT.Identity,
                                            bias=bias[:, c:c + 1], scale=gain[:, c:c + 1])
            last.then_inc(sem(done), 1)

        def at_pe_qkv(pe, pre, s, n, w):
            pe.wait_ge(*after(f"{pre}_xT", n))
            xT = bufs[s].xT
            for c in range(2):
                nc.tensor.matmul(ps[s][:, 0, 0:2 * C], xT[:, c, 0:P], w[:, c, 0:2 * C],
                                 start=(c == 0), stop=(c == 1))
            for c in range(2):
                last = nc.tensor.matmul(ps[s][:, 1, 0:C], xT[:, c, 0:P], w[:, c, 2 * C:3 * C],
                                        start=(c == 0), stop=(c == 1))
            last.then_inc(sem(f"{pre}_qkv"), 1)

        def dve_split_v(dve, pre, s, n):
            b = bufs[s]
            nc.vector.tensor_copy(b.v_hi, b.v_ext[:, 0:HEADS, :]).then_inc(sem(f"{pre}_vhi"), 1)
            dve.wait_ge(*after(f"{pre}_vhi", n))
            nc.vector.tensor_tensor(b.v_lo, b.v_ext[:, 0:HEADS, :], b.v_hi, ALU.subtract)

        def at_dve_qkv(dve, pre, s, n, bias):
            b = bufs[s]
            dve.wait_ge(*after(f"{pre}_qkv", n))
            qk = ps[s][:, 0, 0:2 * C].rearrange("p (h d) -> p h d", d=HD)
            v = ps[s][:, 1, 0:C].rearrange("p (h d) -> p h d", d=HD)
            if bias is None:
                nc.vector.tensor_copy(b.qk_pad[:, 0:2 * HEADS, 0:HD], qk)
                last = nc.vector.tensor_copy(b.v_ext[:, 0:HEADS, 0:HD], v)
            else:
                bv = bias.rearrange("p (h d) -> p h d", d=HD)
                nc.vector.tensor_tensor(b.qk_pad[:, 0:2 * HEADS, 0:HD], qk, bv[:, 0:2 * HEADS, :], ALU.add)
                last = nc.vector.tensor_tensor(b.v_ext[:, 0:HEADS, 0:HD], v, bv[:, 2 * HEADS:, :], ALU.add)
            last.then_inc(sem(f"{pre}_pad"), 1)
            dve.wait_ge(*after(f"{pre}_pad", n))
            dve_split_v(dve, pre, s, n)

        def at_pe_turn_qk(pe, pre, s, n):
            pe.wait_ge(*after(f"{pre}_pad", n))
            b = bufs[s]
            for g in range(2 * GROUPS):
                last = nc.tensor.transpose(ps[s][:, g // 4, (g % 4) * P:(g % 4 + 1) * P],
                                           b.qk_pad[:, 4 * g:4 * g + 4, :], ident[:, :])
            last.then_inc(sem(f"{pre}_qkturned"), 1)

        def at_act_qk(act, pre, s, n):
            b = bufs[s]
            act.wait_ge(*after(f"{pre}_qkturned", n))
            flat = ps[s][:, 0:2, :].rearrange("p b n -> p (b n)")
            nc.scalar.activation(b.kT[:, :, 0, :], flat[:, GROUPS * P:2 * GROUPS * P].rearrange(
                "p (g n) -> p g n", g=GROUPS), ACT.Copy)
            nc.scalar.activation(b.qT, flat[:, 0:GROUPS * P].rearrange("p (g n) -> p g n", g=GROUPS),
                                 ACT.Copy).then_inc(sem(f"{pre}_qkT"), 1)

        HEAD_ORDER = [g * 4 + j for g in range(GROUPS) for j in range(4)]

        SUMS = 400
        BANK_ORDER = (0, 2, 3, 1)
        TOK_PV = 300

        def place(h):
            return (h % 4) * GROUPS + h // 4

        def score_view(s):
            return ps[s][:, :, 0:GROUPS * P].rearrange("p j (g k) -> p j g k", g=GROUPS)

        def at_pe_scores(pe, pre, s, n):
            b = bufs[s]
            pe.wait_ge(*after(f"{pre}_qkT", n))
            for h in HEAD_ORDER:
                g, r = h // 4, 32 * (h % 4)
                last = nc.tensor.matmul(ps[s][:, h % 4, g * P:(g + 1) * P], b.qT[r:r + HD, g, :],
                                        b.kT[r:r + HD, g, 0, :], start=True, stop=True)
            last.then_inc(sem(f"{pre}_scores"), 1)

        def dve_softmax_shift(dve, wait, pre, s, n, sc, a, g, keys):
            b = bufs[s]
            dve.wait_ge(*after(wait, n))
            for k in range(a):
                last = nc.vector.tensor_reduce(b.mx[:, k * g:(k + 1) * g], sc[:, k], X, ALU.max)
            last.then_inc(sem(f"{pre}_max"), 1)
            dve.wait_ge(*after(f"{pre}_max", n))
            p4 = b.p.rearrange("p (a g k) -> p a g k", a=a, g=g)
            for k in range(a):
                last = nc.vector.tensor_tensor(p4[:, k], sc[:, k],
                                               b.mx[:, k * g:(k + 1) * g].unsqueeze(2).to_broadcast([P, g, keys]),
                                               ALU.subtract)
            last.then_inc(sem(f"{pre}_shifted"), 1)

        def act_exp(act, pre, s, n):
            act.wait_ge(*after(f"{pre}_shifted", n))
            nc.scalar.activation(bufs[s].p, bufs[s].p, ACT.Exp, scale=SCALE).then_inc(sem(f"{pre}_probs"), 1)

        def pe_turn_probs(pe, pre, s, n):
            pe.wait_ge(*after(f"{pre}_probs", n))
            for k in range(HEADS):
                last = nc.tensor.transpose(ps[s][:, k // 4, (k % 4) * P:(k % 4 + 1) * P],
                                           bufs[s].p[:, k * P:(k + 1) * P], ident[:, :])
            last.then_inc(sem(f"{pre}_pturned"), 1)

        def act_probs(act, pre, s, n):
            act.wait_ge(*after(f"{pre}_pturned", n))
            nc.scalar.activation(bufs[s].pT[:, 0:8 * P],
                                 ps[s][:, 0:2, :].rearrange("p b n -> p (b n)"),
                                 ACT.Copy).then_inc(sem(f"{pre}_pT_a"), 1)

        def dve_probs(dve, pre, s, n):
            dve.wait_ge(*after(f"{pre}_pturned", n))
            nc.vector.tensor_copy(bufs[s].pT[:, 8 * P:12 * P], ps[s][:, 2, :]).then_inc(sem(f"{pre}_pT_b"), 1)

        def at_act_probs(act, pre, s, n):
            act.wait_ge(*after(f"{pre}_pturned", n))
            nc.scalar.activation(bufs[s].pT_hi, ps[s][:, 0:3, :].rearrange("p b n -> p (b n)"),
                                 ACT.Copy).then_inc(sem(f"{pre}_pT_hi"), 1)

        def at_dve_probs(dve, pre, s, n):
            dve.wait_ge(*after(f"{pre}_pT_hi", n))
            nc.vector.tensor_tensor(bufs[s].pT_lo, ps[s][:, 0:3, :].rearrange("p b n -> p (b n)"),
                                    bufs[s].pT_hi, ALU.subtract).then_inc(sem(f"{pre}_pT_lo"), 1)

        def at_pe_pv(pe, pre, s, n):
            b = bufs[s]
            pe.wait_ge(*after(f"{pre}_pT_lo", n))
            for h in range(HEADS):
                for part in (b.pT_hi, b.pT_lo):
                    for v in (b.v_hi, b.v_lo):
                        last = nc.tensor.matmul(ps[s][:, 3, h * (HD + 1):(h + 1) * (HD + 1)],
                                                part[:, place(h) * P:(place(h) + 1) * P], v[:, h, :],
                                                start=(part is b.pT_hi and v is b.v_hi),
                                                stop=(part is b.pT_lo and v is b.v_lo))
            last.then_inc(sem(f"{pre}_pv"), 1)

        def dve_softmax_norm(dve, pre, s, n, at=0):
            b = bufs[s]
            dve.wait_ge(*after(f"{pre}_pv", n))
            o = ps[s][:, 3, at:at + HEADS * (HD + 1)].rearrange("p (h d) -> p h d", h=HEADS)
            nc.vector.reciprocal(b.rec[:, :], o[:, :, HD]).then_inc(sem(f"{pre}_rec"), 1)
            dve.wait_ge(*after(f"{pre}_rec", n))
            nc.vector.tensor_tensor(b.on.rearrange("p (h d) -> p h d", h=HEADS), o[:, :, 0:HD],
                                    b.rec.unsqueeze(2).to_broadcast([P, HEADS, HD]),
                                    ALU.mult).then_inc(sem(f"{pre}_on"), 1)

        def pe_project(pe, pre, s, n, w):
            pe.wait_ge(*after(f"{pre}_onT", n))
            for c in range(2):
                last = nc.tensor.matmul(ps[s][:, 2, 0:C], bufs[s].onT[:, c, :], w[:, c, :],
                                        start=(c == 0), stop=(c == 1))
            last.then_inc(sem(f"{pre}_proj"), 1)

        def half_steps(n, it):
            return n * (2 * SINKHORN_ITERS) + (it + 1 - 2 * SINKHORN_ITERS)

        def halfs(n, it):
            return n * (2 * SINKHORN_ITERS - 1) + (it + 2 - 2 * SINKHORN_ITERS)

        def pairs(eng, head, pair):
            head(1)
            with eng.Fori(0, B - 3, STREAMS) as i:
                pair(i + 1, i + 3)
            pair(B - 1, None)

        def sinkhorn_stages(eng, stage):
            stage(None, None, (0, 1))
            stage(None, (0, 1), (1, 2))
            with eng.Fori(0, B - 3, 2) as i:
                stage((0, i + 1), (1, i + 2), (0, i + 3))
                stage((1, i + 2), (0, i + 3), (1, i + 4))
            stage((0, B - 1), (1, B), None)
            stage((1, B), None, None)

        def both(step, n0, *args):
            for s in range(STREAMS):
                step(s, n0 + s, *args)

        @block.sync
        def _(sp):
            sp.dma_start(consts[:, 0:TOK_CONSTS], packed[:, 0:TOK_CONSTS]).then_inc(sem("tok_consts_loaded"), 16)
            for s in range(STREAMS):
                sp.dma_start(bufs[s].xT, x[s]).then_inc(sem(f"tok_x{s}"), 16)
            sp.dma_start(consts[:, TOK_CONSTS:], packed[:, TOK_CONSTS:]).then_inc(sem("consts_loaded"), 16)
            with sp.Fori(0, B - 2 * STREAMS + 1, STREAMS) as i:
                for s in range(STREAMS):
                    sp.wait_ge(sem("tok_v"), i + s + 1)
                    sp.dma_start(bufs[s].xT, x[bass.ds(i + s + STREAMS, 1), :, :, :].rearrange(
                        "o p c n -> (o p) c n")).then_inc(sem(f"tok_x{s}"), 16)
            for k in range(2):
                sp.dma_start(ew1[k], w1[k]).then_inc(sem(f"moe_w1_{k}"), 16)
                sp.dma_start(ew2[k], w2[k]).then_inc(sem(f"moe_w2_{k}"), 16)
            with sp.Fori(0, EXPERTS - 3, 2) as e:
                for k in range(2):
                    sp.wait_ge(sem("moe_w_lo"), e + k + 1)
                    sp.dma_start(ew1[k], w1[bass.ds(e + k + 2, 1), :, :, :].rearrange(
                        "o p c n -> (o p) c n")).then_inc(sem(f"moe_w1_{k}"), 16)
                    sp.dma_start(ew2[k], w2[bass.ds(e + k + 2, 1), :, :, :].rearrange(
                        "o p c n -> (o p) c n")).then_inc(sem(f"moe_w2_{k}"), 16)
            sp.wait_ge(sem("result"), 1)
            for w in range(WINDOWS):
                sp.dma_start(out.rearrange("b (q w) c -> w q b c", w=WINDOWS)[w],
                             hs[w * WQ:(w + 1) * WQ, :, :]).then_inc(sem("stored"), 16)
            sp.wait_ge(sem("stored"), 16 * WINDOWS)

        flat_arena = arena[:, :, :].rearrange("p s n -> p (s n)")
        gelu_out = flat_arena[:, 0:HT * T].rearrange("p (m n) -> p m n", m=HT)

        def bf(lo, words):
            return flat_arena[:, lo:lo + words].bitcast(BF16)

        feat32 = flat_arena[0:HC, 0:2 * T].rearrange("p (c n) -> p c n", c=2)
        cwT = flat_arena[0:EXPERTS, 2 * T:3 * T]
        he = flat_arena[:, 0:HT * TG].rearrange("p (m n) -> p m n", m=HT)
        he_hi, he_lo = ([bf(HT * TG * (1 + k) + part * HT * TG // 2, HT * TG // 2).rearrange(
            "p (m n) -> p m n", m=HT) for k in range(2)] for part in range(2))
        W_SET = 2 * HIDDEN + HT * C
        w_at = 3 * HT * TG
        w1_parts = [[bf(w_at + k * W_SET + part * HIDDEN, HIDDEN)[0:HC, :].rearrange("p (c n) -> p c n", c=2)
                     for part in range(2)] for k in range(2)]
        w2_parts = [[bf(w_at + k * W_SET + 2 * HIDDEN + part * HT * C // 2, HT * C // 2).rearrange(
            "p (m n) -> p m n", m=HT) for part in range(2)] for k in range(2)]
        assert w_at + 2 * W_SET <= STREAMS * ARENA
        feat_hi, feat_lo = (featT[:, :, :].rearrange("p c n -> p (c n)").bitcast(BF16)[
            :, part * 2 * T:(part + 1) * 2 * T].rearrange("p (c n) -> p c n", c=2) for part in range(2))

        q_at = HT * T
        wq1T = bf(q_at, HT * P)[0:HC, :].rearrange("p (c n) -> p c n", c=2)
        wq2T = bf(q_at + HT * P, HT * C // 2).rearrange("p (m n) -> p m n", m=HT)
        q_end = q_at + HT * P + HT * C // 2
        w1_s = flat_arena[:, q_end:q_end + HT * C].rearrange("p (m n) -> p m n", m=HT)
        w1_q = bf(q_end + HT * C, HT * C // 2).rearrange("p (m n) -> p m n", m=HT)
        w2_q = bf(q_end + HT * C + HT * C // 2, HIDDEN)[0:HC, :].rearrange("p (c n) -> p c n", c=2)
        q_end2 = q_end + HT * C + HT * C // 2 + HIDDEN
        csb = flat_arena[0:HC, q_end2:q_end2 + 2 * P].rearrange("p (c n) -> p c n", c=2)
        sw2b = flat_arena[0:HC, q_end2 + 2 * P:q_end2 + 4 * P].rearrange("p (c n) -> p c n", c=2)
        assert q_end2 + 4 * P <= STREAMS * ARENA
        oq = flat_arena[:, q_end:q_end + B * C].rearrange("p (b n) -> p b n", b=B)
        wmax = flat_arena[:, q_end2 + 4 * P:q_end2 + 4 * P + C]
        assert q_end2 + 4 * P + C <= STREAMS * ARENA

        @block.gpsimd
        def _(pool):
            nc.gpsimd.memset(ident[:, :], 0.0).then_inc(sem("mask_zero"), 1)
            nc.gpsimd.memset(identb[:, :], 0.0).then_inc(sem("mask_zero"), 1)
            nc.gpsimd.memset(diag_off[:, :, :], 0.0).then_inc(sem("mask_zero"), 1)
            nc.gpsimd.memset(diag_one[:, :], 0.0).then_inc(sem("mask_zero"), 1)
            nc.gpsimd.memset(pick[:, :, :], 0.0).then_inc(sem("mask_zero"), 1)
            nc.gpsimd.memset(ones[:, :], 1.0).then_inc(sem("masks_ready"), 1)
            pool.wait_ge(sem("mask_zero"), 5)
            for k in range(3):
                nc.gpsimd.affine_select(out=pick[:, :, :], in_=pick[:, :, :], compare_op=ALU.not_equal, fill=1.0,
                                        base=-HEADS * k, pattern=[[-1, HEADS], [0, P]],
                                        channel_multiplier=1).then_inc(sem("pick_ready"), 1)
                pool.wait_ge(sem("pick_ready"), k + 1)
            for m, fill in ((ident, 1.0), (identb, 1.0), (diag_one, float(np.exp(SCALE) - 1.0))):
                nc.gpsimd.affine_select(out=m[:, :], in_=m[:, :], compare_op=ALU.not_equal, fill=fill, base=0,
                                        pattern=[[-1, P]], channel_multiplier=1).then_inc(sem("masks_ready"), 1)
            nc.gpsimd.affine_select(out=diag_off[:, :, :], in_=diag_off[:, :, :], compare_op=ALU.not_equal,
                                    fill=-DIAG_VAL, base=0, pattern=[[0, GROUPS], [-1, P]],
                                    channel_multiplier=1).then_inc(sem("masks_ready"), 1)
            nc.gpsimd.iota(iota8[:, :], pattern=[[1, EXPERTS]], base=0, channel_multiplier=0,
                           allow_small_or_imprecise_dtypes=True).then_inc(sem("masks_ready"), 1)

        def turned(t):
            return ps[t // 8][0:HC, t % 8 // 2, (t % 2) * 2 * P:(t % 2 + 1) * 2 * P]

        def pe_turn_all(pe, pre):
            for t in range(B):
                pe.wait_ge(sem(f"{pre}_xn"), t + 1)
                for c in range(2):
                    last = nc.tensor.transpose(turned(t)[:, c * P:(c + 1) * P], x3[:, t, c * HC:(c + 1) * HC],
                                               ident[:, :])
                last.then_inc(sem(f"{pre}_xturned"), 1)

        def act_turned_all(act, pre, dst, gain=None, bias=None):
            for t in range(0, B, 2):
                act.wait_ge(sem(f"{pre}_xturned"), t + 2)
                bank = ps[t // 8][0:HC, t % 8 // 2, :].rearrange("p (t c n) -> p c t n", t=2, c=2)
                for c in range(2):
                    to = dst[:, c, t * P:(t + 2) * P].rearrange("p (t n) -> p t n", t=2)
                    if gain is None:
                        last = nc.scalar.activation(to, bank[:, c], ACT.Copy)
                    else:
                        last = nc.scalar.activation(to, bank[:, c], ACT.Identity, bias=bias[:, c:c + 1],
                                                    scale=gain[:, c:c + 1])
                last.then_inc(sem(f"{pre}_feat"), 1)

        def moe_up(pe, e, k, g):
            for m in range(HT):
                q = g * HT + m
                pe.wait_ge(sem("moe_gelu"), e * (NG * HT) + k * NG * HT + q + 1)
                for c in range(2):
                    for w, x in ((0, feat_hi), (0, feat_lo), (1, feat_hi)):
                        last = nc.tensor.matmul(ps[0][:, q % 4, :], w1_parts[k][w][:, c, m * P:(m + 1) * P],
                                                x[:, c, g * TG:(g + 1) * TG], start=(c == 0 and w == 0 and x is feat_hi),
                                                stop=(c == 1 and w == 1))
                last.then_inc(sem("moe_hidden"), 1)

        def moe_down(pe, e, k, g):
            pe.wait_ge(sem("moe_he_lo"), e * (NG * HT) + k * NG * HT + (g + 1) * HT + HT)
            for t in range(4):
                pe.wait_ge(sem("moe_added"), e * B + k * B + g * 4 + t + 1)
                for m in range(HT):
                    for h, w in ((he_hi, 0), (he_hi, 1), (he_lo, 0)):
                        last = nc.tensor.matmul(ps[1][:, t, 0:C], h[g % 2][:, m, t * P:(t + 1) * P],
                                                w2_parts[k][w][:, m, :], start=(m == 0 and w == 0 and h is he_hi),
                                                stop=(m == HT - 1 and h is he_lo))
                last.then_inc(sem("moe_out"), 1)

        def experts(eng, expert):
            with eng.Fori(0, EXPERTS - 3, 2) as e:
                expert(e, 0, True)
                expert(e, 1, True)
            expert(EXPERTS - 2, 0, True)
            expert(EXPERTS - 2, 1, False)

        @block.tensor
        def _(pe):
            loaded(pe)

            tok_w, tok_pw = chunks("tok_w"), chunks("tok_pw")

            def tiles(s, lo, n):
                return ps[s][:, lo:lo + n // 2, :].rearrange("p b n -> p (b n)").rearrange(
                    "p (t n) -> p t n", t=n)

            def tok_product(s, n, part):
                xT = bufs[s].xT
                o = tiles(s, 2 * part, STRIDE)
                for t in range(STRIDE):
                    for c in range(2):
                        cols = slice(t, N_IN, STRIDE) if part == 0 else slice(t * P, (t + 1) * P)
                        last = nc.tensor.matmul(o[:, t, 0:C], xT[:, c, cols],
                                                tok_w[:, c, part * C:(part + 1) * C],
                                                start=(c == 0), stop=(c == 1))
                last.then_inc(sem(f"tok_{'qk'[part]}"), 1)

            def tok_q(s, n):
                pe.wait_ge(sem(f"tok_x{s}"), (n - (1 + s)) * (16 // STREAMS) + 16)
                tok_product(s, n, 0)

            def tok_k(s, n):
                if not isinstance(n, int):
                    pe.wait_ge(*after("tok_h", n - STREAMS))
                tok_product(s, n, 1)

            def tok_v(s, n):
                pe.wait_ge(*after("tok_pooled", n))
                o = tiles(s, 0, 4)
                for t in range(4):
                    for c in range(2):
                        last = nc.tensor.matmul(o[:, t, 0:C], bufs[s].xT[:, c, t * P:(t + 1) * P],
                                                tok_w[:, c, 2 * C:3 * C], start=(c == 0), stop=(c == 1))
                last.then_inc(sem("tok_v"), 1)

            def tok_turn_k(s, n):
                pe.wait_ge(*after("tok_vpad", n))
                b = bufs[s]
                for g in range(GROUPS):
                    for t in range(STRIDE):
                        at = (1 + t) * HEADS + 4 * g
                        nc.tensor.transpose(ps[s][:, g, t * P:(t + 1) * P], b.qk_pad[:, at:at + 4, :], ident[:, :])
                for g in range(GROUPS):
                    last = nc.tensor.transpose(ps[s][:, 3, g * P:(g + 1) * P], b.qk_pad[:, 4 * g:4 * g + 4, :],
                                               ident[:, :])
                last.then_inc(sem("tok_turned"), 1)

            def tok_scores(s, n, half):
                b = bufs[s]
                if half == 0:
                    pe.wait_ge(*after("tok_kT", n))
                    pe.wait_ge(*after("tok_qT", n))
                else:
                    pe.wait_ge(*after("tok0_pT_a", n))
                    pe.wait_ge(*after("tok0_pT_b", n))
                for g in range(GROUPS):
                    for jj in range(2):
                        r = 32 * (2 * half + jj)
                        for w in range(WINDOWS):
                            last = nc.tensor.matmul(
                                ps[s][w * WQ:(w + 1) * WQ, 2 * jj + g // 2, (g % 2) * 256:(g % 2 + 1) * 256],
                                b.qT[r:r + HD, g, w * WQ:(w + 1) * WQ], b.kT[r:r + HD, g, 2 * w:2 * w + 2, :],
                                start=True, stop=True)
                last.then_inc(sem(f"tok{half}_scores"), 1)

            def tok_pv(s, n, half):
                b = bufs[s]
                pe.wait_ge(*after(f"tok{half}_pT_a", n))
                pe.wait_ge(*after(f"tok{half}_pT_b", n))
                pT = b.pT.rearrange("p (l h n) -> p l h n", l=6, h=2)
                for l in range(6):
                    h = 4 * (l % GROUPS) + 2 * half + l // GROUPS
                    at = TOK_PV + h * (HD + 1)
                    for w in range(WINDOWS):
                        for k in range(2):
                            last = nc.tensor.matmul(
                                ps[s][w * WQ:(w + 1) * WQ, 3, at:at + HD + 1],
                                pT[:, l, k, w * WQ:(w + 1) * WQ], b.v_ext[:, (2 * w + k) * HEADS + h, :],
                                start=(k == 0), stop=(k == 1))
                last.then_inc(sem(f"tok{half}_pv" if half == 0 else "tok_pv"), 1)

            def tok_head(n):
                both(tok_q, n)
                both(tok_k, n)
                both(tok_v, n)
                both(tok_turn_k, n)

            def tok_pair(old, new):
                for half in range(2):
                    both(tok_scores, old, half)
                    both(lambda s, n: pe_turn_probs(pe, f"tok{half}", s, n), old)
                    both(tok_pv, old, half)
                if new is not None:
                    both(tok_q, new)
                both(lambda s, n: pe_turn(pe, "tok_on", "tok_oturned", s, n, bufs[s].on, 3), old)
                both(lambda s, n: pe_project(pe, "tok", s, n, tok_pw), old)
                if new is not None:
                    both(tok_k, new)
                    both(tok_v, new)
                    both(tok_turn_k, new)
            pairs(pe, tok_head, tok_pair)

            pe.wait_ge(sem("consts_loaded"), 16)
            for pre, w, pw in (("at", chunks("at_w"), chunks("at_pw")), ("ff", chunks("ff_w"), chunks("ff_pw"))):
                def at_head(n):
                    both(lambda s, n: pe_turn(pe, f"{pre}_xn", f"{pre}_xturned", s, n, bufs[s].xn, 0), n)
                    both(lambda s, n: at_pe_qkv(pe, pre, s, n, w), n)
                    both(lambda s, n: at_pe_turn_qk(pe, pre, s, n), n)

                def at_pair(old, new):
                    both(lambda s, n: at_pe_scores(pe, pre, s, n), old)
                    both(lambda s, n: pe_turn_probs(pe, pre, s, n), old)
                    both(lambda s, n: at_pe_pv(pe, pre, s, n), old)
                    if new is not None:
                        both(lambda s, n: pe_turn(pe, f"{pre}_xn", f"{pre}_xturned", s, n, bufs[s].xn, 0), new)
                    both(lambda s, n: pe_turn(pe, f"{pre}_on", f"{pre}_oturned", s, n, bufs[s].on, 3), old)
                    for s in range(STREAMS):
                        if new is not None:
                            at_pe_qkv(pe, pre, s, new + s, w)
                        pe_project(pe, pre, s, old + s, pw)
                    if new is not None:
                        both(lambda s, n: at_pe_turn_qk(pe, pre, s, n), new)
                pairs(pe, at_head, at_pair)
            pe_turn_all(pe, "gate")
            pe.wait_ge(sem("gate_feat"), B // 2)
            for t in range(B):
                for c in range(2):
                    last = nc.tensor.matmul(ps[0][:, 0, t * EXPERTS:(t + 1) * EXPERTS],
                                            feat32[:, c, t * P:(t + 1) * P], chunks("gate_w")[:, c, :],
                                            start=(c == 0), stop=(c == 1))
            last.then_inc(sem("gate_logits"), 1)

            pe.wait_ge(sem("moe_cw"), 1)
            for t in range(B):
                last = nc.tensor.transpose(ps[1][0:EXPERTS, t // 4, (t % 4) * P:(t % 4 + 1) * P], cw[:, t, :],
                                           ident[:, :])
            last.then_inc(sem("moe_cwturned"), 1)
            pe.wait_ge(sem("moe_cwT"), 1)
            for t in range(B):
                last = nc.tensor.matmul(ps[t // 8][:, t % 8 // 2, (t % 2) * C:(t % 2 + 1) * C],
                                        cwT[:, t * P:(t + 1) * P], const("b2"), start=True, stop=True)
                if t % 8 == 7:
                    last.then_inc(sem("moe_bias2"), 1)
            pe.wait_ge(sem("moe_start"), 1)

            def expert(e, k, more):
                pe.wait_ge(sem("moe_w_lo"), e + k + 1)
                for g in range(NG):
                    moe_up(pe, e, k, g)
                    if g > 0:
                        moe_down(pe, e, k, g - 1)
                moe_down(pe, e, k, NG - 1)
            experts(pe, expert)

            l1_w, l1_pw = chunks("l1_w"), chunks("l1_pw")

            def l1_qv(s, n, part, c):
                if part == 0 and c == 0:
                    pe.wait_ge(*after("l1_xT", n))
                last = nc.tensor.matmul(ps[s][:, 3 - 2 * part, part * C:(part + 1) * C], bufs[s].xT[:, c, 0:P],
                                        l1_w[:, c, 2 * part * C:(2 * part + 1) * C],
                                        start=(c == 0), stop=(c == 1))
                if c == 1:
                    last.then_inc(sem("l1_" + "qv"[part]), 1)

            def l1_turn_q(s, n):
                pe.wait_ge(*after("l1_pad", n))
                for g in range(GROUPS):
                    last = nc.tensor.transpose(ps[s][:, 0, g * P:(g + 1) * P],
                                               bufs[s].qk_pad[:, 4 * g:4 * g + 4, :], ident[:, :])
                last.then_inc(sem("l1_qturned"), 1)

            def l1_gram(s, n, j, g):
                b = bufs[s]
                if g == 0:
                    nc.tensor.matmul(ps[s][:, j, 0:GROUPS * P], identb[:, :],
                                     diag_off[:, :, :].rearrange("p a n -> p (a n)"),
                                     start=True, stop=False, skip_group_check=True)
                last = nc.tensor.matmul(ps[s][:, j, g * P:(g + 1) * P], b.qT[32 * j:32 * j + HD, g, :],
                                        b.qT[32 * j:32 * j + HD, g, :], start=False, stop=True,
                                        skip_group_check=True)
                if g == GROUPS - 1:
                    last.then_inc(sem("l1_gram"), 1)

            def l1_half_step(s, n, it):
                b = bufs[s]
                if it == 0:
                    pe.wait_ge(*after("l1_kernel_lo", n))
                else:
                    pe.wait_ge(sem("l1_xlo"), halfs(n, it - 1))
                for k in range(HEADS):
                    for part in (b.hi, b.lo):
                        last = nc.tensor.matmul(ps[s][:, 3, SUMS + 2 * k:SUMS + 2 * k + 2],
                                                part[:, k * P:(k + 1) * P], b.x_parts[:, k, :],
                                                start=(part is b.hi), stop=(part is b.lo))
                last.then_inc(sem("l1_sums"), 1)

            def l1_turn_u(s, n):
                pe.wait_ge(*after("l1_uparts", n))
                nc.tensor.transpose(ps[s][:, 0, 0:P // 2].bitcast(BF16), bufs[s].u_parts,
                                    identb[:, :]).then_inc(sem("l1_uturned"), 1)

            def l1_u_rows(s, n, half):
                if half == 0:
                    pe.wait_ge(*after("l1_uT", n))
                for h in range(8 * half, 8 + 4 * half):
                    last = nc.tensor.matmul(ps[s][:, h // 4, (h % 4) * P:(h % 4 + 1) * P],
                                            pick[:, h, :], bufs[s].uT_parts, start=True, stop=True)
                last.then_inc(sem("l1_urows"), 1)

            def l1_turn_max(s, n):
                pe.wait_ge(*after("l1_rowmax", n))
                nc.tensor.transpose(ps[s][0:HEADS, 3, 0:P], bufs[s].stats12, ident[:, :]).then_inc(
                    sem("l1_maxturned"), 1)

            def l1_spread_max(s, n):
                pe.wait_ge(*after("l1_maxdiag", n))
                nc.tensor.matmul(ps[s][:, 3, P:P + HEADS], ones[0:HEADS, :], bufs[s].maxdiag,
                                 start=True, stop=True).then_inc(sem("l1_maxspread"), 1)

            def l1_pv_diagonal(s, n):
                pe.wait_ge(*after("l1_sv", n))
                nc.tensor.matmul(ps[s][:, 3, 0:HEADS * (HD + 1)], diag_one[:, :], bufs[s].v_ext[:, 0:HEADS, :],
                                 start=True, stop=False, skip_group_check=True)

            def l1_pv(s, n, half):
                b = bufs[s]
                o = ps[s][:, 3, 0:HEADS * (HD + 1)]
                if half == 0:
                    pe.wait_ge(*after("l1_probs_lo", n))
                for h in range(HEADS // 2 * half, HEADS // 2 * (half + 1)):
                    for part in (b.hi, b.lo):
                        for v in (b.v_hi, b.v_lo):
                            last = nc.tensor.matmul(o[:, h * (HD + 1):(h + 1) * (HD + 1)],
                                                    part[:, place(h) * P:(place(h) + 1) * P], v[:, h, :],
                                                    start=False, stop=True, skip_group_check=True)
                if half == 1:
                    last.then_inc(sem("l1_pv"), 1)

            def l1_project(s, n, c):
                if c == 0:
                    pe.wait_ge(*after("l1_onT", n))
                last = nc.tensor.matmul(ps[s][:, 1, 0:C], bufs[s].onT[:, c, :], l1_pw[:, c, :],
                                        start=(c == 0), stop=(c == 1))
                if c == 1:
                    last.then_inc(sem("l1_proj"), 1)

            def l1_stage(post, half, pre):
                for it in range(2 * SINKHORN_ITERS):
                    if half:
                        l1_half_step(*half, it)
                    if post:
                        if it == 1:
                            l1_turn_u(*post)
                        if it in (2, 3):
                            l1_u_rows(*post, it - 2)
                        if it == 6:
                            l1_turn_max(*post)
                        if it == 7:
                            l1_spread_max(*post)
                        if it == 9:
                            l1_pv_diagonal(*post)
                        if it in (12, 13):
                            l1_pv(*post, it - 12)
                        if it == 14:
                            pe_turn(pe, "l1_on", "l1_oturned", *post, bufs[post[0]].on, 3)
                    if pre and it == 15:
                        pe.wait_ge(*after("l1_vcopy", pre[1]))
                    if post and it in (15, 16):
                        l1_project(*post, it - 15)
                    if pre:
                        if it == 1:
                            pe_turn(pe, "l1_xn", "l1_xturned", *pre, bufs[pre[0]].xn, 3, 2 * P)
                        if it in (3, 4):
                            l1_qv(*pre, 0, it - 3)
                        if it in (8, 10):
                            l1_qv(*pre, 1, (it - 8) // 2)
                        if it == 10:
                            l1_turn_q(*pre)
                        if it == 11:
                            pe.wait_ge(*after("l1_qT", pre[1]))
                            l1_gram(*pre, 0, 0)
                            l1_gram(*pre, 0, 1)
                        if it == 12:
                            l1_gram(*pre, 2, 0)
                        if it == 13:
                            l1_gram(*pre, 0, 2)
                        if it == 14:
                            l1_gram(*pre, 2, 1)
                            l1_gram(*pre, 2, 2)
                        if it == 16:
                            l1_gram(*pre, 3, 0)
                        if it == 17:
                            l1_gram(*pre, 3, 1)
                            l1_gram(*pre, 3, 2)
                        if it == 18:
                            if post:
                                pe.wait_ge(*after("l1_biased", post[1]))
                            l1_gram(*pre, 1, 0)
                            l1_gram(*pre, 1, 1)
                        if it == 19:
                            l1_gram(*pre, 1, 2)
            sinkhorn_stages(pe, l1_stage)
            pe_turn_all(pe, "q")

            p0 = ps[0]
            pe.wait_ge(sem("q_wmax"), 1)
            pe.wait_ge(sem("q_feat"), B // 4)
            for c in range(2):
                last = nc.tensor.transpose(p0[0:HC, 3, c * P:(c + 1) * P], wmax[:, c * HC:(c + 1) * HC], ident[:, :])
            last.then_inc(sem("q_wmaxturned"), 1)
            pe.wait_ge(sem("q_cs_rows"), 1)
            for c in range(2):
                last = nc.tensor.matmul(p0[:, 0, c * HC:(c + 1) * HC], csb[:, c, :], ident[0:HC, 0:HC],
                                        start=True, stop=True)
            last.then_inc(sem("q_csrow"), 1)
            pe.wait_ge(sem("q_range"), 1)
            nc.tensor.transpose(p0[0:2, 1, 0:HC], small[0:HC, 20:22], ident[0:HC, 0:HC]).then_inc(
                sem("q_rangeturned"), 1)
            pe.wait_ge(sem("q_rangediag"), 1)
            nc.tensor.matmul(p0[:, 2, 0:2], ones[0:2, :], small[0:2, 24:26], start=True,
                             stop=True).then_inc(sem("q_rangespread"), 1)
            pe.wait_ge(sem("q_w_quant"), 1)
            tb = ps[1][:, :, :].rearrange("p b n -> p (b n)").bitcast(BF16).rearrange("p (b n) -> p b n", b=4)
            for c in range(2):
                for m in range(HT):
                    nc.tensor.transpose(tb[0:HC, c, m * P:(m + 1) * P], w1_q[:, m, c * HC:(c + 1) * HC],
                                        identb[:, :])
            for c in range(2):
                for m in range(HT):
                    last = nc.tensor.transpose(tb[:, 2 + m // 3, (m % 3) * C + c * HC:(m % 3) * C + (c + 1) * HC],
                                               w2_q[:, c, m * P:(m + 1) * P], identb[0:HC, 0:HC])
            last.then_inc(sem("q_wturned"), 1)
            for c in range(2):
                last = nc.tensor.matmul(p0[:, 3, c * HC:(c + 1) * HC], sw2b[:, c, :], ident[0:HC, 0:HC],
                                        start=True, stop=True)
            last.then_inc(sem("q_sw2row"), 1)
            pe.wait_ge(sem("q_xq"), 1)
            pe.wait_ge(sem("q_wT"), 1)
            pe.wait_ge(sem("q_sw2"), 1)
            for g in range(NG):
                for m in range(HT):
                    k = g * HT + m
                    if k >= 8:
                        pe.wait_ge(sem("q_gelu"), k - 7)
                    o = ps[k % 8 // 4][:, k % 4, :]
                    for c in range(2):
                        last = nc.tensor.matmul(o, wq1T[:, c, m * P:(m + 1) * P], xq[:, c, g * TG:(g + 1) * TG],
                                                start=(c == 0), stop=(c == 1))
                    last.then_inc(sem("q_up"), 1)
            pe.wait_ge(sem("q_hmax"), 1)
            nc.tensor.transpose(p0[0:1, 0, 0:P], small[:, 30:31], ident[:, :]).then_inc(sem("q_hmaxturned"), 1)
            pe.wait_ge(sem("q_hmaxone"), 1)
            nc.tensor.matmul(p0[:, 1, 0:1], ones[0:1, :], small[0:1, 31:32], start=True,
                             stop=True).then_inc(sem("q_hmaxspread"), 1)
            pe.wait_ge(sem("q_hscale"), 1)
            for t in range(B):
                if t % 4 == 0:
                    pe.wait_ge(sem("q_hq"), t // 4 + 1)
                if t >= 8:
                    pe.wait_ge(sem("q_down_read"), t - 7)
                o = ps[t % 8 // 4][:, t % 4, 0:C]
                for m in range(HT):
                    last = nc.tensor.matmul(o, hqs[t // 4][:, m, (t % 4) * P:(t % 4 + 1) * P], wq2T[:, m, :],
                                            start=(m == 0), stop=(m == HT - 1))
                last.then_inc(sem("q_down"), 1)
            pe.wait_ge(sem("q_orange"), 1)
            nc.tensor.transpose(p0[0:2, 1, 0:P], small[:, 40:42], ident[:, :]).then_inc(sem("q_orangeturned"), 1)
            pe.wait_ge(sem("q_orangediag"), 1)
            nc.tensor.matmul(p0[:, 2, 0:2], ones[0:2, :], small[0:2, 76:78], start=True,
                             stop=True).then_inc(sem("q_orangespread"), 1)

        @block.scalar
        def _(act):
            loaded(act)

            def tok_kT(s, n):
                act.wait_ge(*after("tok_turned", n))
                nc.scalar.activation(bufs[s].kT.rearrange("p g t n -> p (g t n)"),
                                     ps[s][:, 0:3, :].rearrange("p b n -> p (b n)"),
                                     ACT.Copy).then_inc(sem("tok_kT"), 1)
            def tok_head(n):
                both(tok_kT, n)

            def tok_pair(old, new):
                for half in range(2):
                    both(lambda s, n: act_exp(act, f"tok{half}", s, n), old)
                    both(lambda s, n: act_probs(act, f"tok{half}", s, n), old)
                both(lambda s, n: act_turned(act, "tok_oturned", "tok_onT", s, n, bufs[s].onT, 3), old)
                if new is not None:
                    both(tok_kT, new)
            pairs(act, tok_head, tok_pair)

            act.wait_ge(sem("consts_loaded"), 16)
            for pre in ("at", "ff"):
                gain, bias = (const("ln1_g"), const("ln1_b")) if pre == "ff" else (None, None)

                def at_xT(s, n):
                    act_turned(act, f"{pre}_xturned", f"{pre}_xT", s, n, bufs[s].xT[:, :, 0:P], 0, gain, bias)

                def at_head(n):
                    both(at_xT, n)
                    both(lambda s, n: at_act_qk(act, pre, s, n), n)

                def at_pair(old, new):
                    both(lambda s, n: act_exp(act, pre, s, n), old)
                    both(lambda s, n: at_act_probs(act, pre, s, n), old)
                    if new is not None:
                        both(at_xT, new)
                    both(lambda s, n: act_turned(act, f"{pre}_oturned", f"{pre}_onT", s, n, bufs[s].onT, 3), old)
                    if new is not None:
                        both(lambda s, n: at_act_qk(act, pre, s, n), new)
                pairs(act, at_head, at_pair)
            act_turned_all(act, "gate", feat32, const("ln2_g"), const("ln2_b"))
            act.wait_ge(sem("gate_feat"), B // 2)
            nc.scalar.activation(feat_hi, feat32, ACT.Copy).then_inc(sem("gate_feat_hi"), 1)

            def split_weights(k, n):
                act.wait_ge(sem(f"moe_w1_{k}"), (n - (1 + k)) * 8 + 16)
                act.wait_ge(sem(f"moe_w2_{k}"), (n - (1 + k)) * 8 + 16)
                nc.scalar.activation(w1_parts[k][0], ew1[k], ACT.Copy)
                nc.scalar.activation(w2_parts[k][0], ew2[k], ACT.Copy).then_inc(sem("moe_w_hi"), 1)
            split_weights(0, 1)

            act.wait_ge(sem("moe_gap"), 1)
            nc.scalar.activation(gw[:, :, 1:2], gw[:, :, 3:4], ACT.Exp).then_inc(sem("moe_gapexp"), 1)
            act.wait_ge(sem("moe_cwturned"), 1)
            nc.scalar.activation(cwT, ps[1][0:EXPERTS, :, :].rearrange("p b n -> p (b n)"),
                                 ACT.Copy).then_inc(sem("moe_cwT"), 1)
            act.wait_ge(sem("moe_start"), 1)

            def expert(e, k, more):
                nc.scalar.activation(b1cur[:, k, :], const("b1")[:, bass.ds(e * HT + k * HT, HT)],
                                     ACT.Copy).then_inc(sem("moe_b1"), 1)
                act.wait_ge(sem("moe_b1"), e + k + 1)
                for g in range(NG):
                    act.wait_ge(sem("moe_out"), e * B + k * B + g * 4 + 4)
                    for m in range(HT):
                        at = g * HT + m + 1
                        act.wait_ge(sem("moe_hidden"), e * (NG * HT) + k * NG * HT + at)
                        bias = b1cur[:, k, m:m + 1]
                        nc.scalar.activation(he_hi[g % 2][:, m, :], ps[0][:, (at - 1) % 4, :], ACT.Gelu, bias=bias)
                        act.wait_ge(sem("moe_he_lo"), e * (NG * HT) + k * NG * HT + at)
                        nc.scalar.activation(he[:, m, :], ps[0][:, (at - 1) % 4, :], ACT.Gelu,
                                             bias=bias).then_inc(sem("moe_gelu"), 1)
                    if g == 1 and more:
                        split_weights(1 - k, e + k + 2)
            experts(act, expert)

            def qT(s, n):
                act.wait_ge(*after("l1_qturned", n))
                nc.scalar.activation(bufs[s].qT, ps[s][:, 0, 0:GROUPS * P].rearrange(
                    "p (g n) -> p g n", g=GROUPS), ACT.Copy).then_inc(sem("l1_qT"), 1)

            def kernel_exp(s, n, k):
                b = bufs[s]
                j = BANK_ORDER[k]
                act.wait_ge(sem("l1_gram"), n * 4 + (k + 1 - 4))
                for dst in (b.hi, b.p):
                    last = nc.scalar.activation(dst[:, j * GROUPS * P:(j + 1) * GROUPS * P],
                                                ps[s][:, j, 0:GROUPS * P], ACT.Exp,
                                                scale=1.0 / OT_REG, bias=neg_reg[:, 0:1])
                last.then_inc(sem("l1_kernel"), 1)

            def uT(s, n):
                act.wait_ge(*after("l1_uturned", n))
                nc.scalar.activation(bufs[s].uT_parts, ps[s][0:3 * HEADS, 0, 0:P // 2].bitcast(BF16),
                                     ACT.Copy).then_inc(sem("l1_uT"), 1)

            def probs(s, n):
                act.wait_ge(*after("l1_z", n))
                nc.scalar.activation(bufs[s].hi, bufs[s].pT, ACT.Exp).then_inc(sem("l1_probs_hi"), 1)
                act.wait_ge(*after("l1_probs_hi", n))
                nc.scalar.activation(bufs[s].pT, bufs[s].pT, ACT.Exp).then_inc(sem("l1_probs"), 1)

            def l1_stage(post, half, pre):
                if post:
                    uT(*post)
                if pre:
                    act_turned(act, "l1_xturned", "l1_xT", *pre, bufs[pre[0]].xT[:, :, 0:P], 3, at=2 * P)
                if post:
                    probs(*post)
                if pre:
                    qT(*pre)
                    kernel_exp(*pre, 0)
                if post:
                    act_turned(act, "l1_oturned", "l1_onT", *post, bufs[post[0]].onT, 3)
                if pre:
                    for k in range(1, 4):
                        kernel_exp(*pre, k)
            sinkhorn_stages(act, l1_stage)

            act_turned_all(act, "q", featT)

            act.wait_ge(sem("q_hidden_scale"), 1)
            for g in range(NG):
                for m in range(HT):
                    k = g * HT + m
                    act.wait_ge(sem("q_up"), k + 1)
                    nc.scalar.activation(gelu_out[:, m, g * TG:(g + 1) * TG], ps[k % 8 // 4][:, k % 4, :],
                                         ACT.Gelu, bias=const("q_b1")[:, m:m + 1],
                                         scale=small[:, 48 + m:49 + m]).then_inc(sem("q_gelu"), 1)

        @block.vector
        def _(dve):
            for s in range(STREAMS):
                nc.vector.memset(bufs[s].qk_pad, 0.0).then_inc(sem("pads_ready"), 1)
                nc.vector.memset(bufs[s].v_ext, 1.0).then_inc(sem("pads_ready"), 1)
            nc.vector.memset(neg_reg[:, :], -1.0 / OT_REG).then_inc(sem("pads_ready"), 1)
            loaded(dve)

            chain = [0]

            def link(ins):
                chain[0] += 1
                ins.then_inc(sem("dve_chain"), 1)
                dve.wait_ge(sem("dve_chain"), chain[0])

            def row(n, src=None):
                return (hs if src is None else src)[:, bass.ds(n - 1, 1), :].rearrange("p o c -> p (o c)")

            def residual(pre, s, n, h, bias, bank=2):
                dve.wait_ge(*after(f"{pre}_proj", n))
                nc.vector.tensor_tensor(bufs[s].t1, ps[s][:, bank, 0:C], bias, ALU.add).then_inc(sem(f"{pre}_biased"), 1)
                dve.wait_ge(*after(f"{pre}_biased", n))
                nc.vector.tensor_tensor(bufs[s].t1, h, bufs[s].t1, ALU.add).then_inc(sem(f"{pre}_h"), 1)

            tok_b = const("tok_b")

            def tok_pool(s, n):
                dve.wait_ge(*after("tok_q", n))
                q4 = ps[s][:, 0:2, :].rearrange("p b n -> p (b n)").rearrange("p (t n) -> p n t", t=STRIDE)
                nc.vector.tensor_reduce(bufs[s].xn, q4[:, 0:C, :], X, ALU.max).then_inc(sem("tok_pooled"), 1)

            def tok_qk_pad(s, n):
                b = bufs[s]
                dve.wait_ge(*after("tok_pooled", n))
                nc.vector.tensor_tensor(b.qk_pad[:, 0:HEADS, 0:HD], b.xn.rearrange("p (h d) -> p h d", d=HD),
                                        tok_b[:, 0:C].rearrange("p (h d) -> p h d", d=HD), ALU.add)
                dve.wait_ge(*after("tok_k", n))
                k4 = ps[s][:, 2:4, :].rearrange("p b n -> p (b n)").rearrange("p (t n) -> p t n", t=STRIDE)
                for t in range(STRIDE):
                    last = nc.vector.tensor_tensor(
                        b.qk_pad[:, (1 + t) * HEADS:(2 + t) * HEADS, 0:HD],
                        k4[:, t, 0:C].rearrange("p (h d) -> p h d", d=HD),
                        tok_b[:, C:2 * C].rearrange("p (h d) -> p h d", d=HD), ALU.add)

            def tok_v_pad(s, n):
                b = bufs[s]
                dve.wait_ge(*after("tok_v", n))
                v4 = ps[s][:, 0:2, :].rearrange("p b n -> p (b n)").rearrange("p (t n) -> p t n", t=4)
                for t in range(4):
                    last = nc.vector.tensor_tensor(
                        b.v_ext[:, t * HEADS:(t + 1) * HEADS, 0:HD],
                        v4[:, t, 0:C].rearrange("p (h d) -> p h d", d=HD),
                        tok_b[:, 2 * C:3 * C].rearrange("p (h d) -> p h d", d=HD), ALU.add)
                last.then_inc(sem("tok_vpad"), 1)

            def tok_qT(s, n):
                dve.wait_ge(*after("tok_turned", n))
                nc.vector.tensor_copy(bufs[s].qT, ps[s][:, 3, 0:GROUPS * P].rearrange(
                    "p (g n) -> p g n", g=GROUPS)).then_inc(sem("tok_qT"), 1)

            def tok_softmax(s, n, half):
                dve_softmax_shift(dve, f"tok{half}_scores", f"tok{half}", s, n, ps[s][:, :, :].rearrange(
                    "p (a b) n -> p a (b n)", a=2)[:, :, 0:768].rearrange("p a (g k) -> p a g k", g=GROUPS),
                    2, GROUPS, 256)

            def tok_out(s, n):
                dve.wait_ge(*after("tok_proj", n))
                nc.vector.tensor_tensor(bufs[s].t1, ps[s][:, 2, 0:C], const("tok_pb"), ALU.add).then_inc(
                    sem("tok_h"), 1)
                dve.wait_ge(*after("tok_h", n))
                dve_stats(dve, "n0", s, n, row(n))

            def tok_head(n):
                both(tok_pool, n)
                both(tok_qk_pad, n)
                both(tok_v_pad, n)
                both(tok_qT, n)

            def tok_pair(old, new):
                for half in range(2):
                    both(tok_softmax, old, half)
                    both(lambda s, n: dve_probs(dve, f"tok{half}", s, n), old)
                both(lambda s, n: dve_softmax_norm(dve, "tok", s, n, TOK_PV), old)
                if new is not None:
                    both(tok_pool, new)
                both(tok_out, old)
                if new is not None:
                    both(tok_qk_pad, new)
                    both(tok_v_pad, new)
                    both(tok_qT, new)
            pairs(dve, tok_head, tok_pair)

            def rstd_all(part):
                dve.wait_ge(*after(f"{part}_mv", B))
                for t in range(B):
                    ins = nc.vector.bn_aggr(meanvar[:, t, :], allstats[:, t, :])
                link(ins)
                link(nc.vector.tensor_scalar(varp[:, :], meanvar[:, :, 1], LN_EPS, None, ALU.add))
                for step in rsqrt_steps(rstd[:, :], varp[:, :], newton[:, :]):
                    link(step())

            dve.wait_ge(sem("consts_loaded"), 16)
            rstd_all("n0")
            def at_pairs(pre, src, qkv_bias, finish):
                def take_x(s, n):
                    dve_normalize(dve, pre, s, n, row(n, src), bufs[s].xn)

                def head(n):
                    both(take_x, n)
                    both(lambda s, n: at_dve_qkv(dve, pre, s, n, qkv_bias), n)

                def pair(old, new):
                    both(lambda s, n: dve_softmax_shift(dve, f"{pre}_scores", pre, s, n, score_view(s),
                                                        4, GROUPS, P), old)
                    if new is not None:
                        both(take_x, new)
                    both(lambda s, n: at_dve_probs(dve, pre, s, n), old)
                    both(lambda s, n: dve_softmax_norm(dve, pre, s, n), old)
                    for s in range(STREAMS):
                        finish(s, old + s)
                        if new is not None:
                            at_dve_qkv(dve, pre, s, new + s, qkv_bias)
                pairs(dve, head, pair)

            def at_out(s, n):
                residual("at", s, n, row(n), const("at_pb"))
                dve.wait_ge(*after("at_h", n))
                dve_stats(dve, "n1", s, n, row(n))
            at_pairs("at", hs, const("at_b"), at_out)

            rstd_all("n1")
            for t in range(B):
                nc.vector.tensor_scalar(x3[:, t, :], hs[:, t, :], meanvar[:, t, 0:1], rstd[:, t:t + 1],
                                        ALU.subtract, ALU.mult).then_inc(sem("ff_x3"), 1)
            for t in range(B):
                dve.wait_ge(sem("ff_x3"), t + 1)
                nc.vector.bn_stats(allstats[:, t, :], x3[:, t, :]).then_inc(sem("n2_mv"), 1)
            rstd_all("n2")
            def ff_out(s, n):
                residual("ff", s, n, row(n, x3), const("ff_pb"))
                dve.wait_ge(*after("ff_h", n))
                dve_stats(dve, "n3", s, n, row(n, x3))
                nc.vector.tensor_tensor(row(n), row(n), bufs[s].t1, ALU.add).then_inc(sem("ff_sum"), 1)
            at_pairs("ff", x3, None, ff_out)
            rstd_all("n3")
            def normalize_all(pre, src):
                for t in range(B):
                    nc.vector.tensor_scalar(x3[:, t, :], src[:, t, :], meanvar[:, t, 0:1], rstd[:, t:t + 1],
                                            ALU.subtract, ALU.mult).then_inc(sem(f"{pre}_xn"), 1)
            normalize_all("gate", x3)
            dve.wait_ge(sem("gate_logits"), 1)
            nc.vector.tensor_tensor(logits[:, :, :], ps[0][:, 0, 0:B * EXPERTS].rearrange("p (b e) -> p b e", b=B),
                                    const("gate_b").unsqueeze(1).to_broadcast([P, B, EXPERTS]), ALU.add).then_inc(
                                        sem("gate_logits_kept"), 1)

            dve.wait_ge(sem("gate_logits_kept"), 1)
            dve.wait_ge(sem("ff_sum"), B)
            for t in range(B):
                ins = nc.vector.max(top8[:, t, :], logits[:, t, :])
            link(ins)
            for t in range(B):
                ins = nc.vector.max_index(idx8[:, t, :], top8[:, t, :], logits[:, t, :])
            link(ins)
            link(nc.vector.tensor_copy(gidx[:, :, :], idx8[:, :, 0:2]))
            link(nc.vector.tensor_tensor(gw[:, :, 0:1], top8[:, :, 1:2], top8[:, :, 0:1], ALU.subtract))
            nc.vector.tensor_copy(gw[:, :, 3:4], gw[:, :, 0:1]).then_inc(sem("moe_gap"), 1)
            dve.wait_ge(sem("moe_gapexp"), 1)
            link(nc.vector.tensor_scalar(gw[:, :, 2:3], gw[:, :, 1:2], 1.0, None, ALU.add))
            link(nc.vector.reciprocal(gw[:, :, 2:3], gw[:, :, 2:3]))
            link(nc.vector.tensor_tensor(gw[:, :, 1:2], gw[:, :, 1:2], gw[:, :, 2:3], ALU.mult))
            ia = iota8[:, :].unsqueeze(1).to_broadcast([P, B, EXPERTS])
            link(nc.vector.tensor_tensor(cw[:, :, :], ia, gidx[:, :, 0:1].to_broadcast([P, B, EXPERTS]), ALU.is_equal))
            link(nc.vector.tensor_tensor(logits[:, :, :], ia, gidx[:, :, 1:2].to_broadcast([P, B, EXPERTS]),
                                         ALU.is_equal))
            link(nc.vector.tensor_tensor(cw[:, :, :], cw[:, :, :], gw[:, :, 2:3].to_broadcast([P, B, EXPERTS]),
                                         ALU.mult))
            link(nc.vector.tensor_tensor(logits[:, :, :], logits[:, :, :],
                                         gw[:, :, 1:2].to_broadcast([P, B, EXPERTS]), ALU.mult))
            nc.vector.tensor_tensor(cw[:, :, :], cw[:, :, :], logits[:, :, :], ALU.add).then_inc(sem("moe_cw"), 1)
            dve.wait_ge(sem("moe_cw"), 1)

            dve.wait_ge(sem("gate_feat_hi"), 1)
            nc.vector.tensor_tensor(feat_lo, feat32, feat_hi, ALU.subtract).then_inc(sem("gate_feat_lo"), 1)

            def split_weights(k, n):
                dve.wait_ge(sem("moe_w_hi"), n)
                nc.vector.tensor_tensor(w1_parts[k][1], ew1[k], w1_parts[k][0], ALU.subtract)
                nc.vector.tensor_tensor(w2_parts[k][1], ew2[k], w2_parts[k][0], ALU.subtract).then_inc(
                    sem("moe_w_lo"), 1)
            split_weights(0, 1)

            for half in range(2):
                dve.wait_ge(sem("moe_bias2"), half + 1)
                rows = hs[:, half * 8:(half + 1) * 8, :].rearrange("p (b t) c -> p b (t c)", t=2)
                nc.vector.tensor_tensor(rows, rows, ps[half][:, :, 0:2 * C], ALU.add).then_inc(
                    sem("moe_b2_added"), 1)
            dve.wait_ge(sem("moe_b2_added"), 2)
            nc.vector.memset(small[:, 0:1], 0.0).then_inc(sem("moe_gelu"), 4)
            nc.vector.memset(small[:, 1:2], 0.0).then_inc(sem("moe_added"), 4)
            nc.vector.memset(small[:, 2:3], 0.0).then_inc(sem("moe_out"), 8)
            nc.vector.memset(small[:, 4:5], 0.0).then_inc(sem("moe_he_lo"), HT)
            nc.vector.memset(small[:, 3:4], 0.0).then_inc(sem("moe_start"), 1)

            def add_outputs(e, k, g):
                for t in range(4 * g, 4 * g + 4):
                    dve.wait_ge(sem("moe_out"), e * B + k * B + t + 1 + 8)
                    nc.vector.scalar_tensor_tensor(
                        out=hs[:, t, :], in0=ps[1][:, t % 4, 0:C], scalar=cwcur[:, k, t:t + 1],
                        in1=hs[:, t, :], op0=ALU.mult, op1=ALU.add).then_inc(sem("moe_added"), 1)

            def expert(e, k, more):
                nc.vector.tensor_copy(cwcur[:, k, :].unsqueeze(2), cw[:, :, bass.ds(e + k, 1)]).then_inc(
                    sem("moe_cwcur"), 1)
                dve.wait_ge(sem("moe_cwcur"), e + k + 1)
                for g in range(NG):
                    for m in range(HT):
                        dve.wait_ge(sem("moe_gelu"), e * (NG * HT) + k * NG * HT + g * HT + m + 1 + 4)
                        nc.vector.tensor_tensor(he_lo[g % 2][:, m, :], he[:, m, :], he_hi[g % 2][:, m, :],
                                                ALU.subtract).then_inc(sem("moe_he_lo"), 1)
                    if g == 1 and more:
                        split_weights(1 - k, e + k + 2)
                    if g > 0:
                        add_outputs(e, k, g - 1)
                add_outputs(e, k, NG - 1)
            experts(dve, expert)
            dve.wait_ge(sem("moe_added"), EXPERTS * B + 4)
            for s in range(STREAMS):
                nc.vector.memset(bufs[s].qk_pad, 0.0)
                nc.vector.memset(bufs[s].v_ext[:, 0:HEADS, :], 1.0)
            for t in range(B):
                nc.vector.bn_stats(allstats[:, t, :], hs[:, t, :]).then_inc(sem("n4_mv"), 1)
            rstd_all("n4")


            def q_squares(s, n):
                b = bufs[s]
                q, q2 = b.p[:, 0:C], b.p[:, C:2 * C]
                dve.wait_ge(*after("l1_q", n))
                nc.vector.tensor_copy(q, ps[s][:, 3, 0:C]).then_inc(sem("l1_qcopy"), 1)
                dve.wait_ge(*after("l1_qcopy", n))
                nc.vector.tensor_tensor(q2, q, q, ALU.mult).then_inc(sem("l1_squares"), 1)
                dve.wait_ge(*after("l1_squares", n))
                nc.vector.tensor_reduce(b.n2, q2.rearrange("p (h d) -> p h d", d=HD), X,
                                        ALU.add).then_inc(sem("l1_norm2"), 1)
                dve.wait_ge(*after("l1_norm2", n))

            def q_newton(s, n, lo, hi):
                b = bufs[s]
                for k, step in enumerate(rsqrt_steps(b.length, b.n2, b.nt)):
                    if lo <= k < hi:
                        step().then_inc(sem("l1_newton"), 1)
                        dve.wait_ge(sem("l1_newton"), n * 10 + (k + 1 - 10))

            def q_unit(s, n):
                b = bufs[s]
                length = b.length
                nc.vector.tensor_tensor(length, length, b.n2, ALU.mult).then_inc(sem("l1_root"), 1)
                dve.wait_ge(*after("l1_root", n))
                nc.vector.tensor_scalar(length, length, Q_EPS, None, ALU.add).then_inc(sem("l1_norm"), 1)
                dve.wait_ge(*after("l1_norm", n))
                nc.vector.reciprocal(length, length).then_inc(sem("l1_rnorm"), 1)
                dve.wait_ge(*after("l1_rnorm", n))
                nc.vector.tensor_tensor(b.qk_pad[:, 0:HEADS, 0:HD], b.p[:, 0:C].rearrange("p (h d) -> p h d", d=HD),
                                        length.unsqueeze(2).to_broadcast([P, HEADS, HD]),
                                        ALU.mult).then_inc(sem("l1_pad"), 1)
                nc.vector.memset(b.x_parts[:, :, 0:1], 1.0)
                nc.vector.memset(b.x_parts[:, :, 1:2], 0.0)

            def take_v(s, n):
                dve.wait_ge(*after("l1_v", n))
                nc.vector.tensor_copy(bufs[s].v_ext[:, 0:HEADS, 0:HD],
                                      ps[s][:, 1, C:2 * C].rearrange("p (h d) -> p h d", d=HD)).then_inc(
                                          sem("l1_vcopy"), 1)
                dve.wait_ge(*after("l1_vcopy", n))
                dve_split_v(dve, "l1", s, n)

            def kernel_lo(s, n, k):
                b = bufs[s]
                cols = slice(BANK_ORDER[k] * GROUPS * P, (BANK_ORDER[k] + 1) * GROUPS * P)
                dve.wait_ge(sem("l1_kernel"), n * 4 + (k + 1 - 4))
                last = nc.vector.tensor_tensor(b.lo[:, cols], b.p[:, cols], b.hi[:, cols], ALU.subtract)
                if k == 3:
                    last.then_inc(sem("l1_kernel_lo"), 1)

            HALF = HEADS // 2 * P

            def rescale(s, n, it):
                b = bufs[s]
                x = b.rec if it % 2 == 0 else b.mx
                dve.wait_ge(sem("l1_sums"), half_steps(n, it))
                nc.vector.tensor_reduce(b.n2, ps[s][:, 3, SUMS:SUMS + 2 * HEADS].rearrange(
                    "p (h k) -> p h k", k=2), X, ALU.add).then_inc(sem("l1_summed"), 1)
                dve.wait_ge(sem("l1_summed"), half_steps(n, it))
                if it < 2 * SINKHORN_ITERS - 1:
                    with nc.allow_low_precision(reason="the second part holds what this one leaves"):
                        nc.vector.reciprocal(b.x_parts[:, :, 0], b.n2)
                nc.vector.reciprocal(x, b.n2).then_inc(sem("l1_scaled"), 1)
                dve.wait_ge(sem("l1_scaled"), half_steps(n, it))
                if it < 2 * SINKHORN_ITERS - 1:
                    nc.vector.tensor_tensor(b.x_parts[:, :, 1], x, b.x_parts[:, :, 0],
                                            ALU.subtract).then_inc(sem("l1_xlo"), 1)

            def split_u(s, n):
                b = bufs[s]
                nc.vector.tensor_copy(b.u_parts[:, 0:HEADS], b.rec).then_inc(sem("l1_u0"), 1)
                dve.wait_ge(*after("l1_u0", n))
                nc.vector.tensor_tensor(b.nt, b.rec, b.u_parts[:, 0:HEADS], ALU.subtract).then_inc(
                    sem("l1_ur"), 1)
                dve.wait_ge(*after("l1_ur", n))
                nc.vector.tensor_copy(b.u_parts[:, HEADS:2 * HEADS], b.nt).then_inc(sem("l1_u1"), 1)
                dve.wait_ge(*after("l1_u1", n))
                nc.vector.tensor_tensor(b.u_parts[:, 2 * HEADS:3 * HEADS], b.nt, b.u_parts[:, HEADS:2 * HEADS],
                                        ALU.subtract).then_inc(sem("l1_uparts"), 1)

            def transport(s, n, half):
                b = bufs[s]
                cols = slice(8 * P * half, (8 + 4 * half) * P)
                dve.wait_ge(*after("l1_urows", 2 * n + (half - 1)))
                nc.vector.tensor_tensor(b.pT[:, cols], b.p[:, cols],
                                        ps[s][:, 0:3, :].rearrange("p b n -> p (b n)")[:, cols],
                                        ALU.mult).then_inc(sem("l1_ku"), 1)

            def row_max(s, n, half):
                b = bufs[s]
                dve.wait_ge(*after("l1_ku", 2 * n + (half - 1)))
                nc.vector.tensor_reduce(b.stats12[:, 6 * half:6 * half + 6],
                                        b.pT[:, half * HALF:(half + 1) * HALF].rearrange("p (h n) -> p h n", n=P),
                                        X, ALU.max).then_inc(sem("l1_kumax"), 1)
                if half == 1:
                    dve.wait_ge(*after("l1_kumax", 2 * n))
                    nc.vector.tensor_tensor(b.stats12, b.stats12, b.mx, ALU.mult).then_inc(sem("l1_rowmax"), 1)

            def head_max(s, n):
                b = bufs[s]
                dve.wait_ge(*after("l1_maxturned", n))
                nc.vector.tensor_reduce(b.stats[0:HEADS, 0:1], ps[s][0:HEADS, 3, 0:P], X,
                                        ALU.max).then_inc(sem("l1_headmax"), 1)
                dve.wait_ge(*after("l1_headmax", n))
                nc.vector.reciprocal(b.stats[0:HEADS, 1:2], b.stats[0:HEADS, 0:1]).then_inc(
                    sem("l1_headrec"), 1)
                dve.wait_ge(*after("l1_headrec", n))
                nc.vector.tensor_scalar(b.maxdiag, ident[0:HEADS, 0:HEADS], b.stats[0:HEADS, 1:2], SCALE,
                                        ALU.mult, ALU.mult).then_inc(sem("l1_maxdiag"), 1)

            def z_rows(s, n):
                dve.wait_ge(*after("l1_maxspread", n))
                nc.vector.tensor_tensor(bufs[s].sv, bufs[s].mx, ps[s][:, 3, P:P + HEADS], ALU.mult).then_inc(
                    sem("l1_sv"), 1)
                dve.wait_ge(*after("l1_sv", n))

            def scaled_z(s, n, half):
                b = bufs[s]
                z = b.pT[:, half * HALF:(half + 1) * HALF].rearrange("p (h n) -> p h n", n=P)
                last = nc.vector.tensor_tensor(
                    z, z, b.sv[:, 6 * half:6 * half + 6].unsqueeze(2).to_broadcast([P, 6, P]), ALU.mult)
                if half == 1:
                    last.then_inc(sem("l1_z"), 1)

            def probs_lo(s, n, half):
                b = bufs[s]
                cols = slice(half * HALF, (half + 1) * HALF)
                if half == 0:
                    dve.wait_ge(*after("l1_probs", n))
                last = nc.vector.tensor_tensor(b.lo[:, cols], b.pT[:, cols], b.hi[:, cols], ALU.subtract)
                if half == 1:
                    last.then_inc(sem("l1_probs_lo"), 1)

            def l1_out(s, n):
                residual("l1", s, n, row(n), const("l1_pb"), 1)
                dve.wait_ge(*after("l1_h", n))
                dve_stats(dve, "n5", s, n, row(n))

            def l1_stage(post, half, pre):
                for it in range(2 * SINKHORN_ITERS):
                    if half:
                        rescale(*half, it)
                    if post:
                        if it == 0:
                            split_u(*post)
                        if it in (2, 3):
                            transport(*post, it - 2)
                        if it in (4, 5):
                            row_max(*post, it - 4)
                        if it == 6:
                            head_max(*post)
                        if it == 7:
                            z_rows(*post)
                        if it in (7, 8):
                            scaled_z(*post, it - 7)
                        if it in (10, 11):
                            probs_lo(*post, it - 10)
                        if it == 13:
                            dve_softmax_norm(dve, "l1", *post)
                        if it == 16:
                            l1_out(*post)
                    if pre:
                        if it == 0:
                            dve_normalize(dve, "l1", *pre, row(pre[1]), bufs[pre[0]].xn)
                        if it == 4:
                            q_squares(*pre)
                        if it in (5, 6, 7):
                            q_newton(*pre, it - 5, it - 4)
                        if it == 8:
                            q_newton(*pre, 3, 6)
                        if it == 9:
                            q_newton(*pre, 6, 10)
                            q_unit(*pre)
                        if it == 14:
                            take_v(*pre)
                        if it in (16, 17, 18):
                            kernel_lo(*pre, it - 16)
                        if it == 19:
                            kernel_lo(*pre, 3)
            sinkhorn_stages(dve, l1_stage)
            rstd_all("n5")

            normalize_all("q", hs)
            A96 = slice(0, HC)
            hi2, lo2, abs2 = small[A96, 0:2], small[A96, 2:4], small[A96, 4:6]
            wm2, cs2, pw2, up2 = small[A96, 6:8], small[A96, 8:10], small[A96, 10:12], small[A96, 12:14]
            rc2 = small[A96, 16:18]
            w1n = const("q_w1").rearrange("p (m n) -> p m n", m=HT)
            w2n = const("q_w2").rearrange("p (c n) -> p c n", c=2)

            def absmax(dst, src):
                return nc.vector.tensor_reduce(dst, src, X, ALU.max, apply_absolute_value=True)

            nc.vector.tensor_reduce(wmax, w1n.rearrange("p m n -> p n m"), X, ALU.max,
                                    apply_absolute_value=True).then_inc(sem("q_wmax"), 1)
            dve.wait_ge(sem("q_feat"), B // 2)
            nc.vector.tensor_reduce(hi2, featT[:, :, :], X, ALU.max)
            link(nc.vector.tensor_reduce(lo2, featT[:, :, :], X, ALU.min))
            link(nc.vector.tensor_scalar(lo2, lo2, -1.0, None, ALU.mult))
            link(nc.vector.tensor_tensor(abs2, hi2, lo2, ALU.max))
            dve.wait_ge(sem("q_wmaxturned"), 1)
            link(nc.vector.tensor_reduce(wm2, ps[0][A96, 3, 0:2 * P].rearrange("p (c n) -> p c n", c=2), X, ALU.max))
            link(nc.vector.reciprocal(wm2, wm2))
            link(nc.vector.tensor_tensor(wm2, abs2, wm2, ALU.mult))
            for step in rsqrt_steps(abs2, wm2, pw2):
                link(step())
            link(nc.vector.tensor_tensor(abs2, abs2, wm2, ALU.mult))
            link(nc.vector.tensor_scalar(pw2.bitcast(I32), abs2.bitcast(I32), 0x7F800000, None, ALU.bitwise_and))
            link(nc.vector.tensor_scalar(up2, pw2, 1.5, None, ALU.mult))
            link(nc.vector.tensor_tensor(up2, abs2, up2, ALU.is_gt))
            link(nc.vector.tensor_scalar(up2, up2, 1.0, None, ALU.add))
            link(nc.vector.tensor_tensor(cs2, pw2, up2, ALU.mult))
            for c in range(2):
                last = nc.vector.tensor_scalar(csb[:, c, :], ones[A96, :], cs2[:, c:c + 1], None, ALU.mult)
            last.then_inc(sem("q_cs_rows"), 1)
            link(nc.vector.reciprocal(rc2, cs2))
            nc.vector.tensor_tensor(hi2, hi2, rc2, ALU.mult)
            link(nc.vector.tensor_tensor(lo2, lo2, rc2, ALU.mult))
            nc.vector.tensor_tensor(small[A96, 20:21], hi2[:, 0:1], hi2[:, 1:2], ALU.max)
            nc.vector.tensor_tensor(small[A96, 21:22], lo2[:, 0:1], lo2[:, 1:2], ALU.max).then_inc(
                sem("q_range"), 1)

            def quant_range(pre, rows, at):
                dve.wait_ge(sem(f"{pre}turned"), 1)
                link(nc.vector.tensor_reduce(small[0:2, at:at + 1], ps[0][0:2, 1, 0:rows], X, ALU.max))
                link(nc.vector.tensor_scalar(small[0:2, at:at + 1], small[0:2, at:at + 1], 0.0, None, ALU.max))
                nc.vector.tensor_scalar(small[0:2, at + 1:at + 3], ident[0:2, 0:2], small[0:2, at:at + 1], None,
                                        ALU.mult).then_inc(sem(f"{pre}diag"), 1)
                dve.wait_ge(sem(f"{pre}spread"), 1)
                link(nc.vector.tensor_copy(small[:, at + 8:at + 10], ps[0][:, 2, 0:2]))
                sc, lo, hi, rs = (small[:, at + k:at + k + 1] for k in (4, 5, 6, 10))
                link(nc.vector.tensor_tensor(sc, small[:, at + 8:at + 9], small[:, at + 9:at + 10], ALU.add))
                link(nc.vector.tensor_scalar(sc, sc, 1.0 / 255.0, 1e-8, ALU.mult, ALU.max))
                link(nc.vector.reciprocal(rs, sc))
                link(nc.vector.tensor_scalar(lo, small[:, at + 9:at + 10], rs, ROUND, ALU.mult, ALU.add))
                link(nc.vector.tensor_scalar(lo, lo, ROUND, -1.0, ALU.subtract, ALU.mult))
                link(nc.vector.tensor_scalar(hi, lo, 255.0, None, ALU.add))
                return sc, lo, hi, rs

            sx, xlo, xhi, rsx = quant_range("q_range", HC, 23)
            for c in range(2):
                link(nc.vector.tensor_scalar(featT[:, c, :], featT[:, c, :], rc2[:, c:c + 1], rsx[A96],
                                             ALU.mult, ALU.mult))
                link(nc.vector.tensor_scalar(featT[:, c, :], featT[:, c, :], ROUND, ROUND, ALU.add, ALU.subtract))
                last = nc.vector.tensor_scalar(xq[:, c, :], featT[:, c, :], xlo[A96], xhi[A96], ALU.max, ALU.min)
            last.then_inc(sem("q_xq"), 1)

            s1, s2 = small[:, 54:60], small[A96, 60:62]
            dve.wait_ge(sem("q_csrow"), 1)
            link(nc.vector.tensor_tensor(w1_s, w1n, ps[0][:, 0, 0:C].unsqueeze(1).to_broadcast([P, HT, C]), ALU.mult))
            absmax(s1, w1_s)
            link(absmax(s2, w2n))
            r1, r2 = small[:, 86:92], small[A96, 92:94]
            nc.vector.tensor_scalar(s1, s1, 1.0 / 127.0, 1e-8, ALU.mult, ALU.max)
            link(nc.vector.tensor_scalar(s2, s2, 1.0 / 127.0, 1e-8, ALU.mult, ALU.max))
            nc.vector.reciprocal(r1, s1)
            link(nc.vector.reciprocal(r2, s2))
            nc.vector.tensor_tensor(w1_s, w1_s, r1.unsqueeze(2).to_broadcast([P, HT, C]), ALU.mult)
            link(nc.vector.tensor_tensor(w2n, w2n, r2.unsqueeze(2).to_broadcast([HC, 2, HIDDEN]), ALU.mult))
            nc.vector.tensor_scalar(w1_s, w1_s, ROUND, ROUND, ALU.add, ALU.subtract)
            link(nc.vector.tensor_scalar(w2n, w2n, ROUND, ROUND, ALU.add, ALU.subtract))
            nc.vector.tensor_scalar(w1_q, w1_s, -128.0, 127.0, ALU.max, ALU.min)
            nc.vector.tensor_scalar(w2_q, w2n, -128.0, 127.0, ALU.max, ALU.min)
            for c in range(2):
                last = nc.vector.tensor_scalar(sw2b[:, c, :], ones[A96, :], s2[:, c:c + 1], None, ALU.mult)
            last.then_inc(sem("q_w_quant"), 1)
            nc.vector.tensor_scalar(small[:, 48:54], s1, sx, None, ALU.mult).then_inc(sem("q_hidden_scale"), 1)
            dve.wait_ge(sem("q_wturned"), 1)
            tb = ps[1][:, :, :].rearrange("p b n -> p (b n)").bitcast(BF16).rearrange("p (b n) -> p b n", b=4)
            nc.vector.tensor_copy(wq1T, tb[0:HC, 0:2, 0:HIDDEN])
            nc.vector.tensor_copy(wq2T.rearrange("p (b m) n -> p b (m n)", b=2), tb[:, 2:4, 0:3 * C]).then_inc(
                sem("q_wT"), 1)
            dve.wait_ge(sem("q_sw2row"), 1)
            nc.vector.tensor_copy(sw2row[:, :], ps[0][:, 3, 0:C]).then_inc(sem("q_sw2"), 1)

            for g in range(NG):
                dve.wait_ge(sem("q_gelu"), (g + 1) * HT)
                ins = nc.vector.tensor_reduce(small[:, 64 + g:65 + g], gelu_out[:, :, g * TG:(g + 1) * TG],
                                              mybir.AxisListType.XY, ALU.max, apply_absolute_value=True)
            link(ins)
            nc.vector.tensor_reduce(small[:, 30:31], small[:, 64:64 + NG], X, ALU.max).then_inc(sem("q_hmax"), 1)
            dve.wait_ge(sem("q_hmaxturned"), 1)
            nc.vector.tensor_reduce(small[0:1, 31:32], ps[0][0:1, 0, 0:P], X, ALU.max).then_inc(sem("q_hmaxone"), 1)
            dve.wait_ge(sem("q_hmaxspread"), 1)
            sh = small[:, 70:71]
            rsh = small[:, 71:72]
            link(nc.vector.tensor_scalar(sh, ps[0][:, 1, 0:1], 1.0 / 127.0, 1e-8, ALU.mult, ALU.max))
            link(nc.vector.reciprocal(rsh, sh))
            nc.vector.tensor_scalar(sw2row[:, :], sw2row[:, :], sh, None, ALU.mult).then_inc(sem("q_hscale"), 1)
            for g in range(NG):
                part = gelu_out[:, :, g * TG:(g + 1) * TG]
                link(nc.vector.tensor_scalar(part, part, rsh, ROUND, ALU.mult, ALU.add))
                nc.vector.tensor_scalar(hqs[g], part, ROUND, 127.0, ALU.subtract, ALU.min).then_inc(sem("q_hq"), 1)
            for t in range(B):
                dve.wait_ge(sem("q_down"), t + 1)
                nc.vector.tensor_tensor(oq[:, t, :], ps[t % 8 // 4][:, t % 4, 0:C], sw2row[:, :],
                                        ALU.mult).then_inc(sem("q_down_read"), 1)
            dve.wait_ge(sem("q_down_read"), B)
            link(nc.vector.tensor_tensor(oq, oq, const("q_b2").unsqueeze(1).to_broadcast([P, B, C]), ALU.add))
            nc.vector.tensor_reduce(small[:, 40:41], oq, mybir.AxisListType.XY, ALU.max)
            link(nc.vector.tensor_reduce(small[:, 42:43], oq, mybir.AxisListType.XY, ALU.min))
            nc.vector.tensor_scalar(small[:, 41:42], small[:, 42:43], -1.0, None, ALU.mult).then_inc(
                sem("q_orange"), 1)
            so, olo, ohi, rso = quant_range("q_orange", P, 75)
            link(nc.vector.tensor_scalar(oq, oq, rso, ROUND, ALU.mult, ALU.add))
            link(nc.vector.tensor_scalar(oq, oq, ROUND, olo, ALU.subtract, ALU.max))
            link(nc.vector.tensor_scalar(oq, oq, ohi, so, ALU.min, ALU.mult))
            nc.vector.tensor_tensor(hs[:, :, :], hs[:, :, :], oq, ALU.add).then_inc(sem("result"), 1)


def kernel(**inputs):
    import concourse.bacc as bacc
    from concourse.bass_utils import run_bass_kernel_spmd

    a = {k: np.asarray(v) for k, v in inputs.items()}

    def chunked(w):
        return w.reshape(2, HC, -1).transpose(1, 0, 2).reshape(HC, -1)

    def rows(v):
        return np.broadcast_to(v.reshape(1, -1), (P, v.size))

    parts = {
        "tok_w": chunked(a["L0_tok_w_qkv"].T), "tok_b": rows(a["L0_tok_b_qkv"]),
        "tok_pw": chunked(a["L0_tok_w_proj"].T), "tok_pb": rows(a["L0_tok_b_proj"]),
        "at_w": chunked(a["L0_attn_qkv_w"].T), "at_b": rows(a["L0_attn_qkv_b"]),
        "at_pw": chunked(a["L0_attn_proj_w"].T), "at_pb": rows(a["L0_attn_proj_b"]),
        "ff_w": chunked(a["L0_ffn_qkv_w"]), "ff_pw": chunked(a["L0_ffn_proj_w"]), "ff_pb": rows(a["L0_ffn_proj_b"]),
        "ln1_g": chunked(a["L0_ffn_ln1_g"]), "ln1_b": chunked(a["L0_ffn_ln1_b"]),
        "ln2_g": chunked(a["L0_ffn_ln2_g"]), "ln2_b": chunked(a["L0_ffn_ln2_b"]),
        "gate_w": chunked(a["L0_ffn_gate_w"]), "gate_b": rows(a["L0_ffn_gate_b"]),
        "b1": a["L0_ffn_b1"].reshape(EXPERTS, HT, P).transpose(2, 0, 1).reshape(P, -1), "b2": a["L0_ffn_b2"],
        "l1_w": chunked(a["L1_attn_w_qkv"].T), "l1_pw": chunked(a["L1_attn_w_proj"].T),
        "l1_pb": rows(a["L1_attn_b_proj"]),
        "q_b1": a["L1_ffn_b1"].reshape(HT, P).T, "q_b2": rows(a["L1_ffn_b2"]),
        "q_w1": a["L1_ffn_w1"].reshape(HT, P, C).transpose(1, 0, 2).reshape(P, -1),
        "q_w2": a["L1_ffn_w2"].reshape(2, HC, HIDDEN).transpose(1, 0, 2).reshape(HC, -1),
    }
    packed = np.zeros((P, PACKED), np.float32)
    for name, (at, n, cols) in OFFSET.items():
        packed[0:n, at:at + cols] = parts[name]
    x = a["x"].reshape(B, STRIDE, WQ, WINDOWS, 2, HC).transpose(0, 5, 4, 3, 2, 1).reshape(B, HC, 2, N_IN)
    w1 = a["L0_ffn_w1"].reshape(EXPERTS, 2, HC, HIDDEN).transpose(0, 2, 1, 3)
    w2 = a["L0_ffn_w2"].reshape(EXPERTS, HT, P, C).transpose(0, 2, 1, 3)

    nc = bacc.Bacc("TRN2", target_bir_lowering=False, num_devices=1)
    arrays = {"x_dram": x, "packed_dram": packed, "w1_dram": w1, "w2_dram": w2}
    arrays = {k: np.ascontiguousarray(v) for k, v in arrays.items()}
    args = [nc.dram_tensor(k, v.shape, F32, kind="ExternalInput").ap() for k, v in arrays.items()]
    out = nc.dram_tensor("out_dram", (B, P, C), F32, kind="ExternalOutput").ap()
    build(nc, *args, out)
    r = run_bass_kernel_spmd(nc, [arrays], core_ids=[0])
    return r.results[0]["out_dram"]
```
